# Optimizing a Trainium2 kernel written in Bass

```python
import numpy as np
import jax
import jax.numpy as jnp

def _softmax(x, axis=-1):
    return jax.nn.softmax(x, axis=axis)

def _gelu(x):
    return jax.nn.gelu(x, approximate=True)

def _silu(x):
    return jax.nn.silu(x)

def _sigmoid(x):
    return jax.nn.sigmoid(x)

def _layernorm(x, axis=-1, eps=1e-05):
    m = jnp.mean(x, axis=axis, keepdims=True)
    v = jnp.var(x, axis=axis, keepdims=True)
    return (x - m) / jnp.sqrt(v + eps)

def _scatter_add(tgt, idx, src, axis=0):
    return tgt.at[idx].add(src)

def _segment_sum(src, seg, n):
    return jax.ops.segment_sum(src, seg, n)
kernel_name = 'mk_adaln_d4_jaxref_r8_b0ee57'

def setup_inputs(seed: int=0):
    np.random.seed(seed)
    _w = jnp.asarray

    def _L0_attn_setup():
        import math
        import jax, jax.numpy as jnp
        import numpy as np
        L, D, H, F = (4, 128, 16, 512)
        HD = D // H
        EPS = 1e-05

        def get_alibi_slopes(num_heads):
            closest = 2 ** math.floor(math.log2(num_heads))
            base = 2 ** (-2 ** (-(math.log2(closest) - 3)))
            slopes = base ** np.arange(1, closest + 1)
            if closest != num_heads:
                extra_base = 2 ** (-2 ** (-(math.log2(2 * closest) - 3)))
                extra = extra_base ** np.arange(1, 2 * (num_heads - closest) + 1, 2)
                slopes = np.concatenate([slopes, extra])
            return jnp.asarray(slopes, dtype=jnp.float32)

        def build_mask(num_heads, T):
            pos = jnp.arange(T)
            dist = pos[None, :] - pos[:, None]
            alibi = get_alibi_slopes(num_heads)[:, None, None] * dist[None]
            causal = jnp.where(dist > 0, -jnp.inf, 0.0).astype(jnp.float32)
            return causal[None] + alibi

        def layer_norm(x, w, b):
            mu = jnp.mean(x, axis=-1, keepdims=True)
            var = jnp.mean(jnp.square(x - mu), axis=-1, keepdims=True)
            return (x - mu) * jax.lax.rsqrt(var + EPS) * w + b

        def mha(x, mask, Wi, bi, Wo, bo):
            B, T, _ = x.shape
            qkv = x @ Wi.T + bi
            q, k, v = jnp.split(qkv, 3, axis=-1)
            q = q.reshape(B, T, H, HD).transpose(0, 2, 1, 3)
            k = k.reshape(B, T, H, HD).transpose(0, 2, 1, 3)
            v = v.reshape(B, T, H, HD).transpose(0, 2, 1, 3)
            scores = jnp.einsum('bhqd,bhkd->bhqk', q, k) / math.sqrt(HD)
            scores = scores + mask[None]
            attn = jax.nn.softmax(scores, axis=-1)
            out = jnp.einsum('bhqk,bhkd->bhqd', attn, v)
            out = out.transpose(0, 2, 1, 3).reshape(B, T, D)
            return out @ Wo.T + bo
        key = jax.random.key(seed)
        ks = jax.random.split(key, 13)
        s = 0.02
        inp = {'x': jax.random.normal(ks[0], (2, 256, D), dtype=jnp.float32), 'in_proj_w': jax.random.normal(ks[1], (L, 3 * D, D), dtype=jnp.float32) * s, 'in_proj_b': jnp.zeros((L, 3 * D), dtype=jnp.float32), 'out_proj_w': jax.random.normal(ks[2], (L, D, D), dtype=jnp.float32) * s, 'out_proj_b': jnp.zeros((L, D), dtype=jnp.float32), 'ffn1_w': jax.random.normal(ks[3], (L, F, D), dtype=jnp.float32) * s, 'ffn1_b': jnp.zeros((L, F), dtype=jnp.float32), 'ffn2_w': jax.random.normal(ks[4], (L, D, F), dtype=jnp.float32) * s, 'ffn2_b': jnp.zeros((L, D), dtype=jnp.float32), 'ln1_w': jnp.ones((L, D), dtype=jnp.float32), 'ln1_b': jnp.zeros((L, D), dtype=jnp.float32), 'ln2_w': jnp.ones((L, D), dtype=jnp.float32), 'ln2_b': jnp.zeros((L, D), dtype=jnp.float32), 'final_w': jnp.ones((D,), dtype=jnp.float32), 'final_b': jnp.zeros((D,), dtype=jnp.float32)}
        return inp
    _L0_attn_in = _L0_attn_setup()

    def _L0_ffn_setup():
        import jax, jax.numpy as jnp
        import numpy as np
        B, S, H, E = (2, 256, 128, 16)
        key = jax.random.key(seed)
        k0, k1, k2, k3 = jax.random.split(key, 4)
        tokens = jax.random.normal(k0, (B, S, H), dtype=jnp.float32)
        gate_w = jax.random.normal(k1, (E, H), dtype=jnp.float32) * H ** (-0.5)
        expert_w = jax.random.normal(k2, (E, H, H), dtype=jnp.float32) * H ** (-0.5)
        expert_b = jax.random.normal(k3, (E, H), dtype=jnp.float32) * 0.01
        return {'tokens': tokens, 'gate_w': gate_w, 'expert_w': expert_w, 'expert_b': expert_b}
    _L0_ffn_in = _L0_ffn_setup()
    _L0_c = _w((lambda *s: np.random.randn(*s).astype(np.float32) * 0.05)(2, 128))
    _L0_wmod = _w((lambda *s: np.random.randn(*s).astype(np.float32) * 0.05)(128, 6 * 128) * 128 ** (-0.5))

    def _L1_attn_setup():
        import jax, jax.numpy as jnp
        import numpy as np
        BASE_FREQUENCY = 10000.0
        LRP = 17
        MIN_L = 1.0 - LRP / 100.0
        SDT_L = (BASE_FREQUENCY - MIN_L * BASE_FREQUENCY) * 2.0
        ARM_ATTENTION = 2.0
        HEADS_DIM = 64

        def _nrope(xs, base, angle_range):
            N, T, d = xs.shape
            half = d // 2
            inv_freq = base ** (-jnp.arange(half, dtype=jnp.float32) / half)
            pos = jnp.arange(T, dtype=jnp.float32)
            scale = angle_range / jnp.maximum(T - 1, 1)
            ang = pos[:, None] * inv_freq[None, :] * scale
            cos, sin = (jnp.cos(ang), jnp.sin(ang))
            x1, x2 = (xs[..., :half], xs[..., half:])
            return jnp.concatenate([x1 * cos - x2 * sin, x1 * sin + x2 * cos], axis=-1)
        key = jax.random.key(seed)
        ks = jax.random.split(key, 9)
        B, T, E = (4, 128, 128)
        x = jax.random.normal(ks[0], (B, T, E), dtype=jnp.float32)

        def w(k):
            return jax.random.normal(k, (E, E), dtype=jnp.float32) * 0.02
        z = jnp.zeros((E,), dtype=jnp.float32)
        return {'x': x, 'Wq': w(ks[1]), 'bq': z, 'Wk': w(ks[2]), 'bk': z, 'Wv': w(ks[3]), 'bv': z, 'Wo': w(ks[4]), 'bo': z, 'nrope_freq': jnp.zeros((1,), dtype=jnp.float32)}
    _L1_attn_in = _L1_attn_setup()

    def _L1_ffn_setup():
        import jax, jax.numpy as jnp
        import numpy as np
        D_MODEL = 128
        H_SHARED = 256
        H_ROUTED = 128
        N_EXPERTS = 8
        TOP_K = 2
        key = jax.random.key(seed)
        ks = jax.random.split(key, 8)
        B, T = (2, 256)
        sc_d = 1.0 / np.sqrt(D_MODEL)
        sc_hs = 1.0 / np.sqrt(H_SHARED)
        sc_hr = 1.0 / np.sqrt(H_ROUTED)
        return {'x': jax.random.normal(ks[0], (B, T, D_MODEL), dtype=jnp.float32), 'router_w': jax.random.normal(ks[1], (N_EXPERTS, D_MODEL), dtype=jnp.float32) * sc_d, 'router_bias': jnp.zeros((N_EXPERTS,), dtype=jnp.float32), 'sw1': jax.random.normal(ks[2], (D_MODEL, H_SHARED), dtype=jnp.float32) * sc_d, 'sw3': jax.random.normal(ks[3], (D_MODEL, H_SHARED), dtype=jnp.float32) * sc_d, 'sw2': jax.random.normal(ks[4], (H_SHARED, D_MODEL), dtype=jnp.float32) * sc_hs, 'ew1': jax.random.normal(ks[5], (N_EXPERTS, D_MODEL, H_ROUTED), dtype=jnp.float32) * sc_d, 'ew2': jax.random.normal(ks[6], (N_EXPERTS, H_ROUTED, D_MODEL), dtype=jnp.float32) * sc_hr}
    _L1_ffn_in = _L1_ffn_setup()
    _L1_c = _w((lambda *s: np.random.randn(*s).astype(np.float32) * 0.05)(2, 128))
    _L1_wmod = _w((lambda *s: np.random.randn(*s).astype(np.float32) * 0.05)(128, 6 * 128) * 128 ** (-0.5))

    def _L2_attn_setup():
        import jax, jax.numpy as jnp
        import numpy as np
        from jax import lax
        D_MODEL = 128
        D_STATE = 16
        D_CONV = 4
        EXPAND = 2
        D_INNER = EXPAND * D_MODEL
        DT_RANK = (D_MODEL + 15) // 16
        BATCH = 4
        SEQLEN = 128

        def _silu(x):
            return x * jax.nn.sigmoid(x)

        def _init_block(key):
            ks = jax.random.split(key, 5)
            s = 0.02
            in_proj_w = jax.random.normal(ks[0], (2 * D_INNER, D_MODEL), jnp.float32) * s
            conv_w = jax.random.normal(ks[1], (D_INNER, D_CONV), jnp.float32) * s
            conv_b = jnp.zeros((D_INNER,), jnp.float32)
            x_proj_w = jax.random.normal(ks[2], (DT_RANK + 2 * D_STATE, D_INNER), jnp.float32) * s
            dt_proj_w = jax.random.normal(ks[3], (D_INNER, DT_RANK), jnp.float32) * DT_RANK ** (-0.5)
            dt_proj_b = jnp.log(jnp.expm1(jnp.full((D_INNER,), 0.01, jnp.float32)))
            A_log = jnp.log(jnp.broadcast_to(jnp.arange(1, D_STATE + 1, dtype=jnp.float32), (D_INNER, D_STATE)))
            D_param = jnp.ones((D_INNER,), jnp.float32)
            out_proj_w = jax.random.normal(ks[4], (D_MODEL, D_INNER), jnp.float32) * s
            return (in_proj_w, conv_w, conv_b, x_proj_w, dt_proj_w, dt_proj_b, A_log, D_param, out_proj_w)

        def _mamba(x, in_proj_w, conv_w, conv_b, x_proj_w, dt_proj_w, dt_proj_b, A_log, D_param, out_proj_w):
            B, L, _ = x.shape
            xz = jnp.einsum('bld,ed->ble', x, in_proj_w)
            x_in, z = jnp.split(xz, 2, axis=-1)
            x_c = x_in.swapaxes(1, 2)
            x_c = lax.conv_general_dilated(x_c, conv_w[:, None, :], window_strides=(1,), padding=[(D_CONV - 1, 0)], feature_group_count=D_INNER, dimension_numbers=('NCH', 'OIH', 'NCH'))
            x_c = x_c + conv_b[None, :, None]
            u = _silu(x_c).swapaxes(1, 2)
            x_dbl = jnp.einsum('bld,ed->ble', u, x_proj_w)
            dt, Bm, Cm = jnp.split(x_dbl, [DT_RANK, DT_RANK + D_STATE], axis=-1)
            delta = jax.nn.softplus(jnp.einsum('blr,dr->bld', dt, dt_proj_w) + dt_proj_b)
            A = -jnp.exp(A_log)

            def step(h, inp):
                d_t, b_t, c_t, u_t = inp
                h = h * jnp.exp(d_t[:, :, None] * A) + (d_t * u_t)[:, :, None] * b_t[:, None, :]
                y = jnp.einsum('bdn,bn->bd', h, c_t)
                return (h, y)
            h0 = jnp.zeros((B, D_INNER, D_STATE), x.dtype)
            xs = (delta.swapaxes(0, 1), Bm.swapaxes(0, 1), Cm.swapaxes(0, 1), u.swapaxes(0, 1))
            _, ys = lax.scan(step, h0, xs)
            y = ys.swapaxes(0, 1) + u * D_param
            y = y * _silu(z)
            return jnp.einsum('bld,ed->ble', y, out_proj_w)

        def _reference_tuple_inner(hidden, diff, h_in_proj_w, h_conv_w, h_conv_b, h_x_proj_w, h_dt_proj_w, h_dt_proj_b, h_A_log, h_D_param, h_out_proj_w, d_in_proj_w, d_conv_w, d_conv_b, d_x_proj_w, d_dt_proj_w, d_dt_proj_b, d_A_log, d_D_param, d_out_proj_w):
            hidden_out = _mamba(hidden, h_in_proj_w, h_conv_w, h_conv_b, h_x_proj_w, h_dt_proj_w, h_dt_proj_b, h_A_log, h_D_param, h_out_proj_w)
            diff_out = _mamba(diff, d_in_proj_w, d_conv_w, d_conv_b, d_x_proj_w, d_dt_proj_w, d_dt_proj_b, d_A_log, d_D_param, d_out_proj_w)
            return (hidden_out, diff_out)
        key = jax.random.key(seed)
        k_h, k_d, k1, k2 = jax.random.split(key, 4)
        hidden = jax.random.normal(k_h, (BATCH, SEQLEN, D_MODEL), jnp.float32)
        diff = jax.random.normal(k_d, (BATCH, SEQLEN, D_MODEL), jnp.float32)
        hp = _init_block(k1)
        dp = _init_block(k2)
        names = ['in_proj_w', 'conv_w', 'conv_b', 'x_proj_w', 'dt_proj_w', 'dt_proj_b', 'A_log', 'D_param', 'out_proj_w']
        out = {'hidden': hidden, 'diff': diff}
        for n, v in zip(names, hp):
            out['h_' + n] = v
        for n, v in zip(names, dp):
            out['d_' + n] = v
        return out
    _L2_attn_in = _L2_attn_setup()

    def _L2_ffn_setup():
        import jax, jax.numpy as jnp
        import numpy as np
        B, S, D, O, E, K = (2, 256, 128, 128, 8, 2)
        key = jax.random.key(seed)
        ks = jax.random.split(key, 6)

        def w(k, shape, fan_in):
            return jax.random.normal(k, shape, jnp.float32) * fan_in ** (-0.5)
        return {'x': jax.random.normal(ks[0], (B, S, D), jnp.float32), 'gate_w': w(ks[1], (E, D), D), 'gate_b': jnp.zeros((E,), jnp.float32), 'w1': w(ks[2], (E, D, O), D), 'b1': jnp.zeros((E, O), jnp.float32), 'w2': w(ks[3], (E, O, O), O), 'b2': jnp.zeros((E, O), jnp.float32), 'w3': w(ks[4], (E, O, O), O), 'b3': jnp.zeros((E, O), jnp.float32)}
    _L2_ffn_in = _L2_ffn_setup()
    _L2_c = _w((lambda *s: np.random.randn(*s).astype(np.float32) * 0.05)(2, 128))
    _L2_wmod = _w((lambda *s: np.random.randn(*s).astype(np.float32) * 0.05)(128, 6 * 128) * 128 ** (-0.5))

    def _L3_attn_setup():
        import jax, jax.numpy as jnp
        import numpy as np
        import math
        NUM_HEADS = 16
        DIM = 128
        DH = DIM // NUM_HEADS
        THETA = 10000.0
        SCALE_BASE = 512.0

        def _rotate_half(x):
            x = x.reshape(*x.shape[:-1], -1, 2)
            x1, x2 = (x[..., 0], x[..., 1])
            return jnp.stack((-x2, x1), axis=-1).reshape(*x1.shape[:-1], -1)

        def _xpos_rotate(q, k):
            s = q.shape[2]
            t = jnp.arange(s, dtype=jnp.float32)
            inv_freq = 1.0 / THETA ** (jnp.arange(0, DH, 2, dtype=jnp.float32) / DH)
            freqs = t[:, None] * inv_freq[None, :]
            freqs = jnp.repeat(freqs, 2, axis=-1)
            cos, sin = (jnp.cos(freqs), jnp.sin(freqs))
            base = (jnp.arange(0, DH, 2, dtype=jnp.float32) + 0.4 * DH) / (1.4 * DH)
            power = (t - s // 2) / SCALE_BASE
            scale = base[None, :] ** power[:, None]
            scale = jnp.concatenate((scale, scale), axis=-1)
            q = q * cos * scale + _rotate_half(q) * sin * scale
            inv_scale = 1.0 / scale
            k = k * cos * inv_scale + _rotate_half(k) * sin * inv_scale
            return (q, k)
        key = jax.random.key(seed)
        ks = jax.random.split(key, 5)
        b, s = (2, 256)
        w_scale = DIM ** (-0.5)
        return {'x': jax.random.normal(ks[0], (b, s, DIM), jnp.float32), 'Wq': jax.random.normal(ks[1], (DIM, DIM), jnp.float32) * w_scale, 'bq': jnp.zeros((DIM,), jnp.float32), 'Wk': jax.random.normal(ks[2], (DIM, DIM), jnp.float32) * w_scale, 'bk': jnp.zeros((DIM,), jnp.float32), 'Wv': jax.random.normal(ks[3], (DIM, DIM), jnp.float32) * w_scale, 'bv': jnp.zeros((DIM,), jnp.float32), 'Wo': jax.random.normal(ks[4], (DIM, DIM), jnp.float32) * w_scale, 'bo': jnp.zeros((DIM,), jnp.float32)}
    _L3_attn_in = _L3_attn_setup()

    def _L3_ffn_setup():
        import jax, jax.numpy as jnp
        import numpy as np
        import math
        B, S, D = (4, 256, 128)
        E, DFF = (16, 256)
        CAP_FACTOR = 2.0
        ROUTER_HIDDEN = 128
        CAPACITY = int(math.ceil(S * CAP_FACTOR / E))
        key = jax.random.key(seed)
        ks = jax.random.split(key, 6)

        def uinit(k, shape, fan_in):
            bound = math.sqrt(3.0) * math.sqrt(1.0 / 3.0) / math.sqrt(fan_in)
            return jax.random.uniform(k, shape, jnp.float32, -bound, bound)
        return {'hidden_states': jax.random.normal(ks[0], (B, S, D), jnp.float32), 'router_w1': jax.random.normal(ks[1], (D, ROUTER_HIDDEN), jnp.float32) / math.sqrt(D), 'router_w2': jax.random.normal(ks[2], (ROUTER_HIDDEN, E), jnp.float32) / math.sqrt(ROUTER_HIDDEN), 'w1': uinit(ks[3], (E, D, DFF), D), 'w2': uinit(ks[4], (E, D, DFF), D), 'w3': uinit(ks[5], (E, DFF, D), DFF)}
    _L3_ffn_in = _L3_ffn_setup()
    _L3_c = _w((lambda *s: np.random.randn(*s).astype(np.float32) * 0.05)(2, 128))
    _L3_wmod = _w((lambda *s: np.random.randn(*s).astype(np.float32) * 0.05)(128, 6 * 128) * 128 ** (-0.5))
    _d = {'L0_attn_x': _L0_attn_in['x'], 'L0_attn_in_proj_w': _L0_attn_in['in_proj_w'], 'L0_attn_in_proj_b': _L0_attn_in['in_proj_b'], 'L0_attn_out_proj_w': _L0_attn_in['out_proj_w'], 'L0_attn_out_proj_b': _L0_attn_in['out_proj_b'], 'L0_attn_ffn1_w': _L0_attn_in['ffn1_w'], 'L0_attn_ffn1_b': _L0_attn_in['ffn1_b'], 'L0_attn_ffn2_w': _L0_attn_in['ffn2_w'], 'L0_attn_ffn2_b': _L0_attn_in['ffn2_b'], 'L0_attn_ln1_w': _L0_attn_in['ln1_w'], 'L0_attn_ln1_b': _L0_attn_in['ln1_b'], 'L0_attn_ln2_w': _L0_attn_in['ln2_w'], 'L0_attn_ln2_b': _L0_attn_in['ln2_b'], 'L0_attn_final_w': _L0_attn_in['final_w'], 'L0_attn_final_b': _L0_attn_in['final_b'], 'L0_ffn_gate_w': _L0_ffn_in['gate_w'], 'L0_ffn_expert_w': _L0_ffn_in['expert_w'], 'L0_ffn_expert_b': _L0_ffn_in['expert_b'], 'L0_c': _L0_c, 'L0_wmod': _L0_wmod, 'L1_attn_Wq': _L1_attn_in['Wq'], 'L1_attn_bq': _L1_attn_in['bq'], 'L1_attn_Wk': _L1_attn_in['Wk'], 'L1_attn_bk': _L1_attn_in['bk'], 'L1_attn_Wv': _L1_attn_in['Wv'], 'L1_attn_bv': _L1_attn_in['bv'], 'L1_attn_Wo': _L1_attn_in['Wo'], 'L1_attn_bo': _L1_attn_in['bo'], 'L1_attn_nrope_freq': _L1_attn_in['nrope_freq'], 'L1_ffn_router_w': _L1_ffn_in['router_w'], 'L1_ffn_router_bias': _L1_ffn_in['router_bias'], 'L1_ffn_sw1': _L1_ffn_in['sw1'], 'L1_ffn_sw3': _L1_ffn_in['sw3'], 'L1_ffn_sw2': _L1_ffn_in['sw2'], 'L1_ffn_ew1': _L1_ffn_in['ew1'], 'L1_ffn_ew2': _L1_ffn_in['ew2'], 'L1_c': _L1_c, 'L1_wmod': _L1_wmod, 'L2_attn_diff': _L2_attn_in['diff'], 'L2_attn_h_in_proj_w': _L2_attn_in['h_in_proj_w'], 'L2_attn_h_conv_w': _L2_attn_in['h_conv_w'], 'L2_attn_h_conv_b': _L2_attn_in['h_conv_b'], 'L2_attn_h_x_proj_w': _L2_attn_in['h_x_proj_w'], 'L2_attn_h_dt_proj_w': _L2_attn_in['h_dt_proj_w'], 'L2_attn_h_dt_proj_b': _L2_attn_in['h_dt_proj_b'], 'L2_attn_h_A_log': _L2_attn_in['h_A_log'], 'L2_attn_h_D_param': _L2_attn_in['h_D_param'], 'L2_attn_h_out_proj_w': _L2_attn_in['h_out_proj_w'], 'L2_attn_d_in_proj_w': _L2_attn_in['d_in_proj_w'], 'L2_attn_d_conv_w': _L2_attn_in['d_conv_w'], 'L2_attn_d_conv_b': _L2_attn_in['d_conv_b'], 'L2_attn_d_x_proj_w': _L2_attn_in['d_x_proj_w'], 'L2_attn_d_dt_proj_w': _L2_attn_in['d_dt_proj_w'], 'L2_attn_d_dt_proj_b': _L2_attn_in['d_dt_proj_b'], 'L2_attn_d_A_log': _L2_attn_in['d_A_log'], 'L2_attn_d_D_param': _L2_attn_in['d_D_param'], 'L2_attn_d_out_proj_w': _L2_attn_in['d_out_proj_w'], 'L2_ffn_gate_w': _L2_ffn_in['gate_w'], 'L2_ffn_gate_b': _L2_ffn_in['gate_b'], 'L2_ffn_w1': _L2_ffn_in['w1'], 'L2_ffn_b1': _L2_ffn_in['b1'], 'L2_ffn_w2': _L2_ffn_in['w2'], 'L2_ffn_b2': _L2_ffn_in['b2'], 'L2_ffn_w3': _L2_ffn_in['w3'], 'L2_ffn_b3': _L2_ffn_in['b3'], 'L2_c': _L2_c, 'L2_wmod': _L2_wmod, 'L3_attn_Wq': _L3_attn_in['Wq'], 'L3_attn_bq': _L3_attn_in['bq'], 'L3_attn_Wk': _L3_attn_in['Wk'], 'L3_attn_bk': _L3_attn_in['bk'], 'L3_attn_Wv': _L3_attn_in['Wv'], 'L3_attn_bv': _L3_attn_in['bv'], 'L3_attn_Wo': _L3_attn_in['Wo'], 'L3_attn_bo': _L3_attn_in['bo'], 'L3_ffn_router_w1': _L3_ffn_in['router_w1'], 'L3_ffn_router_w2': _L3_ffn_in['router_w2'], 'L3_ffn_w1': _L3_ffn_in['w1'], 'L3_ffn_w2': _L3_ffn_in['w2'], 'L3_ffn_w3': _L3_ffn_in['w3'], 'L3_c': _L3_c, 'L3_wmod': _L3_wmod}
    _x0 = _d['L0_attn_x']
    _d['L0_attn_x'] = jax.random.normal(jax.random.fold_in(jax.random.key(seed), 1), (2, 1024, 128), dtype=_x0.dtype)
    del _x0
    return _d

def reference(L0_attn_x, L0_attn_in_proj_w, L0_attn_in_proj_b, L0_attn_out_proj_w, L0_attn_out_proj_b, L0_attn_ffn1_w, L0_attn_ffn1_b, L0_attn_ffn2_w, L0_attn_ffn2_b, L0_attn_ln1_w, L0_attn_ln1_b, L0_attn_ln2_w, L0_attn_ln2_b, L0_attn_final_w, L0_attn_final_b, L0_ffn_gate_w, L0_ffn_expert_w, L0_ffn_expert_b, L0_c, L0_wmod, L1_attn_Wq, L1_attn_bq, L1_attn_Wk, L1_attn_bk, L1_attn_Wv, L1_attn_bv, L1_attn_Wo, L1_attn_bo, L1_attn_nrope_freq, L1_ffn_router_w, L1_ffn_router_bias, L1_ffn_sw1, L1_ffn_sw3, L1_ffn_sw2, L1_ffn_ew1, L1_ffn_ew2, L1_c, L1_wmod, L2_attn_diff, L2_attn_h_in_proj_w, L2_attn_h_conv_w, L2_attn_h_conv_b, L2_attn_h_x_proj_w, L2_attn_h_dt_proj_w, L2_attn_h_dt_proj_b, L2_attn_h_A_log, L2_attn_h_D_param, L2_attn_h_out_proj_w, L2_attn_d_in_proj_w, L2_attn_d_conv_w, L2_attn_d_conv_b, L2_attn_d_x_proj_w, L2_attn_d_dt_proj_w, L2_attn_d_dt_proj_b, L2_attn_d_A_log, L2_attn_d_D_param, L2_attn_d_out_proj_w, L2_ffn_gate_w, L2_ffn_gate_b, L2_ffn_w1, L2_ffn_b1, L2_ffn_w2, L2_ffn_b2, L2_ffn_w3, L2_ffn_b3, L2_c, L2_wmod, L3_attn_Wq, L3_attn_bq, L3_attn_Wk, L3_attn_bk, L3_attn_Wv, L3_attn_bv, L3_attn_Wo, L3_attn_bo, L3_ffn_router_w1, L3_ffn_router_w2, L3_ffn_w1, L3_ffn_w2, L3_ffn_w3, L3_c, L3_wmod):

    def _L0_attn_ref(x, in_proj_w, in_proj_b, out_proj_w, out_proj_b, ffn1_w, ffn1_b, ffn2_w, ffn2_b, ln1_w, ln1_b, ln2_w, ln2_b, final_w, final_b):
        import math
        import jax, jax.numpy as jnp
        import numpy as np
        L, D, H, F = (4, 128, 16, 512)
        HD = D // H
        EPS = 1e-05

        def get_alibi_slopes(num_heads):
            closest = 2 ** math.floor(math.log2(num_heads))
            base = 2 ** (-2 ** (-(math.log2(closest) - 3)))
            slopes = base ** np.arange(1, closest + 1)
            if closest != num_heads:
                extra_base = 2 ** (-2 ** (-(math.log2(2 * closest) - 3)))
                extra = extra_base ** np.arange(1, 2 * (num_heads - closest) + 1, 2)
                slopes = np.concatenate([slopes, extra])
            return jnp.asarray(slopes, dtype=jnp.float32)

        def build_mask(num_heads, T):
            pos = jnp.arange(T)
            dist = pos[None, :] - pos[:, None]
            alibi = get_alibi_slopes(num_heads)[:, None, None] * dist[None]
            causal = jnp.where(dist > 0, -jnp.inf, 0.0).astype(jnp.float32)
            return causal[None] + alibi

        def layer_norm(x, w, b):
            mu = jnp.mean(x, axis=-1, keepdims=True)
            var = jnp.mean(jnp.square(x - mu), axis=-1, keepdims=True)
            return (x - mu) * jax.lax.rsqrt(var + EPS) * w + b

        def mha(x, mask, Wi, bi, Wo, bo):
            B, T, _ = x.shape
            qkv = x @ Wi.T + bi
            q, k, v = jnp.split(qkv, 3, axis=-1)
            q = q.reshape(B, T, H, HD).transpose(0, 2, 1, 3)
            k = k.reshape(B, T, H, HD).transpose(0, 2, 1, 3)
            v = v.reshape(B, T, H, HD).transpose(0, 2, 1, 3)
            scores = jnp.einsum('bhqd,bhkd->bhqk', q, k) / math.sqrt(HD)
            scores = scores + mask[None]
            attn = jax.nn.softmax(scores, axis=-1)
            out = jnp.einsum('bhqk,bhkd->bhqd', attn, v)
            out = out.transpose(0, 2, 1, 3).reshape(B, T, D)
            return out @ Wo.T + bo
        T = x.shape[1]
        mask = build_mask(H, T)
        for i in range(L):
            xn = layer_norm(x, ln1_w[i], ln1_b[i])
            x = x + mha(xn, mask, in_proj_w[i], in_proj_b[i], out_proj_w[i], out_proj_b[i])
            xn = layer_norm(x, ln2_w[i], ln2_b[i])
            h = jax.nn.gelu(xn @ ffn1_w[i].T + ffn1_b[i], approximate=False)
            x = x + (h @ ffn2_w[i].T + ffn2_b[i])
        return layer_norm(x, final_w, final_b)

    def _L0_ffn_ref(tokens, gate_w, expert_w, expert_b):
        import jax, jax.numpy as jnp
        import numpy as np
        B, S, H, E = (2, 256, 128, 16)
        b, s, h = tokens.shape
        logits = jnp.einsum('bsh,eh->bse', tokens, gate_w)
        weights = jax.nn.softmax(logits, axis=-1)
        top2_w, top2_idx = jax.lax.top_k(weights, 2)
        flat = tokens.reshape(b * s, h)
        flat_w = top2_w.reshape(b * s, 2)
        flat_idx = top2_idx.reshape(b * s, 2)
        y = jax.nn.relu(jnp.einsum('nh,edh->ned', flat, expert_w) + expert_b[None, :, :])
        sel = jnp.take_along_axis(y, flat_idx[:, :, None], axis=1)
        out = jnp.sum(sel * flat_w[:, :, None], axis=1)
        return out.reshape(b, s, h)

    def _L1_attn_ref(x, Wq, bq, Wk, bk, Wv, bv, Wo, bo, nrope_freq):
        import jax, jax.numpy as jnp
        import numpy as np
        BASE_FREQUENCY = 10000.0
        LRP = 17
        MIN_L = 1.0 - LRP / 100.0
        SDT_L = (BASE_FREQUENCY - MIN_L * BASE_FREQUENCY) * 2.0
        ARM_ATTENTION = 2.0
        HEADS_DIM = 64

        def _nrope(xs, base, angle_range):
            N, T, d = xs.shape
            half = d // 2
            inv_freq = base ** (-jnp.arange(half, dtype=jnp.float32) / half)
            pos = jnp.arange(T, dtype=jnp.float32)
            scale = angle_range / jnp.maximum(T - 1, 1)
            ang = pos[:, None] * inv_freq[None, :] * scale
            cos, sin = (jnp.cos(ang), jnp.sin(ang))
            x1, x2 = (xs[..., :half], xs[..., half:])
            return jnp.concatenate([x1 * cos - x2 * sin, x1 * sin + x2 * cos], axis=-1)
        B, T, E = x.shape
        HD = HEADS_DIM
        H = E // HD
        half = HD // 2
        q = (x @ Wq + bq).reshape(B, T, H, HD).transpose(0, 2, 1, 3)
        k = (x @ Wk + bk).reshape(B, T, H, HD).transpose(0, 2, 1, 3)
        v = (x @ Wv + bv).reshape(B, T, H, HD).transpose(0, 2, 1, 3)
        q_content, q_spatial = (q[..., :half], q[..., half:])
        k_content, k_spatial = (k[..., :half], k[..., half:])
        base = jax.nn.sigmoid(nrope_freq[0]) * SDT_L + MIN_L * BASE_FREQUENCY
        rng = ARM_ATTENTION * jnp.pi
        q_spatial = _nrope(q_spatial.reshape(B * H, T, half), base, rng).reshape(B, H, T, half)
        k_spatial = _nrope(k_spatial.reshape(B * H, T, half), base, rng).reshape(B, H, T, half)
        q = jnp.concatenate([q_content, q_spatial], axis=-1)
        k = jnp.concatenate([k_content, k_spatial], axis=-1)
        score = jnp.einsum('bhqd,bhkd->bhqk', q, k) / jnp.sqrt(jnp.float32(HD))
        attn = jax.nn.softmax(score, axis=-1)
        out = jnp.einsum('bhqk,bhkd->bhqd', attn, v)
        out = out.transpose(0, 2, 1, 3).reshape(B, T, E)
        return out @ Wo + bo

    def _L1_ffn_ref(x, router_w, router_bias, sw1, sw3, sw2, ew1, ew2):
        import jax, jax.numpy as jnp
        import numpy as np
        D_MODEL = 128
        H_SHARED = 256
        H_ROUTED = 128
        N_EXPERTS = 8
        TOP_K = 2
        B, T, C = x.shape
        xf = x.reshape(-1, C)
        shared_out = jax.nn.silu(xf @ sw1) * (xf @ sw3) @ sw2
        s = jax.nn.sigmoid((xf @ router_w.T).astype(jnp.float32))
        sel_scores = s + router_bias.astype(jnp.float32)
        _, topk_idx = jax.lax.top_k(sel_scores, TOP_K)
        s_sel = jnp.take_along_axis(s, topk_idx, axis=1)
        denom = s_sel.sum(axis=1, keepdims=True)
        gates = jnp.where(denom > 1e-09, s_sel / (denom + 1e-09), 1.0 / TOP_K).astype(x.dtype)
        one_hot = jax.nn.one_hot(topk_idx, N_EXPERTS, dtype=x.dtype)
        comb = jnp.einsum('nke,nk->ne', one_hot, gates)
        h = jax.nn.gelu(jnp.einsum('nd,edh->neh', xf, ew1), approximate=False)
        y = jnp.einsum('neh,ehd->ned', h, ew2)
        routed_out = jnp.einsum('ned,ne->nd', y, comb)
        return (shared_out + routed_out).reshape(B, T, C)

    def _L2_attn_ref(hidden, diff, h_in_proj_w, h_conv_w, h_conv_b, h_x_proj_w, h_dt_proj_w, h_dt_proj_b, h_A_log, h_D_param, h_out_proj_w, d_in_proj_w, d_conv_w, d_conv_b, d_x_proj_w, d_dt_proj_w, d_dt_proj_b, d_A_log, d_D_param, d_out_proj_w):
        import jax, jax.numpy as jnp
        import numpy as np
        from jax import lax
        D_MODEL = 128
        D_STATE = 16
        D_CONV = 4
        EXPAND = 2
        D_INNER = EXPAND * D_MODEL
        DT_RANK = (D_MODEL + 15) // 16
        BATCH = 4
        SEQLEN = 128

        def _silu(x):
            return x * jax.nn.sigmoid(x)

        def _init_block(key):
            ks = jax.random.split(key, 5)
            s = 0.02
            in_proj_w = jax.random.normal(ks[0], (2 * D_INNER, D_MODEL), jnp.float32) * s
            conv_w = jax.random.normal(ks[1], (D_INNER, D_CONV), jnp.float32) * s
            conv_b = jnp.zeros((D_INNER,), jnp.float32)
            x_proj_w = jax.random.normal(ks[2], (DT_RANK + 2 * D_STATE, D_INNER), jnp.float32) * s
            dt_proj_w = jax.random.normal(ks[3], (D_INNER, DT_RANK), jnp.float32) * DT_RANK ** (-0.5)
            dt_proj_b = jnp.log(jnp.expm1(jnp.full((D_INNER,), 0.01, jnp.float32)))
            A_log = jnp.log(jnp.broadcast_to(jnp.arange(1, D_STATE + 1, dtype=jnp.float32), (D_INNER, D_STATE)))
            D_param = jnp.ones((D_INNER,), jnp.float32)
            out_proj_w = jax.random.normal(ks[4], (D_MODEL, D_INNER), jnp.float32) * s
            return (in_proj_w, conv_w, conv_b, x_proj_w, dt_proj_w, dt_proj_b, A_log, D_param, out_proj_w)

        def _mamba(x, in_proj_w, conv_w, conv_b, x_proj_w, dt_proj_w, dt_proj_b, A_log, D_param, out_proj_w):
            B, L, _ = x.shape
            xz = jnp.einsum('bld,ed->ble', x, in_proj_w)
            x_in, z = jnp.split(xz, 2, axis=-1)
            x_c = x_in.swapaxes(1, 2)
            x_c = lax.conv_general_dilated(x_c, conv_w[:, None, :], window_strides=(1,), padding=[(D_CONV - 1, 0)], feature_group_count=D_INNER, dimension_numbers=('NCH', 'OIH', 'NCH'))
            x_c = x_c + conv_b[None, :, None]
            u = _silu(x_c).swapaxes(1, 2)
            x_dbl = jnp.einsum('bld,ed->ble', u, x_proj_w)
            dt, Bm, Cm = jnp.split(x_dbl, [DT_RANK, DT_RANK + D_STATE], axis=-1)
            delta = jax.nn.softplus(jnp.einsum('blr,dr->bld', dt, dt_proj_w) + dt_proj_b)
            A = -jnp.exp(A_log)

            def step(h, inp):
                d_t, b_t, c_t, u_t = inp
                h = h * jnp.exp(d_t[:, :, None] * A) + (d_t * u_t)[:, :, None] * b_t[:, None, :]
                y = jnp.einsum('bdn,bn->bd', h, c_t)
                return (h, y)
            h0 = jnp.zeros((B, D_INNER, D_STATE), x.dtype)
            xs = (delta.swapaxes(0, 1), Bm.swapaxes(0, 1), Cm.swapaxes(0, 1), u.swapaxes(0, 1))
            _, ys = lax.scan(step, h0, xs)
            y = ys.swapaxes(0, 1) + u * D_param
            y = y * _silu(z)
            return jnp.einsum('bld,ed->ble', y, out_proj_w)

        def _reference_tuple_inner(hidden, diff, h_in_proj_w, h_conv_w, h_conv_b, h_x_proj_w, h_dt_proj_w, h_dt_proj_b, h_A_log, h_D_param, h_out_proj_w, d_in_proj_w, d_conv_w, d_conv_b, d_x_proj_w, d_dt_proj_w, d_dt_proj_b, d_A_log, d_D_param, d_out_proj_w):
            hidden_out = _mamba(hidden, h_in_proj_w, h_conv_w, h_conv_b, h_x_proj_w, h_dt_proj_w, h_dt_proj_b, h_A_log, h_D_param, h_out_proj_w)
            diff_out = _mamba(diff, d_in_proj_w, d_conv_w, d_conv_b, d_x_proj_w, d_dt_proj_w, d_dt_proj_b, d_A_log, d_D_param, d_out_proj_w)
            return (hidden_out, diff_out)
        return _reference_tuple_inner(hidden, diff, h_in_proj_w, h_conv_w, h_conv_b, h_x_proj_w, h_dt_proj_w, h_dt_proj_b, h_A_log, h_D_param, h_out_proj_w, d_in_proj_w, d_conv_w, d_conv_b, d_x_proj_w, d_dt_proj_w, d_dt_proj_b, d_A_log, d_D_param, d_out_proj_w)[0]

    def _L2_ffn_ref(x, gate_w, gate_b, w1, b1, w2, b2, w3, b3):
        import jax, jax.numpy as jnp
        import numpy as np
        B, S, D, O, E, K = (2, 256, 128, 128, 8, 2)
        probs = jax.nn.softmax(x @ gate_w.T + gate_b, axis=-1)
        _, topi = jax.lax.top_k(probs, K)
        onehot = jax.nn.one_hot(topi, E, dtype=probs.dtype)
        cw = jnp.einsum('bske,bsk->bse', onehot, probs[..., :K])
        out = jnp.zeros(x.shape[:2] + (O,), x.dtype)
        for e in range(E):
            h = jax.nn.relu(x @ w1[e] + b1[e])
            h = jax.nn.relu(h @ w2[e] + b2[e])
            h = h @ w3[e] + b3[e]
            out = out + cw[..., e:e + 1] * h
        return out

    def _L3_attn_ref(x, Wq, bq, Wk, bk, Wv, bv, Wo, bo):
        import jax, jax.numpy as jnp
        import numpy as np
        import math
        NUM_HEADS = 16
        DIM = 128
        DH = DIM // NUM_HEADS
        THETA = 10000.0
        SCALE_BASE = 512.0

        def _rotate_half(x):
            x = x.reshape(*x.shape[:-1], -1, 2)
            x1, x2 = (x[..., 0], x[..., 1])
            return jnp.stack((-x2, x1), axis=-1).reshape(*x1.shape[:-1], -1)

        def _xpos_rotate(q, k):
            s = q.shape[2]
            t = jnp.arange(s, dtype=jnp.float32)
            inv_freq = 1.0 / THETA ** (jnp.arange(0, DH, 2, dtype=jnp.float32) / DH)
            freqs = t[:, None] * inv_freq[None, :]
            freqs = jnp.repeat(freqs, 2, axis=-1)
            cos, sin = (jnp.cos(freqs), jnp.sin(freqs))
            base = (jnp.arange(0, DH, 2, dtype=jnp.float32) + 0.4 * DH) / (1.4 * DH)
            power = (t - s // 2) / SCALE_BASE
            scale = base[None, :] ** power[:, None]
            scale = jnp.concatenate((scale, scale), axis=-1)
            q = q * cos * scale + _rotate_half(q) * sin * scale
            inv_scale = 1.0 / scale
            k = k * cos * inv_scale + _rotate_half(k) * sin * inv_scale
            return (q, k)
        b, s, _ = x.shape

        def split_heads(t):
            return t.reshape(b, s, NUM_HEADS, DH).transpose(0, 2, 1, 3)
        q_mat = split_heads(x @ Wq.T + bq)
        k_mat = split_heads(x @ Wv.T + bv)
        v_mat = split_heads(x @ Wk.T + bk)
        q_mat, k_mat = _xpos_rotate(q_mat, k_mat)
        scores = jnp.einsum('bhqd,bhkd->bhqk', q_mat, k_mat) / math.sqrt(DH * NUM_HEADS)
        causal = jnp.tril(jnp.ones((s, s), dtype=bool))
        scores = jnp.where(causal[None, None], scores, -jnp.inf)
        weights = jax.nn.softmax(scores, axis=-1)
        inter = jnp.einsum('bhqk,bhkd->bhqd', weights, v_mat)
        inter = inter.transpose(0, 2, 1, 3).reshape(b, s, DIM)
        return inter @ Wo.T + bo

    def _L3_ffn_ref(hidden_states, router_w1, router_w2, w1, w2, w3):
        import jax, jax.numpy as jnp
        import numpy as np
        import math
        B, S, D = (4, 256, 128)
        E, DFF = (16, 256)
        CAP_FACTOR = 2.0
        ROUTER_HIDDEN = 128
        CAPACITY = int(math.ceil(S * CAP_FACTOR / E))
        b, s, d = hidden_states.shape
        e = w1.shape[0]
        cap = CAPACITY
        router_logits = jax.nn.silu(hidden_states @ router_w1) @ router_w2
        expert_probs = jax.nn.softmax(router_logits.transpose(0, 2, 1), axis=-1)
        expert_weights, token_indices = jax.lax.top_k(expert_probs, cap)
        expert_weights = expert_weights / (expert_weights.sum(-1, keepdims=True) + 1e-09)
        expert_inputs = jax.vmap(lambda h, i: h[i])(hidden_states, token_indices)
        gate = jax.nn.silu(jnp.einsum('becd,edf->becf', expert_inputs, w1))
        value = jnp.einsum('becd,edf->becf', expert_inputs, w2)
        expert_out = jnp.einsum('becf,efd->becd', gate * value, w3)
        weighted = expert_out * expert_weights[..., None]

        def combine(idx, vals):
            return jnp.zeros((s, d), vals.dtype).at[idx.reshape(-1)].add(vals.reshape(-1, d))
        output = jax.vmap(combine)(token_indices, weighted)
        return output
    x = L0_attn_x
    mod = (_silu(L0_c) @ L0_wmod).reshape(L0_c.shape[0], 6, 1, -1)
    sa, ca, ga, sb, cb, gb = (mod[:, 0], mod[:, 1], mod[:, 2], mod[:, 3], mod[:, 4], mod[:, 5])
    ga = (2 * (ga >= 0) - 1) * jnp.maximum(jnp.abs(ga), 0.25)
    gb = (2 * (gb >= 0) - 1) * jnp.maximum(jnp.abs(gb), 0.25)
    h = _layernorm(x, axis=-1) * (1 + ca) + sa
    x = x + ga * _L0_attn_ref(h, L0_attn_in_proj_w, L0_attn_in_proj_b, L0_attn_out_proj_w, L0_attn_out_proj_b, L0_attn_ffn1_w, L0_attn_ffn1_b, L0_attn_ffn2_w, L0_attn_ffn2_b, L0_attn_ln1_w, L0_attn_ln1_b, L0_attn_ln2_w, L0_attn_ln2_b, L0_attn_final_w, L0_attn_final_b)
    h = _layernorm(x, axis=-1) * (1 + cb) + sb
    x = x + gb * _L0_ffn_ref(h, L0_ffn_gate_w, L0_ffn_expert_w, L0_ffn_expert_b)
    mod = (_silu(L1_c) @ L1_wmod).reshape(L1_c.shape[0], 6, 1, -1)
    sa, ca, ga, sb, cb, gb = (mod[:, 0], mod[:, 1], mod[:, 2], mod[:, 3], mod[:, 4], mod[:, 5])
    ga = (2 * (ga >= 0) - 1) * jnp.maximum(jnp.abs(ga), 0.25)
    gb = (2 * (gb >= 0) - 1) * jnp.maximum(jnp.abs(gb), 0.25)
    h = _layernorm(x, axis=-1) * (1 + ca) + sa
    x = x + ga * _L1_attn_ref(h, L1_attn_Wq, L1_attn_bq, L1_attn_Wk, L1_attn_bk, L1_attn_Wv, L1_attn_bv, L1_attn_Wo, L1_attn_bo, L1_attn_nrope_freq)
    h = _layernorm(x, axis=-1) * (1 + cb) + sb
    x = x + gb * _L1_ffn_ref(h, L1_ffn_router_w, L1_ffn_router_bias, L1_ffn_sw1, L1_ffn_sw3, L1_ffn_sw2, L1_ffn_ew1, L1_ffn_ew2)
    mod = (_silu(L2_c) @ L2_wmod).reshape(L2_c.shape[0], 6, 1, -1)
    sa, ca, ga, sb, cb, gb = (mod[:, 0], mod[:, 1], mod[:, 2], mod[:, 3], mod[:, 4], mod[:, 5])
    ga = (2 * (ga >= 0) - 1) * jnp.maximum(jnp.abs(ga), 0.25)
    gb = (2 * (gb >= 0) - 1) * jnp.maximum(jnp.abs(gb), 0.25)
    h = _layernorm(x, axis=-1) * (1 + ca) + sa
    x = x + ga * _L2_attn_ref(h, L2_attn_diff, L2_attn_h_in_proj_w, L2_attn_h_conv_w, L2_attn_h_conv_b, L2_attn_h_x_proj_w, L2_attn_h_dt_proj_w, L2_attn_h_dt_proj_b, L2_attn_h_A_log, L2_attn_h_D_param, L2_attn_h_out_proj_w, L2_attn_d_in_proj_w, L2_attn_d_conv_w, L2_attn_d_conv_b, L2_attn_d_x_proj_w, L2_attn_d_dt_proj_w, L2_attn_d_dt_proj_b, L2_attn_d_A_log, L2_attn_d_D_param, L2_attn_d_out_proj_w)
    h = _layernorm(x, axis=-1) * (1 + cb) + sb
    x = x + gb * _L2_ffn_ref(h, L2_ffn_gate_w, L2_ffn_gate_b, L2_ffn_w1, L2_ffn_b1, L2_ffn_w2, L2_ffn_b2, L2_ffn_w3, L2_ffn_b3)
    mod = (_silu(L3_c) @ L3_wmod).reshape(L3_c.shape[0], 6, 1, -1)
    sa, ca, ga, sb, cb, gb = (mod[:, 0], mod[:, 1], mod[:, 2], mod[:, 3], mod[:, 4], mod[:, 5])
    ga = (2 * (ga >= 0) - 1) * jnp.maximum(jnp.abs(ga), 0.25)
    gb = (2 * (gb >= 0) - 1) * jnp.maximum(jnp.abs(gb), 0.25)
    h = _layernorm(x, axis=-1) * (1 + ca) + sa
    x = x + ga * _L3_attn_ref(h, L3_attn_Wq, L3_attn_bq, L3_attn_Wk, L3_attn_bk, L3_attn_Wv, L3_attn_bv, L3_attn_Wo, L3_attn_bo)
    h = _layernorm(x, axis=-1) * (1 + cb) + sb
    x = x + gb * _L3_ffn_ref(h, L3_ffn_router_w1, L3_ffn_router_w2, L3_ffn_w1, L3_ffn_w2, L3_ffn_w3)
    return x

_drawn_inputs = setup_inputs


def setup_inputs(seed=0):
    import zlib

    import numpy as np

    out = dict(_drawn_inputs(seed))
    spreads = {'L0_attn_in_proj_b': (0.0, 0.431),
     'L0_attn_out_proj_b': (0.0, 0.1),
     'L0_attn_ffn1_b': (0.0, 0.423),
     'L0_attn_ffn2_b': (0.0, 0.1),
     'L0_attn_ln1_w': (1.0, 0.6),
     'L0_attn_ln1_b': (0.0, 0.8),
     'L0_attn_ln2_w': (1.0, 0.6),
     'L0_attn_ln2_b': (0.0, 0.8),
     'L0_attn_final_w': (1.0, 0.2),
     'L0_attn_final_b': (0.0, 0.1),
     'L1_attn_bq': (0.0, 0.8),
     'L1_attn_bk': (0.0, 0.8),
     'L1_attn_bv': (0.0, 0.75),
     'L1_attn_bo': (0.0, 0.272),
     'L1_ffn_router_bias': (0.0, 0.1),
     'L2_attn_h_conv_b': (0.0, 0.8),
     'L2_attn_h_dt_proj_b': (-4.600166320800781, 0.6),
     'L2_attn_h_D_param': (1.0, 0.6),
     'L2_attn_d_conv_b': (0.0, 0.1),
     'L2_attn_d_dt_proj_b': (-4.600166320800781, 0.2),
     'L2_attn_d_D_param': (1.0, 0.2),
     'L2_ffn_gate_b': (0.0, 2.0),
     'L2_ffn_b1': (0.0, 2.0),
     'L2_ffn_b2': (0.0, 2.0),
     'L2_ffn_b3': (0.0, 2.0),
     'L3_attn_bq': (0.0, 2.0),
     'L3_attn_bk': (0.0, 2.0),
     'L3_attn_bv': (0.0, 2.0),
     'L3_attn_bo': (0.0, 2.0)}
    factors = {'L0_attn_in_proj_w': 4.27,
     'L0_attn_out_proj_w': 2.953,
     'L0_ffn_expert_b': 36.347,
     'L1_attn_Wq': 8.0,
     'L1_attn_Wk': 8.0,
     'L1_attn_Wv': 8.0,
     'L1_attn_Wo': 5.776,
     'L2_attn_h_in_proj_w': 8.0,
     'L2_attn_h_conv_w': 8.0,
     'L2_attn_h_x_proj_w': 8.0,
     'L2_attn_h_dt_proj_w': 8.0,
     'L2_attn_h_A_log': 8.0,
     'L2_attn_h_out_proj_w': 8.0,
     'L2_ffn_w1': 21.72,
     'L3_attn_Wq': 64.0,
     'L3_attn_Wv': 64.0,
     'L3_ffn_router_w1': 23.086,
     'L3_ffn_router_w2': 22.684,
     'L3_ffn_w1': 26.366,
     'L3_ffn_w2': 21.641,
     'L3_ffn_w3': 22.689,
     'L2_ffn_gate_w': 8.0,
     'L2_ffn_w2': 8.0,
     'L2_ffn_w3': 8.0,
     'L3_attn_Wk': 8.0,
     'L3_attn_Wo': 8.0}
    for name, (base, spread) in spreads.items():
        noise = np.random.default_rng([zlib.crc32(name.encode()), seed]).standard_normal(out[name].shape)
        drawn = base * np.exp(spread * noise) if base else spread * noise
        out[name] = jnp.asarray(drawn.astype(out[name].dtype))
    for name, factor in factors.items():
        out[name] = (out[name] * factor).astype(out[name].dtype)
    return out
```

```python
from contextlib import ExitStack, contextmanager

import numpy as np
import concourse.bass as bass
from concourse import mybir

F32 = mybir.dt.float32
BF16 = mybir.dt.bfloat16
U32 = mybir.dt.uint32
ALU = mybir.AluOpType
ACT = mybir.ActivationFunctionType
AX_X = mybir.AxisListType.X

P = 128
B, T = 2, 1024
N = B * T
CH = 512
NCH = N // CH
NBLK = N // P
HEADS, DH = 16, 8
NEG = -1.0e30
LN_EPS = 1e-5

PAIR_ROWS = 9 * DH
BIAS_ROWS = 6
MAX_ROWS = 3
S1_ROWS = PAIR_ROWS + BIAS_ROWS
S2_ROWS = S1_ROWS + MAX_ROWS
GROUP = 4
NGRP = HEADS // GROUP
QB = T // P
STACKS = 3

L0_COLS = {}
_at = 0
for _name, _w in (("wq", P), ("wk", P), ("wv", P), ("bv", P), ("wo", NGRP * P), ("w1", 4 * P), ("w2", 4 * P),
                  ("bq", 1), ("bk", 1), ("bo", 1), ("b1", 4), ("b2", 1),
                  ("ln1w", 1), ("ln1b", 1), ("ln2w", 1), ("ln2b", 1)):
    L0_COLS[_name] = (_at, _at + _w)
    _at += _w
L0_WIDTH = _at


_used = {}


def sbuf(nc, name, shape, dt=F32):
    n = _used[name] = _used.get(name, 0) + 1
    return nc.sbuf_tensor(f"sb_{name}_{n}", shape, dt)


@contextmanager
def phase(nc, *names):
    with ExitStack() as ctx:
        sems = [ctx.enter_context(nc.semaphore(n)) for n in names]
        with nc.Block(no_gpsimd_drain=True) as block:
            yield (block, *sems)
        nc.all_engine_barrier(sems_to_clear=range(sems[0].num, sems[-1].num + 1))


def chunk(t, c):
    return t[:, c * CH:(c + 1) * CH]


class Memory:
    pass


def setup(nc, M, D, ctx):
    def sb(name, shape, dt=F32):
        return ctx.enter_context(sbuf(nc, name, shape, dt))

    M.x = sb("x_T", [P, N])
    M.h = sb("h_T", [P, N])
    M.mean = sb("mean_weights", [P, P])
    M.ident = sb("ident", [P, P])
    M.identb = sb("ident_bf16", [P, P], BF16)
    M.mask_qk = sb("mask_qk", [P, P], BF16)
    M.mask_kq = sb("mask_kq", [P, P], BF16)
    M.eps = sb("eps", [P, 1])
    M.mod = sb("mod", [P, 4, 6, B])
    M.ps = ctx.enter_context(nc.psum_tensor("ps", [P, 8, CH], F32))
    with ExitStack() as tmp:
        wmod = tmp.enter_context(sbuf(nc, "wmod", [P, 4, 6 * P], F32))
        cT = tmp.enter_context(sbuf(nc, "c_T", [P, 4, B], F32))
        cs = tmp.enter_context(sbuf(nc, "silu_c", [P, 4, B], F32))
        sg = tmp.enter_context(sbuf(nc, "gate_sign", [P, 4, B], F32))
        ab = tmp.enter_context(sbuf(nc, "gate_abs", [P, 4, B], F32))
        with phase(nc, "loaded", "zeroed", "consts", "silu_ready", "mod_ps", "mod_sb", "gates") as (
                block, loaded, zeroed, consts, silu_ready, mod_ps, mod_sb, gates):
            @block.sync
            def _(sp):
                sp.dma_start(cT[:], D["c_T"].rearrange("p (l b) -> p l b", b=B)).then_inc(loaded, 16)
                sp.dma_start(wmod[:], D["wmod"].rearrange("p (l n) -> p l n", l=4)).then_inc(loaded, 16)
                sp.dma_start(M.x[:], D["x_T"]).then_inc(loaded, 16)
                sp.wait_ge(loaded, 48)

            @block.gpsimd
            def _(pool):
                pool.memset(M.mean[:], 1.0 / P).then_inc(consts, 1)
                pool.memset(M.eps[:], LN_EPS).then_inc(consts, 1)
                for t in (M.ident, M.identb, M.mask_qk, M.mask_kq):
                    pool.memset(t[:], 0.0).then_inc(zeroed, 1)
                pool.wait_ge(zeroed, 4)
                for t in (M.ident, M.identb):
                    pool.affine_select(out=t[:], in_=t[:], compare_op=ALU.not_equal, fill=1.0, base=0,
                                       pattern=[[-1, P]], channel_multiplier=1).then_inc(consts, 1)
                pool.affine_select(out=M.mask_qk[:], in_=M.mask_qk[:], compare_op=ALU.is_ge, fill=NEG, base=0,
                                   pattern=[[-1, P]], channel_multiplier=1).then_inc(consts, 1)
                pool.affine_select(out=M.mask_kq[:], in_=M.mask_kq[:], compare_op=ALU.is_ge, fill=NEG, base=0,
                                   pattern=[[1, P]], channel_multiplier=-1).then_inc(consts, 1)
                pool.wait_ge(consts, 6)

            @block.scalar
            def _(act):
                act.wait_ge(loaded, 48)
                act.activation(cs[:], cT[:], ACT.Silu).then_inc(silu_ready, 1)

            @block.tensor
            def _(pe):
                pe.wait_ge(loaded, 48)
                pe.wait_ge(silu_ready, 1)
                for layer in range(4):
                    for part in range(6):
                        at = (layer * 6 + part) * B
                        mm = pe.matmul(M.ps[:, 0, at:at + B], wmod[:, layer, part * P:(part + 1) * P],
                                       cs[:, layer, :], start=True, stop=True)
                mm.then_inc(mod_ps, 1)

            @block.vector
            def _(dve):
                dve.wait_ge(mod_ps, 1)
                dve.tensor_copy(M.mod[:].rearrange("p l s b -> p (l s b)"), M.ps[:, 0, 0:48]).then_inc(mod_sb, 1)
                dve.wait_ge(mod_sb, 1)
                done = 0
                for part in (2, 5):
                    g = M.mod[:, :, part, :]
                    dve.tensor_scalar(sg[:], g, 0.0, 2.0, ALU.is_ge, ALU.mult).then_inc(gates, 1)
                    dve.wait_ge(gates, done + 1)
                    dve.tensor_scalar(sg[:], sg[:], -1.0, None, ALU.add).then_inc(gates, 1)
                    dve.wait_ge(gates, done + 2)
                    dve.tensor_tensor(ab[:], sg[:], g, ALU.mult).then_inc(gates, 1)
                    dve.wait_ge(gates, done + 3)
                    dve.scalar_tensor_tensor(g, ab[:], 0.25, sg[:], ALU.max, ALU.mult).then_inc(gates, 1)
                    dve.wait_ge(gates, done + 4)
                    done += 4
                for part in (1, 4):
                    g = M.mod[:, :, part, :]
                    dve.tensor_scalar(g, g, 1.0, None, ALU.add).then_inc(gates, 1)


def layer_norm(nc, M, src, dst, scale, shift, load=None):
    with ExitStack() as tmp:
        cen = tmp.enter_context(sbuf(nc, "ln_centred", [P, N], F32))
        sqr = tmp.enter_context(sbuf(nc, "ln_squares", [P, N], F32))
        std = tmp.enter_context(sbuf(nc, "ln_std", [P, N], F32))
        with phase(nc, "mean_ready", "centred", "squared", "var_ready", "std_ready", "rstd_ready", "normed",
                   "loaded") as (block, mean_ready, centred, squared, var_ready, std_ready, rstd_ready, normed,
                                 loaded):
            @block.tensor
            def _(pe):
                for c in range(NCH):
                    pe.matmul(M.ps[:, c, :], M.mean[:], chunk(src, c), start=True, stop=True).then_inc(mean_ready, 1)
                for c in range(NCH):
                    pe.wait_ge(squared, c + 1)
                    pe.matmul(M.ps[:, 4 + c, :], M.mean[:], chunk(sqr, c), start=True,
                              stop=True).then_inc(var_ready, 1)

            @block.vector
            def _(dve):
                for c in range(NCH):
                    dve.wait_ge(mean_ready, c + 1)
                    dve.tensor_tensor(chunk(cen, c), chunk(src, c), M.ps[:, c, :], ALU.subtract).then_inc(centred, 1)
                for c in range(NCH):
                    dve.wait_ge(std_ready, c + 1)
                    dve.reciprocal(chunk(sqr, c), chunk(std, c)).then_inc(rstd_ready, 1)

            @block.scalar
            def _(act):
                for c in range(NCH):
                    act.wait_ge(centred, c + 1)
                    act.activation(chunk(sqr, c), chunk(cen, c), ACT.Square).then_inc(squared, 1)
                for c in range(NCH):
                    act.wait_ge(var_ready, c + 1)
                    act.activation(chunk(std, c), M.ps[:, 4 + c, :], ACT.Sqrt, bias=M.eps[:]).then_inc(std_ready, 1)
                for c in range(NCH):
                    act.wait_ge(normed, c + 1)
                    act.activation(chunk(dst, c), chunk(cen, c), ACT.Identity, bias=shift(c // 2),
                                   scale=scale(c // 2))

            @block.gpsimd
            def _(pool):
                for c in range(NCH):
                    pool.wait_ge(rstd_ready, c + 1)
                    pool.tensor_tensor(chunk(cen, c), chunk(cen, c), chunk(sqr, c), ALU.mult).then_inc(normed, 1)

            @block.sync
            def _(sp):
                if load is not None:
                    sp.dma_start(*load).then_inc(loaded, 16)
                    sp.wait_ge(loaded, 16)


class Attention:

    def __init__(self, nc, D, ctx):
        def sb(name, shape, dt=F32):
            return ctx.enter_context(sbuf(nc, name, shape, dt))
        self.q_dram, self.k_dram = D["q_parts"], D["k_parts"]
        self.v = sb("v_and_one", [P, NBLK, HEADS, DH + 1])
        self.qst = sb("q_stack", [S2_ROWS, STACKS, GROUP, T], BF16)
        self.kst = sb("k_stack", [S2_ROWS, STACKS, GROUP, T], BF16)
        self.o = sb("o_raw", [P, B, NGRP, T])
        self.pick = sb("pick_sums", [P, P])
        with phase(nc, "ones_set", "aux_loaded") as (block, ones_set, aux_loaded):
            @block.gpsimd
            def _(pool):
                pool.memset(self.v[:, :, :, DH:DH + 1], 1.0).then_inc(ones_set, 1)

            @block.sync
            def _(sp):
                for s in range(STACKS):
                    for j in range(GROUP):
                        sp.dma_start(self.kst[PAIR_ROWS:S2_ROWS, s, j, :], D["k_aux"]).then_inc(aux_loaded, 16)
                sp.dma_start(self.pick[:], D["pick_sums"]).then_inc(aux_loaded, 16)
                sp.wait_ge(aux_loaded, 16 * (STACKS * GROUP + 1))


def qkv(nc, M, A, W, cols, scale, tables=None):
    with ExitStack() as tmp:
        full = tmp.enter_context(sbuf(nc, "qk_full", [P, 8, CH], F32))
        rem = tmp.enter_context(sbuf(nc, "qk_rest", [P, 8, CH], F32))
        parts = tmp.enter_context(sbuf(nc, "qk_parts", [P, 2, 3, N], BF16))
        units = [(what, c) for c in range(NCH) for what in range(2)]

        def col(name):
            a, b = cols[name]
            return W[:, a:b]

        with phase(nc, "proj_ready", "part_a", "part_b", "full_ready", "hi_ready", "rest_ready", "mid_ready",
                   "lo_ready", "v_ready", "parts_out") as (
                block, proj_ready, part_a, part_b, full_ready, hi_ready, rest_ready, mid_ready, lo_ready, v_ready,
                parts_out):
            @block.tensor
            def _(pe):
                for u, (what, c) in enumerate(units):
                    if u >= 2:
                        pe.wait_ge(full_ready if tables is None else part_b, u - 1)
                    mm = pe.matmul(M.ps[:, u % 2, :], col("wq" if what == 0 else "wk"), chunk(M.h, c),
                                   start=True, stop=True)
                    if tables is not None:
                        mm = pe.matmul(M.ps[:, 2 + u % 2, :], col("wqr" if what == 0 else "wkr"), chunk(M.h, c),
                                       start=True, stop=True)
                    mm.then_inc(proj_ready, 1)
                for blk in range(NBLK):
                    mm = pe.matmul(M.ps[:, 4 + blk // 4, (blk % 4) * P:(blk % 4 + 1) * P],
                                   M.h[:, blk * P:(blk + 1) * P], col("wv"), start=True, stop=True)
                    if blk % 4 == 3:
                        mm.then_inc(v_ready, 1)

            @block.vector
            def _(dve):
                def rest(u):
                    what, c = units[u]
                    part = parts[:, what]
                    dve.wait_ge(hi_ready, u + 1)
                    dve.wait_ge(full_ready, u + 1)
                    dve.tensor_tensor(rem[:, u, :], full[:, u, :], part[:, 0, c * CH:(c + 1) * CH],
                                      ALU.subtract).then_inc(rest_ready, 1)

                for u, (what, c) in enumerate(units):
                    dve.wait_ge(proj_ready, u + 1)
                    bias = col("bq" if what == 0 else "bk")
                    if tables is None:
                        dve.tensor_scalar(full[:, u, :], M.ps[:, u % 2, :], bias, scale if what == 0 else 1.0,
                                          ALU.add, ALU.mult).then_inc(full_ready, 1)
                    else:
                        plain, swapped = tables(what, c)
                        dve.scalar_tensor_tensor(rem[:, u, :], M.ps[:, u % 2, :], bias, plain,
                                                 ALU.add, ALU.mult).then_inc(part_a, 1)
                        bias = col("bqr" if what == 0 else "bkr")
                        dve.scalar_tensor_tensor(full[:, u, :], M.ps[:, 2 + u % 2, :], bias, swapped,
                                                 ALU.add, ALU.mult).then_inc(part_b, 1)
                        dve.wait_ge(part_a, u + 1)
                        dve.wait_ge(part_b, u + 1)
                        dve.tensor_tensor(full[:, u, :], rem[:, u, :], full[:, u, :], ALU.add).then_inc(full_ready, 1)
                    if u:
                        rest(u - 1)
                rest(len(units) - 1)
                bv = col("bv").rearrange("p (h d) -> p h d", h=HEADS)
                for blk in range(NBLK):
                    dve.wait_ge(v_ready, blk // 4 + 1)
                    dve.tensor_tensor(
                        A.v[:, blk, :, 0:DH],
                        M.ps[:, 4 + blk // 4, (blk % 4) * P:(blk % 4 + 1) * P].rearrange("p (h d) -> p h d", h=HEADS),
                        bv, ALU.add)

            @block.scalar
            def _(act):
                def mid(u):
                    what, c = units[u]
                    act.wait_ge(rest_ready, u + 1)
                    act.activation(parts[:, what, 1, c * CH:(c + 1) * CH], rem[:, u, :],
                                   ACT.Copy).then_inc(mid_ready, 1)

                for u, (what, c) in enumerate(units):
                    act.wait_ge(full_ready, u + 1)
                    act.activation(parts[:, what, 0, c * CH:(c + 1) * CH], full[:, u, :],
                                   ACT.Copy).then_inc(hi_ready, 1)
                    if u >= 2:
                        mid(u - 2)
                mid(len(units) - 2)
                mid(len(units) - 1)

            @block.gpsimd
            def _(pool):
                for u, (what, c) in enumerate(units):
                    part = parts[:, what]
                    pool.wait_ge(mid_ready, u + 1)
                    pool.tensor_tensor(part[:, 2, c * CH:(c + 1) * CH], rem[:, u, :],
                                       part[:, 1, c * CH:(c + 1) * CH], ALU.subtract).then_inc(lo_ready, 1)

            @block.sync
            def _(sp):
                for u, (what, c) in enumerate(units):
                    sp.wait_ge(lo_ready, u + 1)
                    sp.dma_start((A.q_dram, A.k_dram)[what][:, :, c * CH:(c + 1) * CH].rearrange("s p t -> p s t"),
                                 parts[:, what, :, c * CH:(c + 1) * CH]).then_inc(parts_out, 16)
                sp.wait_ge(parts_out, 16 * len(units))


def attention_core(nc, M, A, q_aux):
    groups = [(b, g) for b in range(B) for g in range(NGRP)]
    NG = len(groups)
    pieces = [(i, lo, min(lo + CH, (i + 1) * P)) for i in range(QB) for lo in range(0, (i + 1) * P, CH)]
    S1U = GROUP * len(pieces)
    S2U = GROUP * QB
    S1_BANK, S2_BANK, O_BANK = 0, 2, 6
    STACK_DMAS = 9 + 9 + 1
    with ExitStack() as tmp:
        prob = tmp.enter_context(sbuf(nc, "prob", [P, 2, GROUP, T], F32))
        mparts = tmp.enter_context(sbuf(nc, "max_parts", [P, GROUP, QB, 2], F32))
        rowmax = tmp.enter_context(sbuf(nc, "row_max", [P, GROUP * QB], F32))
        mfull = tmp.enter_context(sbuf(nc, "neg_max", [GROUP * QB, P], F32))
        mrest = tmp.enter_context(sbuf(nc, "neg_max_rest", [GROUP * QB, P], F32))
        m3 = tmp.enter_context(sbuf(nc, "neg_max_parts", [GROUP * QB, 3, P], BF16))
        names = [f"stack_loaded{s}" for s in range(STACKS)] + [f"max_rows_in{s}" for s in range(STACKS)]
        with phase(nc, *names, "cleared", "s1_ready", "piece_max", "max_joined", "max_turned", "max_split",
                   "s2_ready", "exp_done", "pv_done", "o_saved") as (block, *sems):
            stack_loaded, max_rows_in = sems[:STACKS], sems[STACKS:2 * STACKS]
            (cleared, s1_ready, piece_max, max_joined, max_turned, max_split, s2_ready, exp_done, pv_done,
             o_saved) = sems[2 * STACKS:]
            SPLITS = 5

            @block.sync
            def _(sp):
                def stack(n):
                    b, g = groups[n]
                    s = n % STACKS
                    tok = slice(b * T, (b + 1) * T)
                    rows = slice(GROUP * DH * g, GROUP * DH * (g + 1))
                    if n >= STACKS:
                        sp.wait_ge(s2_ready, S2U * (n - STACKS + 1))
                    for k_part in range(3):
                        for q_part in range(3):
                            at = (3 * k_part + q_part) * DH
                            for stack_, parts, part in ((A.kst, A.k_dram, k_part), (A.qst, A.q_dram, q_part)):
                                sp.dma_start(stack_[at:at + DH, s, :, :],
                                             parts[part, rows, tok].rearrange("(j d) t -> d j t", j=GROUP)
                                             ).then_inc(stack_loaded[s], 16)
                    sp.dma_start(A.qst[PAIR_ROWS:S1_ROWS, s, :, :], q_aux[g]).then_inc(stack_loaded[s], 16)

                def max_rows(n):
                    s = n % STACKS
                    sp.wait_ge(max_split, SPLITS * (n + 1))
                    for part in range(3):
                        row = S1_ROWS + part
                        sp.dma_start(A.qst[row:row + 1, s, :, :].rearrange("o j (i q) -> o (j i) q", i=QB),
                                     m3[:, part, :]).then_inc(max_rows_in[s], 16)

                for n in range(STACKS):
                    stack(n)
                for n in range(NG):
                    max_rows(n)
                    if n + STACKS < NG:
                        stack(n + STACKS)
                for s in range(STACKS):
                    sp.wait_ge(max_rows_in[s], 48 * len(range(s, NG, STACKS)))

            @block.tensor
            def _(pe):
                def first(n, u):
                    j, (i, lo, hi) = u // len(pieces), pieces[u % len(pieces)]
                    s = n % STACKS
                    total = S1U * n + u
                    if u == 0:
                        pe.wait_ge(stack_loaded[s], 16 * STACK_DMAS * (n // STACKS + 1))
                    if total >= 2:
                        pe.wait_ge(piece_max, total - 1)
                    if u in (0, 1) and n:
                        pe.wait_ge(max_split, SPLITS * (n - 1) + 1)
                    out = M.ps[:, S1_BANK + total % 2, 0:hi - lo]
                    diag = hi == (i + 1) * P
                    mm = pe.matmul(out, A.qst[0:S1_ROWS, s, j, i * P:(i + 1) * P], A.kst[0:S1_ROWS, s, j, lo:hi],
                                   start=True, stop=not diag)
                    if diag:
                        mm = pe.matmul(out[:, hi - lo - P:hi - lo], M.identb[:], M.mask_qk[:], start=False, stop=True)
                    mm.then_inc(s1_ready, 1)

                def turn(n):
                    pe.wait_ge(max_joined, n + 1)
                    pe.transpose(M.ps[0:GROUP * QB, S1_BANK, 0:P], rowmax[:], M.ident[:]).then_inc(max_turned, 1)

                def second(n, kb, j):
                    s = n % STACKS
                    v = S2U * n + kb * GROUP + j
                    if kb == 0 and j == 0:
                        pe.wait_ge(max_rows_in[s], 48 * (n // STACKS + 1))
                    if v >= 2:
                        pe.wait_ge(exp_done, v - 1)
                    base = S2_BANK + 2 * (v % 2)
                    lhs = A.kst[0:S2_ROWS, s, j, kb * P:(kb + 1) * P]
                    diag_bank = kb // 4
                    for half in range(diag_bank, 2):
                        a = max(kb * P - half * CH, 0)
                        q0 = half * CH + a
                        mm = pe.matmul(M.ps[:, base + half, a:CH], lhs, A.qst[0:S2_ROWS, s, j, q0:(half + 1) * CH],
                                       start=True, stop=half != diag_bank)
                        if half == diag_bank:
                            mm = pe.matmul(M.ps[:, base + half, a:a + P], M.identb[:], M.mask_kq[:],
                                           start=False, stop=True)
                    mm.then_inc(s2_ready, 1)

                def weigh(n, kb):
                    b, g = groups[n]
                    pe.wait_ge(exp_done, S2U * n + GROUP * (kb + 1))
                    if kb == 0:
                        pe.wait_ge(cleared, 2)
                    if kb == 0 and n:
                        pe.wait_ge(o_saved, n)
                    for half in range(kb // 4, 2):
                        a = max(kb * P - half * CH, 0)
                        for j in range(GROUP):
                            mm = pe.matmul(M.ps[32 * j:32 * j + DH + 1, O_BANK + half, a:CH],
                                           A.v[:, b * QB + kb, GROUP * g + j, :],
                                           prob[:, kb % 2, j, half * CH + a:(half + 1) * CH],
                                           start=kb == 0, stop=kb == 4 * half + 3)
                    mm.then_inc(pv_done, 1)

                for u in range(S1U):
                    first(0, u)
                turn(0)
                for n in range(NG):
                    u = 0
                    for kb in range(QB):
                        for j in range(GROUP):
                            second(n, kb, j)
                            for _ in range(2):
                                if n + 1 < NG and u < S1U:
                                    first(n + 1, u)
                                    u += 1
                        if kb:
                            weigh(n, kb - 1)
                        if kb == QB - 2 and n + 1 < NG:
                            turn(n + 1)
                    weigh(n, QB - 1)

            @block.vector
            def _(dve):
                dve.memset(mparts[:], -3.0e38).then_inc(cleared, 1)
                dve.memset(M.ps[:, O_BANK:O_BANK + 2, :], 0.0).then_inc(cleared, 1)
                dve.wait_ge(cleared, 2)
                for n in range(NG):
                    for u in range(S1U):
                        total = S1U * n + u
                        j, (i, lo, hi) = u // len(pieces), pieces[u % len(pieces)]
                        dve.wait_ge(s1_ready, total + 1)
                        if u == 0 and n:
                            dve.wait_ge(max_joined, n)
                        dve.reduce_max(mparts[:, j, i, lo // CH:lo // CH + 1],
                                       M.ps[:, S1_BANK + total % 2, 0:hi - lo], AX_X).then_inc(piece_max, 1)
                    dve.wait_ge(piece_max, S1U * (n + 1))
                    if n:
                        dve.wait_ge(max_turned, n)
                    dve.tensor_reduce(rowmax[:], mparts[:].rearrange("p j i c -> p (j i) c"), AX_X,
                                      ALU.max).then_inc(max_joined, 1)
                    dve.wait_ge(max_turned, n + 1)
                    at = SPLITS * n
                    dve.tensor_scalar(mfull[:], M.ps[0:GROUP * QB, S1_BANK, 0:P], -1.0, None,
                                      ALU.mult).then_inc(max_split, 1)
                    dve.wait_ge(max_split, at + 1)
                    if n:
                        dve.wait_ge(max_rows_in[(n - 1) % STACKS], 48 * ((n - 1) // STACKS + 1))
                    dve.tensor_copy(m3[:, 0, :], mfull[:]).then_inc(max_split, 1)
                    dve.wait_ge(max_split, at + 2)
                    dve.tensor_tensor(mrest[:], mfull[:], m3[:, 0, :], ALU.subtract).then_inc(max_split, 1)
                    dve.wait_ge(max_split, at + 3)
                    dve.tensor_copy(m3[:, 1, :], mrest[:]).then_inc(max_split, 1)
                    dve.wait_ge(max_split, at + 4)
                    dve.tensor_tensor(m3[:, 2, :], mrest[:], m3[:, 1, :], ALU.subtract).then_inc(max_split, 1)

            @block.scalar
            def _(act):
                for n in range(NG):
                    b, g = groups[n]
                    for kb in range(QB):
                        for j in range(GROUP):
                            v = S2U * n + kb * GROUP + j
                            act.wait_ge(s2_ready, v + 1)
                            if j == 0 and n * QB + kb >= 2:
                                act.wait_ge(pv_done, n * QB + kb - 1)
                            base = S2_BANK + 2 * (v % 2)
                            scores = M.ps[:, base:base + 2, :].rearrange("p a q -> p (a q)")
                            act.activation(prob[:, kb % 2, j, kb * P:T], scores[:, kb * P:T],
                                           ACT.Exp).then_inc(exp_done, 1)
                    act.wait_ge(pv_done, QB * (n + 1))
                    act.activation(A.o[:, b, g, :], M.ps[:, O_BANK:O_BANK + 2, :].rearrange("p a q -> p (a q)"),
                                   ACT.Copy).then_inc(o_saved, 1)


def attention_out(nc, M, A, wo, bo, dst, gain=None):
    units = [(c, g) for c in range(NCH) for g in range(NGRP)]

    def raw(u):
        c, g = units[u]
        return A.o[:, c // 2, g, (c % 2) * CH:(c % 2 + 1) * CH]

    with ExitStack() as tmp:
        rec = tmp.enter_context(sbuf(nc, "sum_recip", [P, 2, CH], F32))
        norm = tmp.enter_context(sbuf(nc, "o_normed", [P, 2, CH], F32))
        upd = tmp.enter_context(sbuf(nc, "o_update", [P, 2, CH], F32))
        with phase(nc, "sums_ready", "recip_ready", "norm_ready", "proj_step", "scaled", "added") as (
                block, sums_ready, recip_ready, norm_ready, proj_step, scaled, added):
            @block.tensor
            def _(pe):
                def project(u):
                    c, g = units[u]
                    pe.wait_ge(norm_ready, u + 1)
                    if g == 0 and c >= 2:
                        pe.wait_ge(scaled, c - 1)
                    pe.matmul(M.ps[:, 4 + c % 2, :], wo[:, g * P:(g + 1) * P], norm[:, u % 2, :],
                              start=g == 0, stop=g == NGRP - 1).then_inc(proj_step, 1)

                for u in range(len(units)):
                    if u >= 2:
                        pe.wait_ge(recip_ready, u - 1)
                    pe.matmul(M.ps[:, u % 2, :], A.pick[:], raw(u), start=True, stop=True).then_inc(sums_ready, 1)
                    if u:
                        project(u - 1)
                project(len(units) - 1)

            @block.vector
            def _(dve):
                def last(c):
                    dve.wait_ge(proj_step, NGRP * (c + 1))
                    if gain is None:
                        dve.scalar_tensor_tensor(chunk(dst, c), M.ps[:, 4 + c % 2, :], bo, chunk(dst, c),
                                                 ALU.add, ALU.add).then_inc(scaled, 1)
                    else:
                        if c >= 2:
                            dve.wait_ge(added, c - 1)
                        dve.tensor_scalar(upd[:, c % 2, :], M.ps[:, 4 + c % 2, :], bo, gain(c // 2),
                                          ALU.add, ALU.mult).then_inc(scaled, 1)
                        dve.wait_ge(scaled, c + 1)
                        dve.tensor_tensor(chunk(dst, c), chunk(dst, c), upd[:, c % 2, :], ALU.add).then_inc(added, 1)

                for u, (c, g) in enumerate(units):
                    dve.wait_ge(sums_ready, u + 1)
                    if u >= 2:
                        dve.wait_ge(norm_ready, u - 1)
                    dve.reciprocal(rec[:, u % 2, :], M.ps[:, u % 2, :]).then_inc(recip_ready, 1)
                    if u >= NGRP and g == 1:
                        last(c - 1)
                last(NCH - 1)

            @block.gpsimd
            def _(pool):
                for u in range(len(units)):
                    pool.wait_ge(recip_ready, u + 1)
                    if u >= 2:
                        pool.wait_ge(proj_step, u - 1)
                    pool.tensor_tensor(norm[:, u % 2, :], raw(u), rec[:, u % 2, :], ALU.mult).then_inc(norm_ready, 1)


def feed_forward(nc, M, W, dst):
    def col(name):
        a, b = L0_COLS[name]
        return W[:, a:b]

    with ExitStack() as tmp:
        hid = tmp.enter_context(sbuf(nc, "ffn_hidden", [P, 2, 4, CH], F32))
        with phase(nc, "up_ready", "hidden_ready", "down_ready", "added") as (
                block, up_ready, hidden_ready, down_ready, added):
            @block.tensor
            def _(pe):
                def down(c):
                    if c >= 2:
                        pe.wait_ge(added, c - 1)
                    for f in range(4):
                        pe.wait_ge(hidden_ready, 4 * c + f + 1)
                        mm = pe.matmul(M.ps[:, 4 + c % 2, :], col("w2")[:, f * P:(f + 1) * P], hid[:, c % 2, f, :],
                                       start=f == 0, stop=f == 3)
                    mm.then_inc(down_ready, 1)

                for c in range(NCH):
                    for f in range(4):
                        if c:
                            pe.wait_ge(hidden_ready, 4 * (c - 1) + f + 1)
                        pe.matmul(M.ps[:, f, :], col("w1")[:, f * P:(f + 1) * P], chunk(M.h, c),
                                  start=True, stop=True).then_inc(up_ready, 1)
                    if c:
                        down(c - 1)
                down(NCH - 1)

            @block.scalar
            def _(act):
                for c in range(NCH):
                    for f in range(4):
                        act.wait_ge(up_ready, 4 * c + f + 1)
                        if c >= 2:
                            act.wait_ge(down_ready, c - 1)
                        act.activation(hid[:, c % 2, f, :], M.ps[:, f, :], ACT.Gelu,
                                       bias=col("b1")[:, f:f + 1]).then_inc(hidden_ready, 1)

            @block.vector
            def _(dve):
                for c in range(NCH):
                    dve.wait_ge(down_ready, c + 1)
                    dve.scalar_tensor_tensor(chunk(dst, c), M.ps[:, 4 + c % 2, :], col("b2"), chunk(dst, c),
                                             ALU.add, ALU.add).then_inc(added, 1)


def add_scaled(nc, M, update, gain):
    with phase(nc, "added") as (block, added):
        @block.vector
        def _(dve):
            for b in range(B):
                t = slice(b * T, (b + 1) * T)
                dve.scalar_tensor_tensor(M.x[:, t], update[:, t], gain(b), M.x[:, t], ALU.mult, ALU.add)


def transformer(nc, M, D):
    with ExitStack() as ctx:
        z = ctx.enter_context(sbuf(nc, "z_T", [P, N], F32))
        W = ctx.enter_context(sbuf(nc, "l0_weights", [P, L0_WIDTH], F32))
        fin = ctx.enter_context(sbuf(nc, "l0_final", [P, 2], F32))
        A = Attention(nc, D, ctx)

        def col(name):
            a, b = L0_COLS[name]
            return W[:, a:b]

        layer_norm(nc, M, M.x, z, lambda b: M.mod[:, 0, 1, b:b + 1], lambda b: M.mod[:, 0, 0, b:b + 1],
                   (fin[:], D["l0_final"]))
        with nc.Fori(0, 4) as layer:
            with phase(nc, "weights_in") as (block, weights_in):
                @block.sync
                def _(sp):
                    sp.dma_start(W[:], D["l0_weights"][bass.ds(layer * P, P), :]).then_inc(weights_in, 16)
                    sp.wait_ge(weights_in, 16)
            layer_norm(nc, M, z, M.h, lambda b: col("ln1w"), lambda b: col("ln1b"))
            qkv(nc, M, A, W, L0_COLS, DH ** -0.5)
            attention_core(nc, M, A, [D["alibi"][g * 6:g * 6 + 6].rearrange("r (j t) -> r j t", j=GROUP)
                                      for g in range(NGRP)])
            attention_out(nc, M, A, col("wo"), col("bo"), z)
            layer_norm(nc, M, z, M.h, lambda b: col("ln2w"), lambda b: col("ln2b"))
            feed_forward(nc, M, W, z)
        layer_norm(nc, M, z, M.h, lambda b: fin[:, 0:1], lambda b: fin[:, 1:2])
        add_scaled(nc, M, M.h, lambda b: M.mod[:, 0, 2, b:b + 1])


def store(nc, M, out):
    with phase(nc, "stored") as (block, stored):
        @block.sync
        def _(sp):
            sp.dma_start(out, M.x[:]).then_inc(stored, 16)
            sp.wait_ge(stored, 16)


def wide(ap, n):
    return ap.unsqueeze(len(ap.shape)).to_broadcast([*ap.shape, n])


def steps(eng, sem):
    count = [0]

    def done(ins):
        ins.then_inc(sem, 1)
        count[0] += 1
        eng.wait_ge(sem, count[0])
    return done


class Gates:

    PARTS_AT = 32

    def __init__(self, nc, ctx, full=False):
        self.parts = ctx.enter_context(sbuf(nc, "gate_parts", [96, N], BF16))
        self.full = ctx.enter_context(sbuf(nc, "gate_full", [P if full else 16, N]))
        self.sel = ctx.enter_context(sbuf(nc, "spread_rows", [96, 16, P], BF16))


def route(nc, M, D, G, E, kind, loads, router, bias=None):
    with ExitStack() as tmp:
        def sb(name, shape, dt=F32):
            return tmp.enter_context(sbuf(nc, name, shape, dt))
        lg = sb("logits", [P, NBLK, E])
        pr = sb("scores", [P, NBLK, E])
        sel = sb("selected", [P, NBLK, E])
        one = [sb("first_hot", [P, NBLK, E]), sb("second_hot", [P, NBLK, E])]
        stat = sb("row_stat", [P, NBLK])
        ok = sb("row_ok", [P, NBLK])
        top = sb("top8", [P, NBLK, 8])
        idx = sb("top8_at", [P, NBLK, 8], U32)
        idxf = sb("top8_at_f", [P, NBLK, 8])
        iota = sb("expert_ids", [P, E])
        w = sb("gates", [P, NBLK, E])
        rest = sb("gate_rest", [16, N])
        mid = sb("gate_mid", [16, N], BF16)
        with phase(nc, "loaded", "made", "logits_ready", "shifted", "exped", "chain", "gates_ready",
                   "turned") as (block, loaded, made, logits_ready, shifted, exped, chain, gates_ready, turned):
            nloads = 16 * (len(loads) + 1)

            @block.sync
            def _(sp):
                sp.dma_start(G.sel[:], D["spread"].rearrange("r (e p) -> r e p", p=P)).then_inc(loaded, 16)
                for dst, src in loads:
                    sp.dma_start(dst, src).then_inc(loaded, 16)
                sp.wait_ge(loaded, nloads)

            @block.gpsimd
            def _(pool):
                pool.iota(iota[:], pattern=[[1, E]], base=0, channel_multiplier=0,
                          allow_small_or_imprecise_dtypes=True).then_inc(made, 1)
                pool.memset(G.parts[:], 0.0).then_inc(made, 1)
                pool.memset(G.full[:], 0.0).then_inc(made, 1)

            @block.tensor
            def _(pe):
                pe.wait_ge(loaded, nloads)
                for blk in range(NBLK):
                    mm = pe.matmul(M.ps[:, 0, blk * E:(blk + 1) * E], M.h[:, blk * P:(blk + 1) * P], router,
                                   start=True, stop=True)
                mm.then_inc(logits_ready, 1)
                pe.wait_ge(gates_ready, 1)
                for blk in range(NBLK):
                    mm = pe.transpose(M.ps[0:E, 4 + blk // 4, (blk % 4) * P:(blk % 4 + 1) * P], w[:, blk, :],
                                      M.ident[:])
                mm.then_inc(turned, 1)

            @block.scalar
            def _(act):
                logits = M.ps[:, 0, 0:NBLK * E].rearrange("p (n e) -> p n e", e=E)
                if kind == "sigmoid":
                    act.wait_ge(logits_ready, 1)
                    act.activation(pr[:], logits, ACT.Sigmoid).then_inc(exped, 1)
                else:
                    act.wait_ge(shifted, 1)
                    act.activation(pr[:], lg[:], ACT.Exp).then_inc(exped, 1)

            @block.vector
            def _(dve):
                done = steps(dve, chain)
                logits = M.ps[:, 0, 0:NBLK * E].rearrange("p (n e) -> p n e", e=E)
                dve.wait_ge(loaded, nloads)
                dve.wait_ge(logits_ready, 1)
                if kind == "sigmoid":
                    dve.wait_ge(exped, 1)
                    done(dve.tensor_tensor(sel[:], pr[:], bias.unsqueeze(1).to_broadcast([P, NBLK, E]), ALU.add))
                    choice = sel
                else:
                    if bias is not None:
                        done(dve.tensor_tensor(lg[:], logits, bias.unsqueeze(1).to_broadcast([P, NBLK, E]), ALU.add))
                    else:
                        done(dve.tensor_copy(lg[:], logits))
                    done(dve.tensor_reduce(stat[:], lg[:], AX_X, ALU.max))
                    dve.tensor_tensor(lg[:], lg[:], wide(stat[:], E), ALU.subtract).then_inc(shifted, 1)
                    dve.wait_ge(exped, 1)
                    done(dve.tensor_reduce(stat[:], pr[:], AX_X, ALU.add))
                    done(dve.reciprocal(stat[:], stat[:]))
                    done(dve.tensor_tensor(pr[:], pr[:], wide(stat[:], E), ALU.mult))
                    choice = pr
                for blk in range(NBLK):
                    ins = dve.max(top[:, blk, :], choice[:, blk, :])
                done(ins)
                for blk in range(NBLK):
                    ins = dve.max_index(idx[:, blk, :], top[:, blk, :], choice[:, blk, :])
                done(ins)
                done(dve.tensor_copy(idxf[:], idx[:]))
                dve.wait_ge(made, 3)
                for k in range(2):
                    done(dve.tensor_tensor(one[k][:], iota[:].unsqueeze(1).to_broadcast([P, NBLK, E]),
                                           wide(idxf[:, :, k], E), ALU.is_equal))
                if kind == "sigmoid":
                    done(dve.tensor_tensor(sel[:], one[0][:], one[1][:], ALU.add))
                    done(dve.tensor_tensor(w[:], sel[:], pr[:], ALU.mult))
                    done(dve.tensor_reduce(stat[:], w[:], AX_X, ALU.add))
                    done(dve.tensor_scalar(ok[:], stat[:], 1e-9, None, ALU.is_gt))
                    done(dve.tensor_scalar(stat[:], stat[:], 1e-9, None, ALU.add))
                    done(dve.reciprocal(stat[:], stat[:]))
                    done(dve.tensor_tensor(stat[:], stat[:], ok[:], ALU.mult))
                    done(dve.tensor_tensor(w[:], w[:], wide(stat[:], E), ALU.mult))
                    done(dve.tensor_scalar(ok[:], ok[:], -0.5, 0.5, ALU.mult, ALU.add))
                    done(dve.tensor_tensor(sel[:], sel[:], wide(ok[:], E), ALU.mult))
                    dve.tensor_tensor(w[:], w[:], sel[:], ALU.add).then_inc(gates_ready, 1)
                else:
                    by = [top[:, :, k] if kind == "softmax" else pr[:, :, k] for k in range(2)]
                    for k in range(2):
                        done(dve.tensor_tensor(one[k][:], one[k][:], wide(by[k], E), ALU.mult))
                    dve.tensor_tensor(w[:], one[0][:], one[1][:], ALU.add).then_inc(gates_ready, 1)
                dve.wait_ge(turned, 1)
                done(dve.tensor_copy(G.full[0:E, :], M.ps[0:E, 4:8, :].rearrange("e a t -> e (a t)")))
                done(dve.tensor_copy(G.parts[0:E, :], G.full[0:E, :]))
                done(dve.tensor_tensor(rest[0:E, :], G.full[0:E, :], G.parts[0:E, :], ALU.subtract))
                done(dve.tensor_copy(mid[0:E, :], rest[0:E, :]))
                done(dve.tensor_copy(G.parts[32:32 + E, :], mid[0:E, :]))
                done(dve.tensor_tensor(G.parts[64:64 + E, :], rest[0:E, :], mid[0:E, :], ALU.subtract))


def spread(pe, G, out, e, c):
    return pe.matmul(out, G.sel[:, e, :], chunk(G.parts, c), start=True, stop=True)


def moe_l0(nc, M, D):
    E = 16
    layer_norm(nc, M, M.x, M.h, lambda b: M.mod[:, 0, 4, b:b + 1], lambda b: M.mod[:, 0, 3, b:b + 1])
    with ExitStack() as ctx:
        def sb(name, shape, dt=F32):
            return ctx.enter_context(sbuf(nc, name, shape, dt))
        we = sb("experts", [P, E, P])
        small = sb("router_and_bias", [P, 2 * E])
        G = Gates(nc, ctx)
        route(nc, M, D, G, E, "softmax",
              [(we[:], D["l0_experts"].rearrange("p (e d) -> p e d", e=E)), (small[:], D["l0_small"])], small[:, 0:E])
        R = 3
        act_out = sb("expert_out", [P, R, CH])
        weighed = sb("expert_weighed", [P, R, CH])
        acc = sb("moe_sum", [P, N])
        units = [(e, c) for e in range(E) for c in range(NCH)]
        with phase(nc, "cleared", "proj_ready", "spread_ready", "relu_ready", "weighed_ready", "summed") as (
                block, cleared, proj_ready, spread_ready, relu_ready, weighed_ready, summed):
            @block.tensor
            def _(pe):
                for u, (e, c) in enumerate(units):
                    if u >= 4:
                        pe.wait_ge(relu_ready, u - 3)
                    pe.matmul(M.ps[:, u % 4, :], we[:, e, :], chunk(M.h, c), start=True,
                              stop=True).then_inc(proj_ready, 1)
                    if u >= 4:
                        pe.wait_ge(weighed_ready, u - 3)
                    spread(pe, G, M.ps[:, 4 + u % 4, :], e, c).then_inc(spread_ready, 1)

            @block.scalar
            def _(act):
                for u, (e, c) in enumerate(units):
                    act.wait_ge(proj_ready, u + 1)
                    if u >= R:
                        act.wait_ge(weighed_ready, u - R + 1)
                    act.activation(act_out[:, u % R, :], M.ps[:, u % 4, :], ACT.Relu,
                                   bias=small[:, E + e:E + e + 1]).then_inc(relu_ready, 1)

            @block.vector
            def _(dve):
                for u, (e, c) in enumerate(units):
                    dve.wait_ge(relu_ready, u + 1)
                    dve.wait_ge(spread_ready, u + 1)
                    if u >= R:
                        dve.wait_ge(summed, u - R + 1)
                    dve.tensor_tensor(weighed[:, u % R, :], act_out[:, u % R, :], M.ps[:, 4 + u % 4, :],
                                      ALU.mult).then_inc(weighed_ready, 1)

            @block.gpsimd
            def _(pool):
                pool.memset(acc[:], 0.0).then_inc(cleared, 1)
                pool.wait_ge(cleared, 1)
                for u, (e, c) in enumerate(units):
                    pool.wait_ge(weighed_ready, u + 1)
                    if e:
                        pool.wait_ge(summed, u - NCH + 1)
                    pool.tensor_tensor(chunk(acc, c), chunk(acc, c), weighed[:, u % R, :], ALU.add).then_inc(summed, 1)
        add_scaled(nc, M, acc, lambda b: M.mod[:, 0, 5, b:b + 1])


def moe_l1(nc, M, D):
    E, S = 8, 2
    layer_norm(nc, M, M.x, M.h, lambda b: M.mod[:, 1, 4, b:b + 1], lambda b: M.mod[:, 1, 3, b:b + 1])
    with ExitStack() as ctx:
        def sb(name, shape, dt=F32):
            return ctx.enter_context(sbuf(nc, name, shape, dt))
        up = sb("experts_up", [P, E, P])
        down = sb("experts_down", [P, E, P])
        shared = sb("shared", [P, 3, S, P])
        small = sb("router_and_bias", [P, 2 * E])
        G = Gates(nc, ctx)
        route(nc, M, D, G, E, "sigmoid",
              [(up[:], D["l1_up"].rearrange("p (e d) -> p e d", e=E)),
               (down[:], D["l1_down"].rearrange("p (e d) -> p e d", e=E)),
               (shared[:], D["l1_shared"].rearrange("p (k s d) -> p k s d", k=3, s=S)),
               (small[:], D["l1_small"])], small[:, 0:E], small[:, E:2 * E])
        R = 3
        gated = sb("shared_hidden", [P, NCH, S, CH])
        silu = sb("shared_silu", [P, 2, CH])
        hid = sb("expert_hidden", [P, R, CH])
        weighed = sb("expert_weighed", [P, R, CH])
        pairs = [(c, s) for c in range(NCH) for s in range(S)]
        units = [(c, e) for c in range(NCH) for e in range(E)]
        with phase(nc, "shared_ready", "silu_ready", "gated_ready", "up_ready", "spread_ready", "hidden_ready",
                   "weighed_ready", "down_ready", "added") as (
                block, shared_ready, silu_ready, gated_ready, up_ready, spread_ready, hidden_ready, weighed_ready,
                down_ready, added):
            @block.tensor
            def _(pe):
                for i, (c, s) in enumerate(pairs):
                    if i >= 2:
                        pe.wait_ge(gated_ready, i - 1)
                    pe.matmul(M.ps[:, 2 * (i % 2), :], shared[:, 0, s, :], chunk(M.h, c), start=True, stop=True)
                    pe.matmul(M.ps[:, 2 * (i % 2) + 1, :], shared[:, 1, s, :], chunk(M.h, c), start=True,
                              stop=True).then_inc(shared_ready, 1)
                pe.wait_ge(gated_ready, len(pairs))

                def finish(u):
                    c, e = units[u]
                    if e == 0:
                        if c >= 2:
                            pe.wait_ge(added, c - 1)
                        for s in range(S):
                            pe.matmul(M.ps[:, 6 + c % 2, :], shared[:, 2, s, :], gated[:, c, s, :],
                                      start=s == 0, stop=False)
                    pe.wait_ge(weighed_ready, u + 1)
                    pe.matmul(M.ps[:, 6 + c % 2, :], down[:, e, :], weighed[:, u % R, :], start=False,
                              stop=e == E - 1).then_inc(down_ready, 1)

                for u, (c, e) in enumerate(units):
                    if u >= 3:
                        pe.wait_ge(hidden_ready, u - 2)
                    pe.matmul(M.ps[:, u % 3, :], up[:, e, :], chunk(M.h, c), start=True, stop=True).then_inc(up_ready, 1)
                    if u >= 3:
                        pe.wait_ge(weighed_ready, u - 2)
                    spread(pe, G, M.ps[:, 3 + u % 3, :], e, c).then_inc(spread_ready, 1)
                    if u:
                        finish(u - 1)
                finish(len(units) - 1)

            @block.scalar
            def _(act):
                for i, (c, s) in enumerate(pairs):
                    act.wait_ge(shared_ready, i + 1)
                    if i >= 2:
                        act.wait_ge(gated_ready, i - 1)
                    act.activation(silu[:, i % 2, :], M.ps[:, 2 * (i % 2), :], ACT.Silu).then_inc(silu_ready, 1)
                for u in range(len(units)):
                    act.wait_ge(up_ready, u + 1)
                    if u >= R:
                        act.wait_ge(weighed_ready, u - R + 1)
                    act.activation(hid[:, u % R, :], M.ps[:, u % 3, :], ACT.Gelu).then_inc(hidden_ready, 1)

            @block.vector
            def _(dve):
                for i, (c, s) in enumerate(pairs):
                    dve.wait_ge(silu_ready, i + 1)
                    dve.tensor_tensor(gated[:, c, s, :], silu[:, i % 2, :], M.ps[:, 2 * (i % 2) + 1, :],
                                      ALU.mult).then_inc(gated_ready, 1)
                for u, (c, e) in enumerate(units):
                    dve.wait_ge(hidden_ready, u + 1)
                    dve.wait_ge(spread_ready, u + 1)
                    if u >= R:
                        dve.wait_ge(down_ready, u - R + 1)
                    dve.tensor_tensor(weighed[:, u % R, :], hid[:, u % R, :], M.ps[:, 3 + u % 3, :],
                                      ALU.mult).then_inc(weighed_ready, 1)
                    if e == E - 1:
                        dve.wait_ge(down_ready, u + 1)
                        dve.scalar_tensor_tensor(chunk(M.x, c), M.ps[:, 6 + c % 2, :],
                                                 M.mod[:, 1, 5, c // 2:c // 2 + 1], chunk(M.x, c),
                                                 ALU.mult, ALU.add).then_inc(added, 1)


def moe_l2(nc, M, D):
    E = 8
    layer_norm(nc, M, M.x, M.h, lambda b: M.mod[:, 2, 4, b:b + 1], lambda b: M.mod[:, 2, 3, b:b + 1])
    with ExitStack() as ctx:
        def sb(name, shape, dt=F32):
            return ctx.enter_context(sbuf(nc, name, shape, dt))
        w = sb("experts", [P, 3, E, P])
        bias = sb("expert_bias", [P, 2, E])
        b3 = sb("expert_bias3", [P, P])
        small = sb("router_and_bias", [P, 2 * E])
        G = Gates(nc, ctx, full=True)
        route(nc, M, D, G, E, "softmax01",
              [(w[:], D["l2_experts"].rearrange("p (k e d) -> p k e d", k=3, e=E)),
               (bias[:], D["l2_bias"].rearrange("p (k e) -> p k e", k=2)), (b3[:], D["l2_b3"]),
               (small[:], D["l2_small"])], small[:, 0:E], small[:, E:2 * E])
        R = 3
        h1 = sb("hidden_1", [P, R, CH])
        h2 = sb("hidden_2", [P, R, CH])
        weighed = sb("hidden_weighed", [P, R, CH])
        units = [(c, e) for c in range(NCH) for e in range(E)]
        U = len(units)
        with phase(nc, "up1", "relu1", "up2", "relu2", "spread_ready", "weighed_ready", "down_ready", "added") as (
                block, up1, relu1, up2, relu2, spread_ready, weighed_ready, down_ready, added):
            @block.tensor
            def _(pe):
                for t in range(U + 2):
                    if t < U:
                        c, e = units[t]
                        if t >= 2:
                            pe.wait_ge(relu1, t - 1)
                        pe.matmul(M.ps[:, t % 2, :], w[:, 0, e, :], chunk(M.h, c), start=True, stop=True).then_inc(up1, 1)
                    if 1 <= t <= U:
                        u = t - 1
                        c, e = units[u]
                        pe.wait_ge(relu1, u + 1)
                        if u >= 2:
                            pe.wait_ge(relu2, u - 1)
                        pe.matmul(M.ps[:, 2 + u % 2, :], w[:, 1, e, :], h1[:, u % R, :], start=True,
                                  stop=True).then_inc(up2, 1)
                        if u >= 2:
                            pe.wait_ge(weighed_ready, u - 1)
                        spread(pe, G, M.ps[:, 4 + u % 2, :], e, c).then_inc(spread_ready, 1)
                    if t >= 2:
                        u = t - 2
                        c, e = units[u]
                        if e == 0:
                            if c >= 2:
                                pe.wait_ge(added, c - 1)
                            pe.matmul(M.ps[:, 6 + c % 2, :], b3[:], chunk(G.full, c), start=True, stop=False)
                        pe.wait_ge(weighed_ready, u + 1)
                        pe.matmul(M.ps[:, 6 + c % 2, :], w[:, 2, e, :], weighed[:, u % R, :], start=False,
                                  stop=e == E - 1).then_inc(down_ready, 1)

            @block.scalar
            def _(act):
                for t in range(U + 1):
                    if t < U:
                        act.wait_ge(up1, t + 1)
                        if t >= R:
                            act.wait_ge(up2, t - R + 1)
                        act.activation(h1[:, t % R, :], M.ps[:, t % 2, :], ACT.Relu,
                                       bias=bias[:, 0, units[t][1]:units[t][1] + 1]).then_inc(relu1, 1)
                    if t:
                        u = t - 1
                        act.wait_ge(up2, u + 1)
                        if u >= R:
                            act.wait_ge(weighed_ready, u - R + 1)
                        act.activation(h2[:, u % R, :], M.ps[:, 2 + u % 2, :], ACT.Relu,
                                       bias=bias[:, 1, units[u][1]:units[u][1] + 1]).then_inc(relu2, 1)

            @block.vector
            def _(dve):
                for u, (c, e) in enumerate(units):
                    dve.wait_ge(relu2, u + 1)
                    dve.wait_ge(spread_ready, u + 1)
                    if u >= R:
                        dve.wait_ge(down_ready, u - R + 1)
                    dve.tensor_tensor(weighed[:, u % R, :], h2[:, u % R, :], M.ps[:, 4 + u % 2, :],
                                      ALU.mult).then_inc(weighed_ready, 1)
                    if e == E - 1:
                        dve.wait_ge(down_ready, u + 1)
                        dve.scalar_tensor_tensor(chunk(M.x, c), M.ps[:, 6 + c % 2, :],
                                                 M.mod[:, 2, 5, c // 2:c // 2 + 1], chunk(M.x, c),
                                                 ALU.mult, ALU.add).then_inc(added, 1)


L3_COLS = {}
_at = 0
for _name, _w in (("wq", P), ("wqr", P), ("wk", P), ("wkr", P), ("wv", P), ("bv", P), ("wo", NGRP * P),
                  ("bq", 1), ("bqr", 1), ("bk", 1), ("bkr", 1), ("bo", 1)):
    L3_COLS[_name] = (_at, _at + _w)
    _at += _w
L3_WIDTH = _at


def attn_l3(nc, M, D):
    layer_norm(nc, M, M.x, M.h, lambda b: M.mod[:, 3, 1, b:b + 1], lambda b: M.mod[:, 3, 0, b:b + 1])
    with ExitStack() as ctx:
        W = ctx.enter_context(sbuf(nc, "l3_weights", [P, L3_WIDTH]))
        A = Attention(nc, D, ctx)
        with ExitStack() as tmp:
            xpos = tmp.enter_context(sbuf(nc, "xpos", [P, 4, T]))
            with phase(nc, "weights_in") as (block, weights_in):
                @block.sync
                def _(sp):
                    sp.dma_start(W[:], D["l3_weights"]).then_inc(weights_in, 16)
                    sp.dma_start(xpos[:], D["xpos"].rearrange("p (k t) -> p k t", k=4)).then_inc(weights_in, 16)
                    sp.wait_ge(weights_in, 32)

            def tables(what, c):
                t = slice((c % 2) * CH, (c % 2 + 1) * CH)
                return xpos[:, 2 * what, t], xpos[:, 2 * what + 1, t]

            qkv(nc, M, A, W, L3_COLS, 1.0, tables)
        attention_core(nc, M, A, [D["no_bias"].rearrange("r (j t) -> r j t", j=GROUP)] * NGRP)
        a, b = L3_COLS["wo"]
        o = L3_COLS["bo"]
        attention_out(nc, M, A, W[:, a:b], W[:, o[0]:o[1]], M.x, lambda b: M.mod[:, 3, 2, b:b + 1])


L1_COLS = {}
_at = 0
for _name, _w in (("wq", P), ("wqr", P), ("wk", P), ("wkr", P), ("wv", P), ("bv", P), ("wo", P),
                  ("bq", 1), ("bqr", 1), ("bk", 1), ("bkr", 1), ("bo", 1),
                  ("freq", 1), ("bit0", 1), ("bit1", 1), ("bit2", 1), ("bit3", 1), ("turn", 1), ("sign", 1)):
    L1_COLS[_name] = (_at, _at + _w)
    _at += _w
L1_WIDTH = _at


def attn_l1(nc, M, D):
    H1, DH1 = 2, 64
    layer_norm(nc, M, M.x, M.h, lambda b: M.mod[:, 1, 1, b:b + 1], lambda b: M.mod[:, 1, 0, b:b + 1])
    PI = 3.1415925
    with ExitStack() as ctx:
        def sb(name, shape, dt=F32):
            return ctx.enter_context(sbuf(nc, name, shape, dt))
        W = sb("l1_weights", [P, L1_WIDTH])

        def col(name):
            a, b = L1_COLS[name]
            return W[:, a:b]

        cos = sb("cos", [P, T])
        sin = sb("sin", [P, T])
        kT = sb("k_T", [P, N])
        qz = [sb("q_T_head0", [P, N]), sb("q_T_head1", [P, N])]
        v = sb("v_and_ones", [P, NBLK, H1, P])
        onT = sb("o_normed_T", [P, N])
        ones = sb("ones", [96, P], BF16)
        mrow = sb("neg_max_rows", [96, B * H1, T], BF16)
        with ExitStack() as tmp:
            def tb(name, shape, dt=F32):
                return tmp.enter_context(sbuf(nc, name, shape, dt))
            f = tb("freq", [P, 16])
            pos = tb("positions", [P, T])
            ang = tb("angle", [P, T])
            half = tb("half_angle", [P, T])
            with phase(nc, "weights_in", "positions_made", "cleared", "base_ready", "log_ready", "root_ready",
                       "chain", "angles_ready", "half_ready", "sines_ready") as (
                    block, weights_in, positions_made, cleared, base_ready, log_ready, root_ready, chain,
                    angles_ready, half_ready, sines_ready):
                @block.sync
                def _(sp):
                    sp.dma_start(W[:], D["l1_weights"]).then_inc(weights_in, 16)
                    sp.wait_ge(weights_in, 16)

                @block.gpsimd
                def _(pool):
                    pool.iota(pos[:], pattern=[[1, T]], base=0, channel_multiplier=0,
                              allow_small_or_imprecise_dtypes=True).then_inc(positions_made, 1)
                    pool.wait_ge(positions_made, 1)
                    done = steps(pool, cleared)
                    done(pool.memset(qz[0][DH1:P, :], 0.0))
                    done(pool.memset(qz[1][0:DH1, :], 0.0))
                    done(pool.memset(v[:, :, :, DH1:P], 1.0))
                    done(pool.memset(ones[:], 1.0))
                    done(pool.memset(mrow[:], 0.0))

                @block.scalar
                def _(act):
                    act.wait_ge(weights_in, 16)
                    act.activation(f[:, 0:1], col("freq"), ACT.Sigmoid).then_inc(base_ready, 1)
                    act.wait_ge(base_ready, 2)
                    act.activation(f[:, 2:3], f[:, 1:2], ACT.Ln).then_inc(log_ready, 1)
                    act.wait_ge(log_ready, 1)
                    act.activation(f[:, 3:4], f[:, 2:3], ACT.Exp, scale=-1.0 / 16).then_inc(root_ready, 1)
                    act.wait_ge(angles_ready, 1)
                    act.activation(sin[:], ang[:], ACT.Sin).then_inc(sines_ready, 1)
                    act.wait_ge(half_ready, 1)
                    act.activation(cos[:], half[:], ACT.Sin).then_inc(sines_ready, 1)

                @block.vector
                def _(dve):
                    done = steps(dve, chain)

                    def c(k):
                        return f[:, k:k + 1]

                    dve.wait_ge(base_ready, 1)
                    dve.tensor_scalar(c(1), c(0), (10000.0 - 0.83 * 10000.0) * 2.0, 0.83 * 10000.0,
                                      ALU.mult, ALU.add).then_inc(base_ready, 1)
                    dve.wait_ge(root_ready, 1)
                    for a, b in ((3, 4), (4, 5), (5, 6), (6, 7)):
                        done(dve.tensor_tensor(c(b), c(a), c(a), ALU.mult))
                    done(dve.tensor_tensor(c(7), c(7), c(1), ALU.mult))
                    done(dve.tensor_scalar(c(7), c(7), -1.0 / 16, 17.0 / 16, ALU.mult, ALU.add))
                    done(dve.tensor_tensor(c(3), c(3), c(7), ALU.mult))
                    done(dve.tensor_copy(c(8), col("turn")))
                    for k in range(4):
                        done(dve.tensor_scalar(c(9), c(3), -1.0, None, ALU.add))
                        done(dve.tensor_scalar(c(9), c(9), col(f"bit{k}"), 1.0, ALU.mult, ALU.add))
                        done(dve.tensor_tensor(c(8), c(8), c(9), ALU.mult))
                        done(dve.tensor_tensor(c(3), c(3), c(3), ALU.mult))
                    dve.wait_ge(positions_made, 1)
                    done(dve.tensor_scalar(pos[:], pos[:], c(8), None, ALU.mult))
                    dve.tensor_scalar(ang[:], pos[:], -3.14159265, PI, ALU.add, ALU.min).then_inc(angles_ready, 1)
                    dve.tensor_scalar(half[:], pos[:], 0.5, PI, ALU.mult, ALU.min).then_inc(half_ready, 1)
                    dve.wait_ge(sines_ready, 1)
                    dve.tensor_scalar(sin[:], sin[:], col("sign"), None, ALU.mult)
                    dve.wait_ge(sines_ready, 2)
                    done(dve.tensor_tensor(cos[:], cos[:], cos[:], ALU.mult))
                    dve.tensor_scalar(cos[:], cos[:], -2.0, 1.0, ALU.mult, ALU.add)

        units = [(what, c) for c in range(NCH) for what in range(2)]
        with ExitStack() as tmp:
            plain = tmp.enter_context(sbuf(nc, "plain", [P, 2, CH]))
            turned = tmp.enter_context(sbuf(nc, "turned", [P, 2, CH]))
            with phase(nc, "proj_ready", "part_a", "part_b", "v_ready") as (block, proj_ready, part_a, part_b,
                                                                             v_ready):
                @block.tensor
                def _(pe):
                    for u, (what, c) in enumerate(units):
                        if u >= 2:
                            pe.wait_ge(part_b, u - 1)
                        for k, name in enumerate(("wq", "wqr") if what == 0 else ("wk", "wkr")):
                            mm = pe.matmul(M.ps[:, 2 * (u % 2) + k, :], col(name), chunk(M.h, c), start=True, stop=True)
                        mm.then_inc(proj_ready, 1)
                    for blk in range(NBLK):
                        mm = pe.matmul(M.ps[:, 4 + blk // 4, (blk % 4) * P:(blk % 4 + 1) * P],
                                       M.h[:, blk * P:(blk + 1) * P], col("wv"), start=True, stop=True)
                        if blk % 4 == 3:
                            mm.then_inc(v_ready, 1)

                @block.vector
                def _(dve):
                    for u, (what, c) in enumerate(units):
                        t = slice((c % 2) * CH, (c % 2 + 1) * CH)
                        dve.wait_ge(proj_ready, u + 1)
                        dve.scalar_tensor_tensor(plain[:, u % 2, :], M.ps[:, 2 * (u % 2), :],
                                                 col("bq" if what == 0 else "bk"), cos[:, t],
                                                 ALU.add, ALU.mult).then_inc(part_a, 1)
                        dve.scalar_tensor_tensor(turned[:, u % 2, :], M.ps[:, 2 * (u % 2) + 1, :],
                                                 col("bqr" if what == 0 else "bkr"), sin[:, t],
                                                 ALU.add, ALU.mult).then_inc(part_b, 1)
                        dve.wait_ge(part_a, u + 1)
                        dve.wait_ge(part_b, u + 1)
                        for dst, rows in (((qz[0], slice(0, DH1)), (qz[1], slice(DH1, P))) if what == 0
                                          else ((kT, slice(0, P)),)):
                            dve.tensor_tensor(dst[rows, c * CH:(c + 1) * CH], plain[rows, u % 2, :],
                                              turned[rows, u % 2, :], ALU.add)
                    bv = col("bv").rearrange("p (h d) -> p h d", h=H1)
                    for blk in range(NBLK):
                        dve.wait_ge(v_ready, blk // 4 + 1)
                        src = M.ps[:, 4 + blk // 4, (blk % 4) * P:(blk % 4 + 1) * P]
                        dve.tensor_tensor(v[:, blk, :, 0:DH1], src.rearrange("p (h d) -> p h d", h=H1), bv, ALU.add)

        pairs = [(b, h) for b in range(B) for h in range(H1)]
        with ExitStack() as tmp:
            mparts = tmp.enter_context(sbuf(nc, "max_parts", [P, len(pairs) * QB, 2]))
            rowmax = tmp.enter_context(sbuf(nc, "row_max", [P, len(pairs) * QB]))
            mfull = tmp.enter_context(sbuf(nc, "neg_max", [len(pairs) * QB, P]))
            mrest = tmp.enter_context(sbuf(nc, "neg_max_rest", [len(pairs) * QB, P]))
            m3 = tmp.enter_context(sbuf(nc, "neg_max_parts", [len(pairs) * QB, 3, P], BF16))
            pieces = [(n, i, half) for n in range(len(pairs)) for i in range(QB) for half in range(2)]
            with phase(nc, "s1_ready", "piece_max", "max_joined", "max_turned", "chain", "max_rows_in") as (
                    block, s1_ready, piece_max, max_joined, max_turned, chain, max_rows_in):
                @block.tensor
                def _(pe):
                    for u, (n, i, half) in enumerate(pieces):
                        b, h = pairs[n]
                        if u >= 4:
                            pe.wait_ge(piece_max, u - 3)
                        q0 = b * T + i * P
                        k0 = b * T + half * CH
                        pe.matmul(M.ps[:, u % 4, :], qz[h][:, q0:q0 + P], kT[:, k0:k0 + CH], start=True,
                                  stop=True).then_inc(s1_ready, 1)
                    pe.wait_ge(max_joined, 1)
                    pe.transpose(M.ps[0:len(pairs) * QB, 4, 0:P], rowmax[:], M.ident[:]).then_inc(max_turned, 1)

                @block.vector
                def _(dve):
                    done = steps(dve, chain)
                    for u, (n, i, half) in enumerate(pieces):
                        dve.wait_ge(s1_ready, u + 1)
                        dve.reduce_max(mparts[:, n * QB + i, half:half + 1], M.ps[:, u % 4, :],
                                       AX_X).then_inc(piece_max, 1)
                    dve.wait_ge(piece_max, len(pieces))
                    dve.tensor_reduce(rowmax[:], mparts[:], AX_X, ALU.max).then_inc(max_joined, 1)
                    dve.wait_ge(max_turned, 1)
                    done(dve.tensor_scalar(mfull[:], M.ps[0:len(pairs) * QB, 4, 0:P], -1.0, None, ALU.mult))
                    done(dve.tensor_copy(m3[:, 0, :], mfull[:]))
                    done(dve.tensor_tensor(mrest[:], mfull[:], m3[:, 0, :], ALU.subtract))
                    done(dve.tensor_copy(m3[:, 1, :], mrest[:]))
                    done(dve.tensor_tensor(m3[:, 2, :], mrest[:], m3[:, 1, :], ALU.subtract))

                @block.sync
                def _(sp):
                    sp.wait_ge(chain, 5)
                    for part in range(3):
                        sp.dma_start(mrow[part:part + 1, :, :].rearrange("o n (i q) -> o (n i) q", i=QB),
                                     m3[:, part, :]).then_inc(max_rows_in, 16)
                    sp.wait_ge(max_rows_in, 48)

        sets = [(n, half) for n in range(len(pairs)) for half in range(2)]
        units = [(s, kb) for s in range(len(sets)) for kb in range(QB)]
        with ExitStack() as tmp:
            prob = tmp.enter_context(sbuf(nc, "prob", [P, 3, CH]))
            rec = tmp.enter_context(sbuf(nc, "sum_recip", [DH1, 2, CH]))
            with phase(nc, "s2_ready", "exp_done", "pv_done", "recip_ready", "normed") as (
                    block, s2_ready, exp_done, pv_done, recip_ready, normed):
                @block.tensor
                def _(pe):
                    def weigh(u):
                        s, kb = units[u]
                        b, h = pairs[sets[s][0]]
                        pe.wait_ge(exp_done, u + 1)
                        if kb == 0 and s >= 2:
                            pe.wait_ge(normed, s - 1)
                        pe.matmul(M.ps[:, 4 + s % 2, :], v[:, b * QB + kb, h, :], prob[:, u % 3, :],
                                  start=kb == 0, stop=kb == QB - 1).then_inc(pv_done, 1)

                    for u, (s, kb) in enumerate(units):
                        n, half = sets[s]
                        b, h = pairs[n]
                        if u >= 4:
                            pe.wait_ge(exp_done, u - 3)
                        k0, q0 = b * T + kb * P, b * T + half * CH
                        pe.matmul(M.ps[:, u % 4, :], kT[:, k0:k0 + P], qz[h][:, q0:q0 + CH], start=True, stop=False)
                        pe.matmul(M.ps[:, u % 4, :], ones[:], mrow[:, n, half * CH:(half + 1) * CH], start=False,
                                  stop=True).then_inc(s2_ready, 1)
                        if u:
                            weigh(u - 1)
                    weigh(len(units) - 1)

                @block.scalar
                def _(act):
                    for u in range(len(units)):
                        act.wait_ge(s2_ready, u + 1)
                        if u >= 3:
                            act.wait_ge(pv_done, u - 2)
                        act.activation(prob[:, u % 3, :], M.ps[:, u % 4, :], ACT.Exp,
                                       scale=DH1 ** -0.5).then_inc(exp_done, 1)

                @block.vector
                def _(dve):
                    for s, (n, half) in enumerate(sets):
                        b, h = pairs[n]
                        q0 = b * T + half * CH
                        dve.wait_ge(pv_done, QB * (s + 1))
                        dve.reciprocal(rec[:, s % 2, :], M.ps[DH1:P, 4 + s % 2, :]).then_inc(recip_ready, 1)
                        dve.wait_ge(recip_ready, s + 1)
                        dve.tensor_tensor(onT[h * DH1:(h + 1) * DH1, q0:q0 + CH], M.ps[0:DH1, 4 + s % 2, :],
                                          rec[:, s % 2, :], ALU.mult).then_inc(normed, 1)

            upd = tmp.enter_context(sbuf(nc, "o_update", [P, NCH, CH]))
            with phase(nc, "out_ready", "scaled") as (block, out_ready, scaled):
                @block.tensor
                def _(pe):
                    for c in range(NCH):
                        pe.matmul(M.ps[:, c, :], col("wo"), chunk(onT, c), start=True, stop=True).then_inc(out_ready, 1)

                @block.vector
                def _(dve):
                    for c in range(NCH):
                        dve.wait_ge(out_ready, c + 1)
                        dve.tensor_scalar(upd[:, c, :], M.ps[:, c, :], col("bo"), M.mod[:, 1, 2, c // 2:c // 2 + 1],
                                          ALU.add, ALU.mult).then_inc(scaled, 1)

                @block.gpsimd
                def _(pool):
                    for c in range(NCH):
                        pool.wait_ge(scaled, c + 1)
                        pool.tensor_tensor(chunk(M.x, c), chunk(M.x, c), upd[:, c, :], ALU.add)


L2_COLS = {}
_at = 0
DI, NS, TAPS, RANK = 2, 16, 4, 8
for _name, _w in (("in", 2 * DI * P), ("xproj", DI * 96), ("dtproj", DI * P), ("out", DI * P),
                  ("conv_w", DI * TAPS), ("conv_b", DI), ("dt_b", DI), ("a_log", DI * NS), ("d", DI)):
    L2_COLS[_name] = (_at, _at + _w)
    _at += _w
L2_WIDTH = _at


def mamba(nc, M, D):
    layer_norm(nc, M, M.x, M.h, lambda b: M.mod[:, 2, 1, b:b + 1], lambda b: M.mod[:, 2, 0, b:b + 1])
    seqs = [(d, b) for d in range(DI) for b in range(B)]
    PAD = TAPS - 1
    with ExitStack() as ctx:
        def sb(name, shape, dt=F32):
            return ctx.enter_context(sbuf(nc, name, shape, dt))
        W = sb("l2_weights", [P, L2_WIDTH])

        def col(name, k=0, w=None):
            a, b = L2_COLS[name]
            return W[:, a:b] if w is None else W[:, a + k * w:a + (k + 1) * w]

        u = sb("u", [P, DI, N])
        gate = sb("silu_z", [P, DI, N])
        delta = sb("delta", [P, DI, N])
        du = sb("delta_u", [P, DI, N])
        negA = sb("neg_a", [P, DI * NS])
        bparts = sb("b_parts", [96, N], BF16)
        cparts = sb("c_parts", [96, N], BF16)
        sel = sb("spread_rows", [96, 16, P], BF16)
        with ExitStack() as tmp:
            def tb(name, shape, dt=F32):
                return tmp.enter_context(sbuf(nc, name, shape, dt))
            xin = tb("x_in", [P, DI, B, T + PAD])
            conv = tb("conv", [P, DI, N])
            with phase(nc, "weights_in", "padded", "in_ready", "copied", "gated", "a_ready", "tap", "silu_done") as (
                    block, weights_in, padded, in_ready, copied, gated, a_ready, tap, silu_done):
                units = [(k, c) for c in range(NCH) for k in range(2 * DI)]

                @block.sync
                def _(sp):
                    sp.dma_start(W[:], D["l2_weights"]).then_inc(weights_in, 16)
                    sp.dma_start(sel[:], D["spread"].rearrange("r (e p) -> r e p", p=P)).then_inc(weights_in, 16)
                    sp.wait_ge(weights_in, 32)

                @block.gpsimd
                def _(pool):
                    pool.memset(xin[:, :, :, 0:PAD], 0.0).then_inc(padded, 1)
                    pool.memset(bparts[:], 0.0)
                    pool.memset(cparts[:], 0.0)

                @block.tensor
                def _(pe):
                    pe.wait_ge(weights_in, 32)
                    for i, (k, c) in enumerate(units):
                        if i >= 8:
                            pe.wait_ge(copied if k < DI else gated, DI * (c - 2) + k % DI + 1)
                        pe.matmul(M.ps[:, i % 8, :], col("in", k, P), chunk(M.h, c), start=True,
                                  stop=True).then_inc(in_ready, 1)

                @block.scalar
                def _(act):
                    act.wait_ge(weights_in, 32)
                    for i, (k, c) in enumerate(units):
                        if k >= DI:
                            act.wait_ge(in_ready, i + 1)
                            act.activation(chunk(gate[:, k - DI, :], c), M.ps[:, i % 8, :], ACT.Silu).then_inc(gated, 1)
                    for s, (d, b) in enumerate(seqs):
                        act.wait_ge(tap, TAPS * (s + 1))
                        act.activation(u[:, d, b * T:(b + 1) * T], conv[:, d, b * T:(b + 1) * T], ACT.Silu,
                                       bias=col("conv_b", d, 1)).then_inc(silu_done, 1)
                    act.activation(negA[:], col("a_log"), ACT.Exp).then_inc(a_ready, 1)

                @block.vector
                def _(dve):
                    for i, (k, c) in enumerate(units):
                        if k < DI:
                            at = PAD + (c % 2) * CH
                            dve.wait_ge(in_ready, i + 1)
                            dve.tensor_copy(xin[:, k, c // 2, at:at + CH], M.ps[:, i % 8, :]).then_inc(copied, 1)
                    dve.wait_ge(copied, DI * NCH)
                    dve.wait_ge(padded, 1)
                    for s, (d, b) in enumerate(seqs):
                        out = conv[:, d, b * T:(b + 1) * T]
                        for k in range(TAPS):
                            wk = W[:, L2_COLS["conv_w"][0] + d * TAPS + k:L2_COLS["conv_w"][0] + d * TAPS + k + 1]
                            if k == 0:
                                dve.tensor_scalar(out, xin[:, d, b, 0:T], wk, None, ALU.mult).then_inc(tap, 1)
                            else:
                                dve.wait_ge(tap, TAPS * s + k)
                                dve.scalar_tensor_tensor(out, xin[:, d, b, k:k + T], wk, out, ALU.mult,
                                                         ALU.add).then_inc(tap, 1)
                    dve.wait_ge(a_ready, 1)
                    dve.tensor_scalar(negA[:], negA[:], -1.0, None, ALU.mult)

        with ExitStack() as tmp:
            def tb(name, shape, dt=F32):
                return tmp.enter_context(sbuf(nc, name, shape, dt))
            dbl = tb("x_dbl", [96, N])
            rest = tb("bc_rest", [NS, 2, CH])
            mid = tb("bc_mid", [NS, 2, CH], BF16)
            pre = tb("step_pre", [P, DI, N])
            ex = tb("step_exp", [P, DI, N])
            one = tb("step_one_plus", [P, DI, N])
            ln = tb("step_log", [P, DI, N])
            with phase(nc, "dbl_ready", "dbl_copied", "step_ready", "chain", "biased", "abs_done", "exp_done", "plus",
                       "log_done", "delta_ready") as (
                    block, dbl_ready, dbl_copied, step_ready, chain, biased, abs_done, exp_done, plus, log_done,
                    delta_ready):
                @block.tensor
                def _(pe):
                    for c in range(NCH):
                        for d in range(DI):
                            mm = pe.matmul(M.ps[0:96, c, :], col("xproj", d, 96), chunk(u[:, d, :], c), start=d == 0,
                                           stop=d == DI - 1)
                        mm.then_inc(dbl_ready, 1)
                    for c in range(NCH):
                        pe.wait_ge(dbl_copied, c + 1)
                        for d in range(DI):
                            i = c * DI + d
                            if i >= 4:
                                pe.wait_ge(biased, i - 3)
                            pe.matmul(M.ps[:, 4 + i % 4, :], W[0:96, L2_COLS["dtproj"][0] + d * P:
                                                               L2_COLS["dtproj"][0] + (d + 1) * P],
                                      chunk(dbl, c), start=True, stop=True).then_inc(step_ready, 1)

                @block.scalar
                def _(act):
                    for c in range(NCH):
                        act.wait_ge(dbl_ready, c + 1)
                        act.activation(chunk(dbl, c), M.ps[0:96, c, :], ACT.Copy).then_inc(dbl_copied, 1)
                    for i in range(NCH * DI):
                        c, d = divmod(i, DI)
                        act.wait_ge(step_ready, i + 1)
                        act.activation(chunk(pre[:, d, :], c), M.ps[:, 4 + i % 4, :], ACT.Identity,
                                       bias=col("dt_b", d, 1)).then_inc(biased, 1)
                    act.wait_ge(biased, NCH * DI)
                    for d in range(DI):
                        act.activation(ex[:, d, :], pre[:, d, :], ACT.Abs).then_inc(abs_done, 1)
                    for d in range(DI):
                        act.wait_ge(abs_done, d + 1)
                        act.activation(ex[:, d, :], ex[:, d, :], ACT.Exp, scale=-1.0).then_inc(exp_done, 1)
                    for d in range(DI):
                        act.wait_ge(plus, d + 1)
                        act.activation(ln[:, d, :], one[:, d, :], ACT.Ln).then_inc(log_done, 1)

                @block.gpsimd
                def _(pool):
                    for d in range(DI):
                        pool.wait_ge(exp_done, d + 1)
                        pool.tensor_scalar(one[:, d, :], ex[:, d, :], 1.0, None, ALU.add).then_inc(plus, 1)
                    for d in range(DI):
                        pool.wait_ge(delta_ready, d + 1)
                        pool.tensor_tensor(du[:, d, :], delta[:, d, :], u[:, d, :], ALU.mult)

                @block.vector
                def _(dve):
                    done = steps(dve, chain)
                    for c in range(NCH):
                        dve.wait_ge(dbl_copied, c + 1)
                        for k, (parts, row) in enumerate(((bparts, 32), (cparts, 64))):
                            src = dbl[row:row + NS, c * CH:(c + 1) * CH]
                            done(dve.tensor_copy(chunk(parts, c)[0:NS], src))
                            done(dve.tensor_copy(rest[:, k, :], src))
                            done(dve.tensor_tensor(rest[:, k, :], rest[:, k, :], chunk(parts, c)[0:NS], ALU.subtract))
                            done(dve.tensor_copy(mid[:, k, :], rest[:, k, :]))
                            done(dve.tensor_copy(chunk(parts, c)[32:32 + NS], mid[:, k, :]))
                            done(dve.tensor_tensor(chunk(parts, c)[64:64 + NS], rest[:, k, :], mid[:, k, :],
                                                   ALU.subtract))
                    for d in range(DI):
                        dve.wait_ge(log_done, d + 1)
                        t, e, l = one[:, d, :], ex[:, d, :], ln[:, d, :]
                        flag = delta[:, d, :]
                        done(dve.tensor_scalar(flag, t, 1.0, None, ALU.is_equal))
                        done(dve.scalar_tensor_tensor(t, t, -1.0, flag, ALU.add, ALU.add))
                        done(dve.reciprocal(t, t))
                        done(dve.tensor_tensor(t, t, l, ALU.mult))
                        done(dve.tensor_tensor(t, t, flag, ALU.add))
                        done(dve.tensor_tensor(t, t, e, ALU.mult))
                        dve.scalar_tensor_tensor(delta[:, d, :], pre[:, d, :], 0.0, t, ALU.max,
                                                 ALU.add).then_inc(delta_ready, 1)

        y = sb("y", [P, DI, N])
        with ExitStack() as tmp:
            def tb(name, shape, dt=F32):
                return tmp.enter_context(sbuf(nc, name, shape, dt))
            dA = tb("decay", [P, 2, T])
            dBu = tb("inflow", [P, 2, T])
            st = tb("states", [P, 2, T])
            hc = tb("read_out", [P, 2, T])
            bsb = tb("b_spread", [P, 2, T])
            groups = [(b, n) for b in range(B) for n in range(NS)]
            with phase(nc, "b_ready", "b_copied", "c_ready", "decay_ready", "inflow_ready", "scanned", "read",
                       "summed", "y_saved") as (
                    block, b_ready, b_copied, c_ready, decay_ready, inflow_ready, scanned, read, summed, y_saved):
                @block.tensor
                def _(pe):
                    def gather(i):
                        b, n = groups[i // DI]
                        d = i % DI
                        pe.wait_ge(read, i + 1)
                        if n == 0 and b:
                            pe.wait_ge(y_saved, DI * (b - 1) + d + 1)
                        for half in range(2):
                            mm = pe.matmul(M.ps[:, 4 + 2 * d + half, :], M.ident[:],
                                           hc[:, i % 2, half * CH:(half + 1) * CH], start=n == 0, stop=n == NS - 1)
                        mm.then_inc(summed, 1)

                    for g, (b, n) in enumerate(groups):
                        if g:
                            pe.wait_ge(b_copied, g)
                        for half in range(2):
                            mm = pe.matmul(M.ps[:, half, :], sel[:, n, :], chunk(bparts, 2 * b + half),
                                           start=True, stop=True)
                        mm.then_inc(b_ready, 1)
                        if g:
                            pe.wait_ge(read, DI * g)
                        for half in range(2):
                            mm = pe.matmul(M.ps[:, 2 + half, :], sel[:, n, :], chunk(cparts, 2 * b + half),
                                           start=True, stop=True)
                        mm.then_inc(c_ready, 1)
                        if g:
                            for d in range(DI):
                                gather(DI * (g - 1) + d)
                    for d in range(DI):
                        gather(DI * (len(groups) - 1) + d)

                @block.scalar
                def _(act):
                    for g, (b, n) in enumerate(groups):
                        act.wait_ge(b_ready, g + 1)
                        if g >= 2:
                            act.wait_ge(inflow_ready, DI * (g - 1))
                        act.activation(bsb[:, g % 2, :], M.ps[:, 0:2, :].rearrange("p a t -> p (a t)"),
                                       ACT.Copy).then_inc(b_copied, 1)
                        for d in range(DI):
                            i = DI * g + d
                            if i >= 2:
                                act.wait_ge(scanned, i - 1)
                            act.activation(dA[:, i % 2, :], delta[:, d, b * T:(b + 1) * T], ACT.Exp,
                                           scale=negA[:, d * NS + n:d * NS + n + 1]).then_inc(decay_ready, 1)

                @block.gpsimd
                def _(pool):
                    for g, (b, n) in enumerate(groups):
                        pool.wait_ge(b_copied, g + 1)
                        for d in range(DI):
                            i = DI * g + d
                            if i >= 2:
                                pool.wait_ge(scanned, i - 1)
                            pool.tensor_tensor(dBu[:, i % 2, :], du[:, d, b * T:(b + 1) * T], bsb[:, g % 2, :],
                                               ALU.mult).then_inc(inflow_ready, 1)

                @block.vector
                def _(dve):
                    for g, (b, n) in enumerate(groups):
                        for d in range(DI):
                            i = DI * g + d
                            dve.wait_ge(decay_ready, i + 1)
                            dve.wait_ge(inflow_ready, i + 1)
                            if i >= 2:
                                dve.wait_ge(read, i - 1)
                            dve.tensor_tensor_scan(st[:, i % 2, :], dA[:, i % 2, :], dBu[:, i % 2, :], 0.0, ALU.mult,
                                                   ALU.add).then_inc(scanned, 1)
                            dve.wait_ge(scanned, i + 1)
                            dve.wait_ge(c_ready, g + 1)
                            if i >= 2:
                                dve.wait_ge(summed, i - 1)
                            dve.tensor_tensor(hc[:, i % 2, :], st[:, i % 2, :],
                                              M.ps[:, 2:4, :].rearrange("p a t -> p (a t)"),
                                              ALU.mult).then_inc(read, 1)
                        if n == NS - 1:
                            for d in range(DI):
                                dve.wait_ge(summed, DI * g + d + 1)
                                t = slice(b * T, (b + 1) * T)
                                dve.scalar_tensor_tensor(
                                    y[:, d, t], u[:, d, t], col("d", d, 1),
                                    M.ps[:, 4 + 2 * d:6 + 2 * d, :].rearrange("p a t -> p (a t)"),
                                    ALU.mult, ALU.add).then_inc(y_saved, 1)

        with phase(nc, "gated", "out_ready", "added") as (block, gated, out_ready, added):
            @block.gpsimd
            def _(pool):
                for c in range(NCH):
                    for d in range(DI):
                        pool.tensor_tensor(chunk(y[:, d, :], c), chunk(y[:, d, :], c), chunk(gate[:, d, :], c),
                                           ALU.mult).then_inc(gated, 1)

            @block.tensor
            def _(pe):
                for c in range(NCH):
                    for d in range(DI):
                        pe.wait_ge(gated, DI * c + d + 1)
                        mm = pe.matmul(M.ps[:, c, :], col("out", d, P), chunk(y[:, d, :], c), start=d == 0,
                                       stop=d == DI - 1)
                    mm.then_inc(out_ready, 1)

            @block.vector
            def _(dve):
                for c in range(NCH):
                    dve.wait_ge(out_ready, c + 1)
                    dve.scalar_tensor_tensor(chunk(M.x, c), M.ps[:, c, :], M.mod[:, 2, 2, c // 2:c // 2 + 1],
                                             chunk(M.x, c), ALU.mult, ALU.add)


class ExpertsL3:
    E, F = 16, 2

    def __init__(self, nc, ctx, D):
        self.up = ctx.enter_context(sbuf(nc, "l3_gate_and_value", [P, 2, self.E, self.F, P]))
        self.down = ctx.enter_context(sbuf(nc, "l3_down", [P, self.E, self.F, P]))
        self.loads = [(self.up[:].rearrange("p k e f d -> p (k e f d)"), D["l3_up"]),
                      (self.down[:].rearrange("p e f d -> p (e f d)"), D["l3_down"])]


def moe_l3(nc, M, D, X=None):
    E, F, CAP = 16, 2, 32
    ROWS = 64
    SEL = E * CAP
    EG = P // CAP
    layer_norm(nc, M, M.x, M.h, lambda b: M.mod[:, 3, 4, b:b + 1], lambda b: M.mod[:, 3, 3, b:b + 1])
    with ExitStack() as ctx:
        def sb(name, shape, dt=F32):
            return ctx.enter_context(sbuf(nc, name, shape, dt))
        loads = []
        if X is None:
            X = ExpertsL3(nc, ctx, D)
            loads = X.loads
        idxb = sb("chosen_at", [P, B, SEL])
        wb = sb("chosen_weight", [P, B, SEL])
        icol = sb("chosen_at_col", [P, B * E // EG])
        xtok = sb("h_by_token", [P, NBLK, P])
        tokid = sb("token_ids", [P, QB])
        pos = sb("positions", [P, T])
        ysel = sb("chosen_out", [P, B, SEL])
        with ExitStack() as tmp:
            def tb(name, shape, dt=F32):
                return tmp.enter_context(sbuf(nc, name, shape, dt))
            router = tb("router", [P, P + 32])
            r1 = tb("router_hidden", [P, N])
            pr = tb("probs", [ROWS, T])
            work = tb("probs_left", [ROWS, T])
            stat = tb("row_stat", [ROWS, 4])
            top = tb("top32", [ROWS, CAP])
            idx = tb("top32_at", [ROWS, CAP], U32)
            idxf = tb("top32_at_f", [ROWS, CAP])
            diag = tb("diagonal", [ROWS, 2, B, SEL])
            ones = tb("ones", [ROWS, P])
            with phase(nc, "loaded", "made", "r1_ready", "r1_done", "logits_ready", "max_ready", "exped", "chain",
                       "diag_ready", "spread_ready", "spread_done", "cols_ready", "turned", "turned_copied") as (
                    block, loaded, made, r1_ready, r1_done, logits_ready, max_ready, exped, chain, diag_ready,
                    spread_ready, spread_done, cols_ready, turned, turned_copied):
                @block.sync
                def _(sp):
                    sp.dma_start(router[:], D["l3_router"]).then_inc(loaded, 16)
                    for dst, src in loads:
                        sp.dma_start(dst, src).then_inc(loaded, 16)
                    sp.wait_ge(loaded, 16 * (1 + len(loads)))

                @block.gpsimd
                def _(pool):
                    pool.iota(tokid[:], pattern=[[P, QB]], base=0, channel_multiplier=1,
                              allow_small_or_imprecise_dtypes=True)
                    pool.iota(pos[:], pattern=[[1, T]], base=0, channel_multiplier=0,
                              allow_small_or_imprecise_dtypes=True)
                    pool.memset(ones[:], 1.0).then_inc(made, 1)

                @block.tensor
                def _(pe):
                    pe.wait_ge(loaded, 16 * (1 + len(loads)))
                    for c in range(NCH):
                        pe.matmul(M.ps[:, c, :], router[:, 0:P], chunk(M.h, c), start=True, stop=True).then_inc(r1_ready, 1)
                    for c in range(NCH):
                        b = c // 2
                        pe.wait_ge(r1_done, c + 1)
                        mm = pe.matmul(M.ps[32 * b:32 * b + 32, 4 + c % 2, :], router[:, P:P + 32], chunk(r1, c),
                                       start=True, stop=True)
                    mm.then_inc(logits_ready, 1)
                    for blk in range(NBLK):
                        mm = pe.transpose(M.ps[:, blk // 4, (blk % 4) * P:(blk % 4 + 1) * P],
                                          M.h[:, blk * P:(blk + 1) * P], M.ident[:])
                        if blk % 4 == 3:
                            mm.then_inc(turned, 1)
                    pe.wait_ge(made, 1)
                    for k in range(2):
                        pe.wait_ge(diag_ready, k + 1)
                        for b in range(B):
                            mm = pe.matmul(M.ps[:, 6 + b, :] if k == 0 else M.ps[:, 4 + b, :], ones[:],
                                           diag[:, k, b, :], start=True, stop=True)
                        mm.then_inc(spread_ready, 1)
                    pe.wait_ge(spread_done, 1)
                    pe.wait_ge(turned_copied, NBLK // 4)
                    for k in range(B * E // EG):
                        b, g = divmod(k, E // EG)
                        mm = pe.matmul(M.ps[:, 0, k:k + 1], idxb[:, b, g * P:(g + 1) * P], M.ident[:, 0:1],
                                       start=True, stop=True)
                    mm.then_inc(cols_ready, 1)

                @block.scalar
                def _(act):
                    for c in range(NCH):
                        act.wait_ge(r1_ready, c + 1)
                        act.activation(chunk(r1, c), M.ps[:, c, :], ACT.Silu).then_inc(r1_done, 1)
                    for k in range(NBLK // 4):
                        act.wait_ge(turned, k + 1)
                        act.activation(xtok[:, 4 * k:4 * k + 4, :].rearrange("p n d -> p (n d)"), M.ps[:, k, :],
                                       ACT.Copy).then_inc(turned_copied, 1)
                    act.wait_ge(max_ready, 1)
                    act.activation(pr[:], M.ps[0:ROWS, 4:6, :].rearrange("p a t -> p (a t)"), ACT.Exp,
                                   bias=stat[:, 0:1]).then_inc(exped, 1)

                @block.vector
                def _(dve):
                    done = steps(dve, chain)
                    logits = M.ps[0:ROWS, 4:6, :].rearrange("p a t -> p (a t)")
                    dve.wait_ge(logits_ready, 1)
                    done(dve.reduce_max(stat[:, 1:2], logits, AX_X))
                    dve.tensor_scalar(stat[:, 0:1], stat[:, 1:2], -1.0, None, ALU.mult).then_inc(max_ready, 1)
                    dve.wait_ge(exped, 1)
                    done(dve.reduce_sum(stat[:, 2:3], pr[:], AX_X))
                    done(dve.reciprocal(stat[:, 2:3], stat[:, 2:3]))
                    done(dve.tensor_scalar(pr[:], pr[:], stat[:, 2:3], None, ALU.mult))
                    left = pr
                    for r in range(CAP // 8):
                        part = slice(8 * r, 8 * r + 8)
                        done(dve.max(top[:, part], left[:]))
                        done(dve.max_index(idx[:, part], top[:, part], left[:]))
                        if r < CAP // 8 - 1:
                            done(dve.match_replace(work[:], top[:, part], left[:], -1.0))
                            left = work
                    done(dve.tensor_copy(idxf[:], idx[:]))
                    done(dve.reduce_sum(stat[:, 3:4], top[:], AX_X))
                    done(dve.tensor_scalar(stat[:, 3:4], stat[:, 3:4], 1e-9, None, ALU.add))
                    done(dve.reciprocal(stat[:, 3:4], stat[:, 3:4]))
                    done(dve.tensor_scalar(top[:], top[:], stat[:, 3:4], None, ALU.mult))
                    for k, vals in enumerate((idxf, top)):
                        for b in range(B):
                            ins = dve.tensor_tensor(
                                diag[:, k, b, :].rearrange("p (e s) -> p e s", s=CAP),
                                vals[:].unsqueeze(1).to_broadcast([ROWS, E, CAP]),
                                wide(M.ident[0:ROWS, 32 * b:32 * b + E], CAP), ALU.mult)
                        ins.then_inc(diag_ready, 1)
                    for k, dst in enumerate((idxb, wb)):
                        dve.wait_ge(spread_ready, k + 1)
                        src = M.ps[:, 6:8, :] if k == 0 else M.ps[:, 4:6, :]
                        dve.tensor_copy(dst[:], src).then_inc(spread_done, 1)
                    dve.wait_ge(cols_ready, 1)
                    dve.tensor_copy(icol[:], M.ps[:, 0, 0:B * E // EG])

        with ExitStack() as tmp:
            def tb(name, shape, dt=F32):
                return tmp.enter_context(sbuf(nc, name, shape, dt))
            hot = tb("one_hot", [P, 4, SEL])
            xsel = tb("chosen_in", [P, B, E, CAP])
            silu = tb("silu_gate", [P, 2, CH])
            hid = tb("hidden", [P, 2, CH])
            NT = B * CAP
            GE = CH // (F * NT)
            with phase(nc, "hot_ready", "gathered", "xsel_ready", "gate_ready", "value_ready", "silu_ready",
                       "hidden_ready", "down_ready", "weighed") as (
                    block, hot_ready, gathered, xsel_ready, gate_ready, value_ready, silu_ready, hidden_ready,
                    down_ready, weighed):
                @block.tensor
                def _(pe):
                    for k in range(NBLK):
                        b, blk = divmod(k, QB)
                        pe.wait_ge(hot_ready, k + 1)
                        pe.matmul(M.ps[:, b, :], xtok[:, k, :], hot[:, k % 4, :], start=blk == 0,
                                  stop=blk == QB - 1).then_inc(gathered, 1)
                    pe.wait_ge(xsel_ready, B)

                    def down(g):
                        pe.wait_ge(hidden_ready, g + 1)
                        if g >= 2:
                            pe.wait_ge(weighed, B * (g - 1))
                        for k in range(GE):
                            for f in range(F):
                                at = (k * F + f) * NT
                                mm = pe.matmul(M.ps[:, 6 + g % 2, k * NT:(k + 1) * NT], X.down[:, g * GE + k, f, :],
                                               hid[:, g % 2, at:at + NT], start=f == 0, stop=f == F - 1)
                        mm.then_inc(down_ready, 1)

                    for g in range(E // GE):
                        for which, ready in ((0, gate_ready), (1, value_ready)):
                            if g >= 2:
                                pe.wait_ge(silu_ready if which == 0 else hidden_ready, g - 1)
                            for k in range(GE):
                                for f in range(F):
                                    at = (k * F + f) * NT
                                    mm = pe.matmul(M.ps[:, 2 + 2 * which + g % 2, at:at + NT],
                                                   X.up[:, which, g * GE + k, f, :], xsel[:, :, g * GE + k, :],
                                                   start=True, stop=True)
                            mm.then_inc(ready, 1)
                        if g:
                            down(g - 1)
                    down(E // GE - 1)

                @block.scalar
                def _(act):
                    for b in range(B):
                        act.wait_ge(gathered, QB * (b + 1))
                        act.activation(xsel[:, b].rearrange("p e s -> p (e s)"), M.ps[:, b, :],
                                       ACT.Copy).then_inc(xsel_ready, 1)
                    for g in range(E // GE):
                        act.wait_ge(gate_ready, g + 1)
                        if g >= 2:
                            act.wait_ge(hidden_ready, g - 1)
                        act.activation(silu[:, g % 2, :], M.ps[:, 2 + g % 2, :], ACT.Silu).then_inc(silu_ready, 1)

                @block.vector
                def _(dve):
                    for k in range(NBLK):
                        b, blk = divmod(k, QB)
                        if k >= 4:
                            dve.wait_ge(gathered, k - 3)
                        dve.tensor_scalar(hot[:, k % 4, :], idxb[:, b, :], tokid[:, blk:blk + 1], None,
                                          ALU.is_equal).then_inc(hot_ready, 1)
                    for g in range(E // GE):
                        dve.wait_ge(silu_ready, g + 1)
                        dve.wait_ge(value_ready, g + 1)
                        if g >= 2:
                            dve.wait_ge(down_ready, g - 1)
                        dve.tensor_tensor(hid[:, g % 2, :], silu[:, g % 2, :], M.ps[:, 4 + g % 2, :],
                                          ALU.mult).then_inc(hidden_ready, 1)
                        dve.wait_ge(down_ready, g + 1)
                        for b in range(B):
                            es = slice(g * GE * CAP, (g + 1) * GE * CAP)
                            src = M.ps[:, 6 + g % 2, 0:GE * NT].rearrange("p (e b s) -> p b e s", b=B, s=CAP)[:, b]
                            dve.tensor_tensor(ysel[:, b, es].rearrange("p (e s) -> p e s", s=CAP), src,
                                              wb[:, b, es].rearrange("p (e s) -> p e s", s=CAP),
                                              ALU.mult).then_inc(weighed, 1)

        with ExitStack() as tmp:
            def tb(name, shape, dt=F32):
                return tmp.enter_context(sbuf(nc, name, shape, dt))
            K = E // EG
            hot = tb("one_hot_rows", [P, B * K, T])
            yT = tb("chosen_out_rows", [P, B * K, P])
            with phase(nc, "hot_ready", "turned", "turned_copied", "scattered", "added") as (
                    block, hot_ready, turned, turned_copied, scattered, added):
                @block.tensor
                def _(pe):
                    for k in range(B * K):
                        b, g = divmod(k, K)
                        pe.transpose(M.ps[:, b, g * P:(g + 1) * P], ysel[:, b, g * P:(g + 1) * P],
                                     M.ident[:]).then_inc(turned, 1)
                    for c in range(NCH):
                        b, half = divmod(c, 2)
                        pe.wait_ge(turned_copied, b + 1)
                        for g in range(K):
                            pe.wait_ge(hot_ready, b * K + g + 1)
                            mm = pe.matmul(M.ps[:, 4 + c, :], yT[:, b * K + g, :],
                                           hot[:, b * K + g, half * CH:(half + 1) * CH], start=g == 0, stop=g == K - 1)
                        mm.then_inc(scattered, 1)

                @block.scalar
                def _(act):
                    for b in range(B):
                        act.wait_ge(turned, K * (b + 1))
                        act.activation(yT[:, b * K:(b + 1) * K, :].rearrange("p k d -> p (k d)"), M.ps[:, b, :],
                                       ACT.Copy).then_inc(turned_copied, 1)

                @block.vector
                def _(dve):
                    for k in range(B * K):
                        dve.tensor_scalar(hot[:, k, :], pos[:], icol[:, k:k + 1], None,
                                          ALU.is_equal).then_inc(hot_ready, 1)
                    for c in range(NCH):
                        dve.wait_ge(scattered, c + 1)
                        dve.scalar_tensor_tensor(chunk(M.x, c), M.ps[:, 4 + c, :], M.mod[:, 3, 5, c // 2:c // 2 + 1],
                                                 chunk(M.x, c), ALU.mult, ALU.add)



def program(nc, D, out, start=0, stop=8):
    stages = [transformer, moe_l0, attn_l1, moe_l1, mamba, moe_l2, attn_l3, moe_l3]
    _used.clear()
    with ExitStack() as ctx:
        M = Memory()
        for name in ("q_parts", "k_parts"):
            D = {**D, name: nc.dram_tensor(name, (3, P, N), BF16, kind="Internal").ap()}
        setup(nc, M, D, ctx)
        for stage in stages[start:stop]:
            stage(nc, M, D)
        store(nc, M, out)


def constants():
    import math
    bf = np.dtype("bfloat16")
    pos = np.arange(T)
    k_aux = np.zeros((9, T), np.float32)
    k_aux[0:3] = (pos // P) * P
    k_aux[3:6] = pos % P
    k_aux[6:9] = 1.0
    base = 2.0 ** (-2.0 ** (-(math.log2(HEADS) - 3)))
    slopes = (base ** np.arange(1, HEADS + 1)).astype(np.float32)
    hi = slopes.astype(bf)
    r = slopes - hi.astype(np.float32)
    mid = r.astype(bf)
    lo = (r - mid.astype(np.float32)).astype(bf)
    alibi = np.zeros((NGRP, 6, GROUP, T), np.float32)
    for i, part in enumerate((hi, mid, lo)):
        v = part.astype(np.float32).reshape(NGRP, GROUP)[:, :, None]
        alibi[:, i] = v
        alibi[:, 3 + i] = v
    pick = np.zeros((P, P), np.float32)
    for j in range(GROUP):
        pick[32 * j + DH, 32 * j:32 * j + 32] = 1.0
    spread_rows = np.zeros((96, 16, P), np.float32)
    for e in range(16):
        spread_rows[[e, 32 + e, 64 + e], e] = 1.0
    t = np.arange(T, dtype=np.float32)
    even = np.arange(0, DH, 2, dtype=np.float32)
    inv = (np.float32(1.0) / np.float32(10000.0) ** (even / np.float32(DH))).astype(np.float32)
    ang = np.repeat(t[:, None] * inv[None, :], 2, axis=-1).astype(np.float32)
    sbase = ((even + np.float32(0.4 * DH)) / np.float32(1.4 * DH)).astype(np.float32)
    power = ((t - T // 2) / np.float32(512.0)).astype(np.float32)
    sc = sbase[None, :].astype(np.float64) ** power[:, None].astype(np.float64)
    sc = np.concatenate((sc, sc), axis=-1)
    sign = np.tile([-1.0, 1.0], DH // 2)
    cos, sin = np.cos(ang.astype(np.float64)), np.sin(ang.astype(np.float64)) * sign
    qs = 1.0 / math.sqrt(DH * HEADS)
    tab = np.stack([cos * sc * qs, sin * sc * qs, cos / sc, sin / sc], 0)
    xpos = np.tile(tab.transpose(2, 0, 1), (HEADS, 1, 1)).astype(np.float32)
    return {"spread": spread_rows.reshape(96, -1).astype(bf), "xpos": xpos.reshape(P, -1),
            "no_bias": np.zeros((6, GROUP * T), bf), "k_aux": k_aux.astype(bf), "alibi": alibi.reshape(NGRP * 6, GROUP * T).astype(bf),
            "pick_sums": pick}


def wo_groups(w):
    wt = np.asarray(w)
    out = np.zeros((P, NGRP, P), np.float32)
    for h in range(HEADS):
        g, j = divmod(h, GROUP)
        out[32 * j:32 * j + DH, g] = wt[DH * h:DH * h + DH]
    return out.reshape(P, NGRP * P)


def layout(i):
    i = {k: np.asarray(v) for k, v in i.items()}
    a = constants()
    a["x_T"] = np.ascontiguousarray(i["L0_attn_x"].reshape(N, P).T)
    a["c_T"] = np.stack([i[f"L{l}_c"].T for l in range(4)], 1).reshape(P, 4 * B)
    a["wmod"] = np.concatenate([i[f"L{l}_wmod"] for l in range(4)], 1)
    layers = []
    for l in range(4):
        w, b = i["L0_attn_in_proj_w"][l], i["L0_attn_in_proj_b"][l]
        v = lambda n: i["L0_attn_" + n][l][:, None]
        layers.append(np.concatenate([
            w[0:P].T, w[P:2 * P].T, w[2 * P:].T, np.broadcast_to(b[2 * P:], (P, P)),
            wo_groups(i["L0_attn_out_proj_w"][l].T), i["L0_attn_ffn1_w"][l].T,
            i["L0_attn_ffn2_w"][l].T.reshape(4, P, P).transpose(1, 0, 2).reshape(P, 4 * P),
            b[0:P, None], b[P:2 * P, None], v("out_proj_b"), i["L0_attn_ffn1_b"][l].reshape(4, P).T,
            v("ffn2_b"), v("ln1_w"), v("ln1_b"), v("ln2_w"), v("ln2_b")], 1))
    a["l0_weights"] = np.concatenate(layers, 0)
    a["l0_final"] = np.stack([i["L0_attn_final_w"], i["L0_attn_final_b"]], 1)
    a["l0_experts"] = i["L0_ffn_expert_w"].transpose(2, 0, 1).reshape(P, -1)
    a["l0_small"] = np.concatenate([i["L0_ffn_gate_w"].T, i["L0_ffn_expert_b"].T], 1)
    a["l1_up"] = i["L1_ffn_ew1"].transpose(1, 0, 2).reshape(P, -1)
    a["l1_down"] = i["L1_ffn_ew2"].transpose(1, 0, 2).reshape(P, -1)
    a["l1_shared"] = np.concatenate([i["L1_ffn_sw1"], i["L1_ffn_sw3"],
                                     i["L1_ffn_sw2"].reshape(2, P, P).transpose(1, 0, 2).reshape(P, -1)], 1)
    a["l1_small"] = np.concatenate([i["L1_ffn_router_w"].T, np.broadcast_to(i["L1_ffn_router_bias"], (P, 8))], 1)
    a["l2_experts"] = np.concatenate([i[f"L2_ffn_w{k}"].transpose(1, 0, 2).reshape(P, -1) for k in (1, 2, 3)], 1)
    a["l2_bias"] = np.concatenate([i["L2_ffn_b1"].T, i["L2_ffn_b2"].T], 1)
    b3 = np.zeros((P, P), np.float32)
    b3[0:8] = i["L2_ffn_b3"]
    a["l2_b3"] = b3
    a["l2_small"] = np.concatenate([i["L2_ffn_gate_w"].T, np.broadcast_to(i["L2_ffn_gate_b"], (P, 8))], 1)
    swap = np.arange(P) ^ 1
    col = lambda n: i["L3_attn_" + n][:, None]
    wq, wk, wv = (i["L3_attn_" + n].T for n in ("Wq", "Wv", "Wk"))
    a["l3_weights"] = np.concatenate([
        wq, wq[:, swap], wk, wk[:, swap], wv, np.broadcast_to(i["L3_attn_bk"], (P, P)),
        wo_groups(i["L3_attn_Wo"].T), col("bq"), col("bq")[swap], col("bv"), col("bv")[swap], col("bo")], 1)
    dim = np.arange(P) % 64
    spatial = dim >= 32
    swap1 = np.where(spatial, np.arange(P) ^ 16, np.arange(P))
    j = np.where(spatial, (dim - 32) % 16, 0)
    bits = [((j >> k) & 1).astype(np.float32)[:, None] for k in range(4)]
    turn = np.where(spatial, 2 * np.pi / (T - 1), 0.0).astype(np.float32)[:, None]
    sign = np.where(spatial, np.where(dim < 48, 1.0, -1.0), 0.0).astype(np.float32)[:, None]
    g = {n: i["L1_attn_" + n] for n in ("Wq", "Wk", "Wv", "Wo", "bq", "bk", "bv", "bo")}
    a["l1_weights"] = np.concatenate([
        g["Wq"], g["Wq"][:, swap1], g["Wk"], g["Wk"][:, swap1], g["Wv"], np.broadcast_to(g["bv"], (P, P)), g["Wo"],
        g["bq"][:, None], g["bq"][swap1, None], g["bk"][:, None], g["bk"][swap1, None], g["bo"][:, None],
        np.broadcast_to(i["L1_attn_nrope_freq"], (P, 1)), *bits, turn, sign], 1)
    m = {n: i["L2_attn_h_" + n] for n in ("in_proj_w", "conv_w", "conv_b", "x_proj_w", "dt_proj_w", "dt_proj_b",
                                          "A_log", "D_param", "out_proj_w")}
    tiles = lambda v: v.reshape(DI, P, -1).transpose(1, 0, 2).reshape(P, -1)
    xproj = np.zeros((DI * P, 96), np.float32)
    xproj[:, 0:RANK] = m["x_proj_w"][0:RANK].T
    xproj[:, 32:32 + NS] = m["x_proj_w"][RANK:RANK + NS].T
    xproj[:, 64:64 + NS] = m["x_proj_w"][RANK + NS:].T
    dtproj = np.zeros((P, DI * P), np.float32)
    dtproj[0:RANK] = m["dt_proj_w"].T
    a["l2_weights"] = np.concatenate([
        m["in_proj_w"].T, tiles(xproj), dtproj, tiles(m["out_proj_w"].T), tiles(m["conv_w"]), tiles(m["conv_b"]),
        tiles(m["dt_proj_b"]), tiles(m["A_log"]), tiles(m["D_param"])], 1)
    rw2 = np.zeros((P, 32), np.float32)
    rw2[:, 0:16] = i["L3_ffn_router_w2"]
    a["l3_router"] = np.concatenate([i["L3_ffn_router_w1"], rw2], 1)
    byp = lambda w: w.reshape(16, P, -1).transpose(1, 0, 2).reshape(P, -1)
    a["l3_up"] = np.concatenate([byp(i["L3_ffn_w1"]), byp(i["L3_ffn_w2"])], 1)
    a["l3_down"] = i["L3_ffn_w3"].reshape(16, 2, P, P).transpose(2, 0, 1, 3).reshape(P, -1)
    return {k: np.ascontiguousarray(v) for k, v in a.items()}


def kernel(**inputs):
    import concourse.bacc as bacc
    from concourse.bass_utils import run_bass_kernel_spmd

    nc = bacc.Bacc("TRN2", target_bir_lowering=False, num_devices=1)
    arrays = layout(inputs)
    drams = {k: nc.dram_tensor(k, v.shape, mybir.dt.from_np(v.dtype), kind="ExternalInput").ap()
             for k, v in arrays.items()}
    out = nc.dram_tensor("out", (P, N), F32, kind="ExternalOutput").ap()
    program(nc, drams, out)
    r = run_bass_kernel_spmd(nc, [arrays], core_ids=[0])
    return np.ascontiguousarray(r.results[0]["out"].T).reshape(B, T, P)
```

```python
from contextlib import ExitStack, contextmanager

import numpy as np
import concourse.bass as bass
from concourse import mybir

F32 = mybir.dt.float32
BF16 = mybir.dt.bfloat16
U32 = mybir.dt.uint32
ALU = mybir.AluOpType
ACT = mybir.ActivationFunctionType
AX_X = mybir.AxisListType.X

P = 128
B, T = 2, 1024
N = B * T
CH = 512
NCH = N // CH
NBLK = N // P
HEADS, DH = 16, 8
NEG = -1.0e30
LN_EPS = 1e-5

PAIR_ROWS = 9 * DH
BIAS_ROWS = 6
MAX_ROWS = 3
S1_ROWS = PAIR_ROWS + BIAS_ROWS
S2_ROWS = S1_ROWS + MAX_ROWS
GROUP = 4
NGRP = HEADS // GROUP
QB = T // P
STACKS = 3
TURN_LAG = 2
FIRST_AHEAD = 20
STEP_EARLY, STEP_LATE = 3, 2
STACK_DMAS = 13

L0_COLS = {}
_at = 0
for _name, _w in (("wq", P), ("wk", P), ("wv", P), ("bv", P), ("wo", NGRP * P), ("w1", 4 * P), ("w2", 4 * P),
                  ("bq", 1), ("bk", 1), ("bo", 1), ("b1", 4), ("b2", 1),
                  ("ln1w", 1), ("ln1b", 1), ("ln2w", 1), ("ln2b", 1)):
    L0_COLS[_name] = (_at, _at + _w)
    _at += _w
L0_WIDTH = _at


_used = {}


def sbuf(nc, name, shape, dt=F32):
    n = _used[name] = _used.get(name, 0) + 1
    return nc.sbuf_tensor(f"sb_{name}_{n}", shape, dt)


@contextmanager
def phase(nc, *names):
    with ExitStack() as ctx:
        sems = [ctx.enter_context(nc.semaphore(n)) for n in names]
        with nc.Block(no_gpsimd_drain=True) as block:
            yield (block, *sems)
        numbers = sorted(s.num for s in sems)
        cuts = [i for i in range(1, len(numbers)) if numbers[i] != numbers[i - 1] + 1]
        for a, b in zip([0, *cuts], [*cuts, len(numbers)]):
            nc.all_engine_barrier(sems_to_clear=range(numbers[a], numbers[b - 1] + 1))


def chunk(t, c):
    return t[:, c * CH:(c + 1) * CH]


def wide(ap, n):
    return ap.unsqueeze(len(ap.shape)).to_broadcast([*ap.shape, n])


class Memory:
    pass


def setup(nc, M, D, ctx):
    def sb(name, shape, dt=F32):
        return ctx.enter_context(sbuf(nc, name, shape, dt))

    M.x = sb("x_T", [P, N])
    M.h = sb("h_T", [P, N])
    M.mean = sb("mean_weights", [P, P])
    M.ident = sb("ident", [P, P])
    M.ones = sb("ones_weights", [P, P])
    M.identb = sb("ident_bf16", [P, P], BF16)
    M.mask_qk = sb("mask_qk", [P, P], BF16)
    M.mask_kq = sb("mask_kq", [P, P], BF16)
    M.eps = sb("eps", [P, 1])
    M.mod = sb("mod", [P, 4, 6, B])
    M.ps = ctx.enter_context(nc.psum_tensor("ps", [P, 8, CH], F32))
    with ExitStack() as tmp:
        wmod = tmp.enter_context(sbuf(nc, "wmod", [P, 4, 6 * P], F32))
        cT = tmp.enter_context(sbuf(nc, "c_T", [P, 4, B], F32))
        cs = tmp.enter_context(sbuf(nc, "silu_c", [P, 4, B], F32))
        sg = tmp.enter_context(sbuf(nc, "gate_sign", [P, 4, B], F32))
        ab = tmp.enter_context(sbuf(nc, "gate_abs", [P, 4, B], F32))
        with phase(nc, "loaded", "zeroed", "consts", "silu_ready", "mod_ps", "mod_sb", "gates") as (
                block, loaded, zeroed, consts, silu_ready, mod_ps, mod_sb, gates):
            @block.sync
            def _(sp):
                sp.dma_start(cT[:], D["c_T"].rearrange("p (l b) -> p l b", b=B)).then_inc(loaded, 16)
                sp.dma_start(wmod[:], D["wmod"].rearrange("p (l n) -> p l n", l=4)).then_inc(loaded, 16)
                sp.dma_start(M.x[:], D["x_T"]).then_inc(loaded, 16)
                sp.wait_ge(loaded, 48)

            @block.gpsimd
            def _(pool):
                pool.memset(M.mean[:], 1.0 / P).then_inc(consts, 1)
                pool.memset(M.eps[:], LN_EPS).then_inc(consts, 1)
                pool.memset(M.ones[:], 1.0).then_inc(consts, 1)
                for t in (M.ident, M.identb, M.mask_qk, M.mask_kq):
                    pool.memset(t[:], 0.0).then_inc(zeroed, 1)
                pool.wait_ge(zeroed, 4)
                for t in (M.ident, M.identb):
                    pool.affine_select(out=t[:], in_=t[:], compare_op=ALU.not_equal, fill=1.0, base=0,
                                       pattern=[[-1, P]], channel_multiplier=1).then_inc(consts, 1)
                pool.affine_select(out=M.mask_qk[:], in_=M.mask_qk[:], compare_op=ALU.is_ge, fill=NEG, base=0,
                                   pattern=[[-1, P]], channel_multiplier=1).then_inc(consts, 1)
                pool.affine_select(out=M.mask_kq[:], in_=M.mask_kq[:], compare_op=ALU.is_ge, fill=NEG, base=0,
                                   pattern=[[1, P]], channel_multiplier=-1).then_inc(consts, 1)
                pool.wait_ge(consts, 7)

            @block.scalar
            def _(act):
                act.wait_ge(loaded, 48)
                act.activation(cs[:], cT[:], ACT.Silu).then_inc(silu_ready, 1)

            @block.tensor
            def _(pe):
                pe.wait_ge(loaded, 48)
                pe.wait_ge(silu_ready, 1)
                for layer in range(4):
                    for part in range(6):
                        at = (layer * 6 + part) * B
                        mm = pe.matmul(M.ps[:, 0, at:at + B], wmod[:, layer, part * P:(part + 1) * P],
                                       cs[:, layer, :], start=True, stop=True)
                mm.then_inc(mod_ps, 1)

            @block.vector
            def _(dve):
                dve.wait_ge(mod_ps, 1)
                dve.tensor_copy(M.mod[:].rearrange("p l s b -> p (l s b)"), M.ps[:, 0, 0:48]).then_inc(mod_sb, 1)
                dve.wait_ge(mod_sb, 1)
                done = 0
                for part in (2, 5):
                    g = M.mod[:, :, part, :]
                    dve.tensor_scalar(sg[:], g, 0.0, 2.0, ALU.is_ge, ALU.mult).then_inc(gates, 1)
                    dve.wait_ge(gates, done + 1)
                    dve.tensor_scalar(sg[:], sg[:], -1.0, None, ALU.add).then_inc(gates, 1)
                    dve.wait_ge(gates, done + 2)
                    dve.tensor_tensor(ab[:], sg[:], g, ALU.mult).then_inc(gates, 1)
                    dve.wait_ge(gates, done + 3)
                    dve.scalar_tensor_tensor(g, ab[:], 0.25, sg[:], ALU.max, ALU.mult).then_inc(gates, 1)
                    dve.wait_ge(gates, done + 4)
                    done += 4
                for part in (1, 4):
                    g = M.mod[:, :, part, :]
                    dve.tensor_scalar(g, g, 1.0, None, ALU.add).then_inc(gates, 1)


def layer_norm(nc, M, src, dst, scale, shift, loads=()):
    PER = CH // P
    with ExitStack() as tmp:
        cen = tmp.enter_context(sbuf(nc, "ln_centred", [P, N]))
        sqr = tmp.enter_context(sbuf(nc, "ln_squares", [P, N]))
        std = tmp.enter_context(sbuf(nc, "ln_std", [P, NBLK]))
        rstd = tmp.enter_context(sbuf(nc, "ln_rstd", [P, NBLK]))
        diag = tmp.enter_context(sbuf(nc, "ln_diagonal", [P, NBLK, P]))
        with phase(nc, "mean_ready", "centred", "squared", "var_ready", "std_ready", "rstd_ready", "diag_ready",
                   "rstd_spread", "normed", "loaded") as (
                block, mean_ready, centred, squared, var_ready, std_ready, rstd_ready, diag_ready, rstd_spread,
                normed, loaded):
            @block.tensor
            def _(pe):
                def variance(c):
                    pe.wait_ge(squared, c + 1)
                    for blk in range(PER * c, PER * (c + 1)):
                        mm = pe.matmul(M.ps[:, 2 + c, blk:blk + 1], sqr[:, blk * P:(blk + 1) * P], M.mean[:, 0:1],
                                       start=True, stop=True)
                    mm.then_inc(var_ready, 1)

                def spread_back(c):
                    pe.wait_ge(diag_ready, c + 1)
                    pe.matmul(M.ps[:, 6 + c if c < 2 else c - 2, :], M.ones[:],
                              diag[:, PER * c:PER * (c + 1), :].rearrange("p n q -> p (n q)"),
                              start=True, stop=True).then_inc(rstd_spread, 1)

                for c in range(NCH):
                    if c >= 2:
                        pe.wait_ge(centred, c - 1)
                        variance(c - 2)
                    pe.matmul(M.ps[:, c % 2, :], M.mean[:], chunk(src, c), start=True, stop=True).then_inc(mean_ready, 1)
                variance(2)
                spread_back(0)
                variance(3)
                pe.wait_ge(centred, NCH)
                for c in range(1, NCH):
                    spread_back(c)

            @block.vector
            def _(dve):
                def center(c):
                    dve.wait_ge(mean_ready, c + 1)
                    dve.tensor_tensor(chunk(cen, c), chunk(src, c), M.ps[:, c % 2, :], ALU.subtract).then_inc(centred, 1)

                def roots(c):
                    part = slice(PER * c, PER * (c + 1))
                    dve.wait_ge(std_ready, c + 1)
                    dve.reciprocal(rstd[:, part], std[:, part]).then_inc(rstd_ready, 1)
                    dve.wait_ge(rstd_ready, c + 1)
                    dve.tensor_tensor(diag[:, part, :], M.ident[:].unsqueeze(1).to_broadcast([P, PER, P]),
                                      wide(rstd[:, part], P), ALU.mult).then_inc(diag_ready, 1)

                def norm(c):
                    dve.wait_ge(rstd_spread, c + 1)
                    dve.tensor_tensor(chunk(sqr, c), chunk(cen, c), M.ps[:, 6 + c if c < 2 else c - 2, :],
                                      ALU.mult).then_inc(normed, 1)

                for c in range(3):
                    center(c)
                roots(0)
                center(3)
                for c in range(1, NCH):
                    roots(c)
                    norm(c - 1)
                norm(NCH - 1)

            @block.scalar
            def _(act):
                def root(c):
                    part = slice(PER * c, PER * (c + 1))
                    act.wait_ge(var_ready, c + 1)
                    act.activation(std[:, part], M.ps[:, 2 + c, part], ACT.Sqrt, bias=M.eps[:]).then_inc(std_ready, 1)

                for c in range(NCH):
                    act.wait_ge(centred, c + 1)
                    act.activation(chunk(sqr, c), chunk(cen, c), ACT.Square).then_inc(squared, 1)
                    if c:
                        root(c - 1)
                root(NCH - 1)
                if loads:
                    act.wait_ge(loaded, 16 * len(loads))
                for c in range(NCH):
                    act.wait_ge(normed, c + 1)
                    act.activation(chunk(dst, c), chunk(sqr, c), ACT.Identity, bias=shift(c // 2),
                                   scale=scale(c // 2))

            @block.sync
            def _(sp):
                for target, source in loads:
                    sp.dma_start(target, source).then_inc(loaded, 16)
                if loads:
                    sp.wait_ge(loaded, 16 * len(loads))


class Attention:

    def __init__(self, nc, D, ctx):
        def sb(name, shape, dt=F32):
            return ctx.enter_context(sbuf(nc, name, shape, dt))
        self.q_dram, self.k_dram = D["q_parts"], D["k_parts"]
        self.v = sb("v_and_one", [P, NBLK, HEADS, DH + 1])
        self.qst = sb("q_stack", [S2_ROWS, STACKS, GROUP, T], BF16)
        self.kst = sb("k_stack", [S2_ROWS, STACKS, GROUP, T], BF16)
        self.o = sb("o_raw", [P, B, NGRP, T])
        self.pick = sb("pick_sums", [P, NGRP, 32])
        self.unpick_dram = D["unpick_sums"]
        self.loads = [(self.kst[PAIR_ROWS:S2_ROWS, s, :, :], D["k_aux"].rearrange("r (j t) -> r j t", j=GROUP))
                      for s in range(STACKS)]
        self.loads.append((self.pick[:].rearrange("p g r -> p (g r)"), D["pick_sums"]))


def load_q_stack(eng, A, q_aux, b, g, s, sem):
    tok = slice(b * T, (b + 1) * T)
    for k_part in range(3):
        at = 3 * DH * k_part
        eng.dma_start(A.qst[at:at + 3 * DH, s, :, :],
                      A.q_dram[g, :, tok].rearrange("(sd j) t -> sd j t", j=GROUP)).then_inc(sem, 16)
    eng.dma_start(A.qst[PAIR_ROWS:S1_ROWS, s, :, :], q_aux[g]).then_inc(sem, 16)


def load_k_stack(eng, A, b, g, s, sem):
    tok = slice(b * T, (b + 1) * T)
    for k_part in range(3):
        part = A.k_dram[g, 4 * DH * k_part:4 * DH * (k_part + 1), tok].rearrange("(d j) t -> d j t", j=GROUP)
        for q_part in range(3):
            at = (3 * k_part + q_part) * DH
            eng.dma_start(A.kst[at:at + DH, s, :, :], part).then_inc(sem, 16)


def qkv(nc, M, A, W, cols, scale, tables=None):
    with ExitStack() as tmp:
        full = tmp.enter_context(sbuf(nc, "qk_full", [P, 8, CH], F32))
        rem = tmp.enter_context(sbuf(nc, "qk_rest", [P, 8, CH], F32))
        parts = tmp.enter_context(sbuf(nc, "qk_parts", [P, 2, 3, N], BF16))
        units = [(what, c) for c in range(NCH) for what in range(2)]

        def col(name):
            a, b = cols[name]
            return W[:, a:b]

        with phase(nc, "proj_ready", "part_a", "part_b", "full_ready", "hi_ready", "rest_ready", "mid_ready",
                   "lo_ready", "v_ready", "parts_out") as (
                block, proj_ready, part_a, part_b, full_ready, hi_ready, rest_ready, mid_ready, lo_ready, v_ready,
                parts_out):
            @block.tensor
            def _(pe):
                for u, (what, c) in enumerate(units):
                    if u >= 2:
                        pe.wait_ge(full_ready if tables is None else part_b, u - 1)
                    mm = pe.matmul(M.ps[:, u % 2, :], col("wq" if what == 0 else "wk"), chunk(M.h, c),
                                   start=True, stop=True)
                    if tables is not None:
                        mm = pe.matmul(M.ps[:, 2 + u % 2, :], col("wqr" if what == 0 else "wkr"), chunk(M.h, c),
                                       start=True, stop=True)
                    mm.then_inc(proj_ready, 1)
                for blk in range(NBLK):
                    mm = pe.matmul(M.ps[:, 4 + blk // 4, (blk % 4) * P:(blk % 4 + 1) * P],
                                   M.h[:, blk * P:(blk + 1) * P], col("wv"), start=True, stop=True)
                    if blk % 4 == 3:
                        mm.then_inc(v_ready, 1)

            @block.vector
            def _(dve):
                def rest(u):
                    what, c = units[u]
                    part = parts[:, what]
                    dve.wait_ge(hi_ready, u + 1)
                    dve.wait_ge(full_ready, u + 1)
                    dve.tensor_tensor(rem[:, u, :], full[:, u, :], part[:, 0, c * CH:(c + 1) * CH],
                                      ALU.subtract).then_inc(rest_ready, 1)

                for u, (what, c) in enumerate(units):
                    dve.wait_ge(proj_ready, u + 1)
                    bias = col("bq" if what == 0 else "bk")
                    if tables is None:
                        dve.tensor_scalar(full[:, u, :], M.ps[:, u % 2, :], bias, scale if what == 0 else 1.0,
                                          ALU.add, ALU.mult).then_inc(full_ready, 1)
                    else:
                        plain, swapped = tables(what, c)
                        dve.scalar_tensor_tensor(rem[:, u, :], M.ps[:, u % 2, :], bias, plain,
                                                 ALU.add, ALU.mult).then_inc(part_a, 1)
                        bias = col("bqr" if what == 0 else "bkr")
                        dve.scalar_tensor_tensor(full[:, u, :], M.ps[:, 2 + u % 2, :], bias, swapped,
                                                 ALU.add, ALU.mult).then_inc(part_b, 1)
                        dve.wait_ge(part_a, u + 1)
                        dve.wait_ge(part_b, u + 1)
                        dve.tensor_tensor(full[:, u, :], rem[:, u, :], full[:, u, :], ALU.add).then_inc(full_ready, 1)
                    if u:
                        rest(u - 1)
                rest(len(units) - 1)
                bv = col("bv").rearrange("p (h d) -> p h d", h=HEADS)
                for blk in range(NBLK):
                    dve.wait_ge(v_ready, blk // 4 + 1)
                    dve.tensor_tensor(
                        A.v[:, blk, :, 0:DH],
                        M.ps[:, 4 + blk // 4, (blk % 4) * P:(blk % 4 + 1) * P].rearrange("p (h d) -> p h d", h=HEADS),
                        bv, ALU.add)

            @block.scalar
            def _(act):
                def mid(u):
                    what, c = units[u]
                    act.wait_ge(rest_ready, u + 1)
                    act.activation(parts[:, what, 1, c * CH:(c + 1) * CH], rem[:, u, :],
                                   ACT.Copy).then_inc(mid_ready, 1)

                for u, (what, c) in enumerate(units):
                    act.wait_ge(full_ready, u + 1)
                    act.activation(parts[:, what, 0, c * CH:(c + 1) * CH], full[:, u, :],
                                   ACT.Copy).then_inc(hi_ready, 1)
                    if u >= 2:
                        mid(u - 2)
                mid(len(units) - 2)
                mid(len(units) - 1)

            @block.gpsimd
            def _(pool):
                pool.memset(A.v[:, :, :, DH:DH + 1], 1.0)
                for u, (what, c) in enumerate(units):
                    part = parts[:, what]
                    pool.wait_ge(mid_ready, u + 1)
                    pool.tensor_tensor(part[:, 2, c * CH:(c + 1) * CH], rem[:, u, :],
                                       part[:, 1, c * CH:(c + 1) * CH], ALU.subtract).then_inc(lo_ready, 1)

            @block.sync
            def _(sp):
                for u, (what, c) in enumerate(units):
                    sp.wait_ge(lo_ready, u + 1)
                    out = (A.q_dram, A.k_dram)[what]
                    for g in range(NGRP):
                        sp.dma_start(out[g, :, c * CH:(c + 1) * CH].rearrange("(s r) t -> r s t", s=3),
                                     parts[32 * g:32 * g + 32, what, :, c * CH:(c + 1) * CH]).then_inc(parts_out, 16)
                sp.wait_ge(parts_out, 16 * len(units) * NGRP)


def attention_core(nc, M, A, q_aux):
    groups = [(b, g) for b in range(B) for g in range(NGRP)]
    NG = len(groups)
    pieces = [(i, lo, min(lo + CH, (i + 1) * P)) for i in range(QB) for lo in range(0, (i + 1) * P, CH)]
    S1U = GROUP * len(pieces)
    S2U = GROUP * QB
    S1_BANK, S2_BANK, O_BANK = 0, 2, 6
    SPLITS = 5
    first_items = []
    for n in range(NG):
        mine = [(n, u) for u in range(S1U)]
        if n:
            mine.insert(TURN_LAG, (n - 1, None))
        first_items += mine
    first_items.append((NG - 1, None))
    HEAD = S1U + TURN_LAG + 1 + FIRST_AHEAD
    banks = [k % O_BANK if k < HEAD else S1_BANK + k % 2 for k in range(len(first_items))]
    last_in_bank = [max((i for i in range(k) if banks[i] == banks[k]), default=None) for k in range(len(banks))]
    per_step = [STEP_EARLY if kb < QB // 2 else STEP_LATE for kb in range(QB) for _ in range(GROUP)]
    scale = (S1U + 1) / sum(per_step)

    def items_by(v):
        return min(len(first_items),
                   HEAD + (v // S2U) * (S1U + 1) + int(round(scale * sum(per_step[:v % S2U + 1]))))

    with ExitStack() as tmp:
        prob = tmp.enter_context(sbuf(nc, "prob", [P, 2, GROUP, T], F32))
        mparts = tmp.enter_context(sbuf(nc, "max_parts", [P, GROUP, QB, 2], F32))
        rowmax = tmp.enter_context(sbuf(nc, "row_max", [P, GROUP * QB], F32))
        mfull = tmp.enter_context(sbuf(nc, "neg_max", [GROUP * QB, P], F32))
        mrest = tmp.enter_context(sbuf(nc, "neg_max_rest", [GROUP * QB, P], F32))
        m3 = tmp.enter_context(sbuf(nc, "neg_max_parts", [GROUP * QB, 3, P], BF16))
        names = [f"stack_loaded{s}" for s in range(STACKS)] + [f"max_rows_in{s}" for s in range(STACKS)]
        with phase(nc, *names, "cleared", "first_ready", "first_read", "max_joined", "max_split",
                   "s2_ready", "exp_done", "pv_done", "o_saved") as (block, *sems):
            stack_loaded, max_rows_in = sems[:STACKS], sems[STACKS:2 * STACKS]
            (cleared, first_ready, first_read, max_joined, max_split, s2_ready, exp_done, pv_done,
             o_saved) = sems[2 * STACKS:]

            @block.sync
            def _(sp):
                def stack(n):
                    b, g = groups[n]
                    s = n % STACKS
                    if n >= STACKS:
                        sp.wait_ge(s2_ready, S2U * (n - STACKS + 1))
                    load_k_stack(sp, A, b, g, s, stack_loaded[s])
                    load_q_stack(sp, A, q_aux, b, g, s, stack_loaded[s])

                def max_rows(n):
                    s = n % STACKS
                    sp.wait_ge(max_split, SPLITS * (n + 1))
                    for part in range(3):
                        row = S1_ROWS + part
                        sp.dma_start(A.qst[row:row + 1, s, :, :].rearrange("o j (i q) -> o (j i) q", i=QB),
                                     m3[:, part, :]).then_inc(max_rows_in[s], 16)

                for n in range(STACKS):
                    stack(n)
                for n in range(NG):
                    max_rows(n)
                    if n and n - 1 + STACKS < NG:
                        stack(n - 1 + STACKS)
                for s in range(STACKS):
                    sp.wait_ge(max_rows_in[s], 48 * len(range(s, NG, STACKS)))

            @block.tensor
            def _(pe):
                def first(k):
                    n, u = first_items[k]
                    if last_in_bank[k] is not None:
                        pe.wait_ge(first_read, last_in_bank[k] + 1)
                    if u is None:
                        pe.wait_ge(max_joined, n + 1)
                        pe.transpose(M.ps[0:GROUP * QB, banks[k], 0:P], rowmax[:], M.ident[:]).then_inc(first_ready, 1)
                        return
                    j, (i, lo, hi) = u // len(pieces), pieces[u % len(pieces)]
                    s = n % STACKS
                    if u == 0:
                        pe.wait_ge(stack_loaded[s], 16 * STACK_DMAS * (n // STACKS + 1))
                    out = M.ps[:, banks[k], 0:hi - lo]
                    diag = hi == (i + 1) * P
                    mm = pe.matmul(out, A.qst[0:S1_ROWS, s, j, i * P:(i + 1) * P], A.kst[0:S1_ROWS, s, j, lo:hi],
                                   start=True, stop=not diag)
                    if diag:
                        mm = pe.matmul(out[:, hi - lo - P:hi - lo], M.identb[:], M.mask_qk[:], start=False, stop=True)
                    mm.then_inc(first_ready, 1)

                def second(n, kb, j):
                    s = n % STACKS
                    v = S2U * n + kb * GROUP + j
                    if kb == 0 and j == 0:
                        pe.wait_ge(max_rows_in[s], 48 * (n // STACKS + 1))
                    if v >= 2:
                        pe.wait_ge(exp_done, v - 1)
                    else:
                        pe.wait_ge(first_read, HEAD)
                    base = S2_BANK + 2 * (v % 2)
                    lhs = A.kst[0:S2_ROWS, s, j, kb * P:(kb + 1) * P]
                    diag_bank = kb // 4
                    for half in range(diag_bank, 2):
                        a = max(kb * P - half * CH, 0)
                        q0 = half * CH + a
                        mm = pe.matmul(M.ps[:, base + half, a:CH], lhs, A.qst[0:S2_ROWS, s, j, q0:(half + 1) * CH],
                                       start=True, stop=half != diag_bank)
                        if half == diag_bank:
                            mm = pe.matmul(M.ps[:, base + half, a:a + P], M.identb[:], M.mask_kq[:],
                                           start=False, stop=True)
                    mm.then_inc(s2_ready, 1)

                def weigh(n, kb, half):
                    if half < kb // 4:
                        return
                    b, g = groups[n]
                    pe.wait_ge(exp_done, S2U * n + GROUP * (kb + 1))
                    if kb == 0 and half == 0:
                        pe.wait_ge(cleared, 2)
                        if n:
                            pe.wait_ge(o_saved, n)
                    a = max(kb * P - half * CH, 0)
                    for j in range(GROUP):
                        mm = pe.matmul(M.ps[32 * j:32 * j + DH + 1, O_BANK + half, a:CH],
                                       A.v[:, b * QB + kb, GROUP * g + j, :],
                                       prob[:, kb % 2, j, half * CH + a:(half + 1) * CH],
                                       start=kb == 0, stop=kb == 4 * half + 3)
                    if half == 1:
                        mm.then_inc(pv_done, 1)

                k = 0
                while k < HEAD:
                    first(k)
                    k += 1
                for n in range(NG):
                    for kb in range(QB):
                        for j in range(GROUP):
                            second(n, kb, j)
                            while k < items_by(S2U * n + GROUP * kb + j):
                                first(k)
                                k += 1
                            if j % 2 and (n or kb):
                                weigh(n if kb else n - 1, (kb - 1) % QB, j // 2)
                for half in range(2):
                    weigh(NG - 1, QB - 1, half)

            @block.vector
            def _(dve):
                def take_turned(k):
                    n = first_items[k][0]
                    at = SPLITS * n
                    dve.wait_ge(first_ready, k + 1)
                    dve.tensor_scalar(mfull[:], M.ps[0:GROUP * QB, banks[k], 0:P], -1.0, None,
                                      ALU.mult).then_inc(max_split, 1)
                    dve.wait_ge(max_split, at + 1)
                    if n:
                        dve.wait_ge(max_rows_in[(n - 1) % STACKS], 48 * ((n - 1) // STACKS + 1))
                    dve.tensor_copy(m3[:, 0, :], mfull[:]).then_inc(max_split, 1)
                    dve.wait_ge(max_split, at + 2)
                    dve.tensor_tensor(mrest[:], mfull[:], m3[:, 0, :], ALU.subtract).then_inc(max_split, 1)
                    dve.wait_ge(max_split, at + 3)
                    dve.tensor_copy(m3[:, 1, :], mrest[:]).then_inc(max_split, 1)
                    dve.wait_ge(max_split, at + 4)
                    dve.tensor_tensor(m3[:, 2, :], mrest[:], m3[:, 1, :], ALU.subtract).then_inc(max_split, 1)
                    dve.sem_inc(first_read, 1)

                dve.memset(mparts[:], -3.0e38).then_inc(cleared, 1)
                dve.memset(M.ps[:, O_BANK:O_BANK + 2, :], 0.0).then_inc(cleared, 1)
                dve.wait_ge(cleared, 2)
                for k, (n, u) in enumerate(first_items):
                    if u is None:
                        take_turned(k)
                        continue
                    j, (i, lo, hi) = u // len(pieces), pieces[u % len(pieces)]
                    dve.wait_ge(first_ready, k + 1)
                    if u == 0 and n:
                        dve.wait_ge(max_joined, n)
                    dve.reduce_max(mparts[:, j, i, lo // CH:lo // CH + 1],
                                   M.ps[:, banks[k], 0:hi - lo], AX_X).then_inc(first_read, 1)
                    if u == S1U - 1:
                        dve.wait_ge(first_read, k + 1)
                        dve.tensor_reduce(rowmax[:], mparts[:].rearrange("p j i c -> p (j i) c"), AX_X,
                                          ALU.max).then_inc(max_joined, 1)

            @block.scalar
            def _(act):
                def save(n):
                    b, g = groups[n]
                    act.wait_ge(pv_done, QB * (n + 1))
                    act.activation(A.o[:, b, g, :], M.ps[:, O_BANK:O_BANK + 2, :].rearrange("p a q -> p (a q)"),
                                   ACT.Copy).then_inc(o_saved, 1)

                for n in range(NG):
                    for kb in range(QB):
                        for j in range(GROUP):
                            v = S2U * n + kb * GROUP + j
                            act.wait_ge(s2_ready, v + 1)
                            if j == 0 and n * QB + kb >= 2:
                                act.wait_ge(pv_done, n * QB + kb - 1)
                            base = S2_BANK + 2 * (v % 2)
                            scores = M.ps[:, base:base + 2, :].rearrange("p a q -> p (a q)")
                            act.activation(prob[:, kb % 2, j, kb * P:T], scores[:, kb * P:T],
                                           ACT.Exp).then_inc(exp_done, 1)
                            if n and kb == 1 and j == 0:
                                save(n - 1)
                save(NG - 1)


def attention_out(nc, M, A, wo, bo, dst, gain=None):
    units = [(c, g) for c in range(NCH) for g in range(NGRP)]
    SUM_BANK = 7

    def raw(u):
        c, g = units[u]
        return A.o[:, c // 2, g, (c % 2) * CH:(c % 2 + 1) * CH]

    with ExitStack() as tmp:
        unpick = tmp.enter_context(sbuf(nc, "unpick_sums", [P, NCH, NGRP, P]))
        rec = tmp.enter_context(sbuf(nc, "sum_recip", [P, CH]))
        norm = tmp.enter_context(sbuf(nc, "o_normed", [P, 3, CH]))
        upd = tmp.enter_context(sbuf(nc, "o_update", [P, 2, CH]))
        with phase(nc, "unpick_in", "sums_ready", "recip_ready", "spread_ready", "norm_ready", "proj_step", "scaled",
                   "added") as (
                block, unpick_in, sums_ready, recip_ready, spread_ready, norm_ready, proj_step, scaled, added):
            @block.sync
            def _(sp):
                sp.dma_start(unpick[:].rearrange("p c g q -> p (c g q)"), A.unpick_dram).then_inc(unpick_in, 16)

            @block.tensor
            def _(pe):
                def project(u):
                    c, g = units[u]
                    pe.wait_ge(norm_ready, u + 1)
                    if g == 0 and c >= 2:
                        pe.wait_ge(scaled, c - 1)
                    pe.matmul(M.ps[:, 4 + c % 2, :], wo[:, g * P:(g + 1) * P], norm[:, u % 3, :],
                              start=g == 0, stop=g == NGRP - 1).then_inc(proj_step, 1)

                for g in range(NGRP):
                    for c in range(NCH):
                        mm = pe.matmul(M.ps[32 * c:32 * c + 32, SUM_BANK, :], A.pick[:, g, :], raw(c * NGRP + g),
                                       start=g == 0, stop=g == NGRP - 1)
                mm.then_inc(sums_ready, 1)
                pe.wait_ge(unpick_in, 16)
                pe.wait_ge(recip_ready, 1)
                for u, (c, g) in enumerate(units):
                    if u >= 4:
                        pe.wait_ge(norm_ready, u - 3)
                    pe.matmul(M.ps[:, u % 4, :], unpick[:, c, g, :], rec[:], start=True, stop=True).then_inc(spread_ready, 1)
                    if u >= 2:
                        project(u - 2)
                project(len(units) - 2)
                project(len(units) - 1)

            @block.vector
            def _(dve):
                def last(c):
                    dve.wait_ge(proj_step, NGRP * (c + 1))
                    if gain is None:
                        dve.scalar_tensor_tensor(chunk(dst, c), M.ps[:, 4 + c % 2, :], bo, chunk(dst, c),
                                                 ALU.add, ALU.add).then_inc(scaled, 1)
                    else:
                        if c >= 2:
                            dve.wait_ge(added, c - 1)
                        dve.tensor_scalar(upd[:, c % 2, :], M.ps[:, 4 + c % 2, :], bo, gain(c // 2),
                                          ALU.add, ALU.mult).then_inc(scaled, 1)
                        dve.wait_ge(scaled, c + 1)
                        dve.tensor_tensor(chunk(dst, c), chunk(dst, c), upd[:, c % 2, :], ALU.add).then_inc(added, 1)

                dve.wait_ge(sums_ready, 1)
                dve.reciprocal(rec[:], M.ps[:, SUM_BANK, :]).then_inc(recip_ready, 1)
                for u, (c, g) in enumerate(units):
                    dve.wait_ge(spread_ready, u + 1)
                    if u >= 3:
                        dve.wait_ge(proj_step, u - 2)
                    dve.tensor_tensor(norm[:, u % 3, :], raw(u), M.ps[:, u % 4, :], ALU.mult).then_inc(norm_ready, 1)
                    if u >= NGRP and g == 2:
                        last(c - 1)
                last(NCH - 1)


def feed_forward(nc, M, W, dst):
    def col(name):
        a, b = L0_COLS[name]
        return W[:, a:b]

    with ExitStack() as tmp:
        hid = tmp.enter_context(sbuf(nc, "ffn_hidden", [P, 2, 4, CH], F32))
        with phase(nc, "up_ready", "hidden_ready", "down_ready", "added") as (
                block, up_ready, hidden_ready, down_ready, added):
            @block.tensor
            def _(pe):
                def down(c):
                    if c >= 2:
                        pe.wait_ge(added, c - 1)
                    for f in range(4):
                        pe.wait_ge(hidden_ready, 4 * c + f + 1)
                        mm = pe.matmul(M.ps[:, 4 + c % 2, :], col("w2")[:, f * P:(f + 1) * P], hid[:, c % 2, f, :],
                                       start=f == 0, stop=f == 3)
                    mm.then_inc(down_ready, 1)

                for c in range(NCH):
                    for f in range(4):
                        if c:
                            pe.wait_ge(hidden_ready, 4 * (c - 1) + f + 1)
                        pe.matmul(M.ps[:, f, :], col("w1")[:, f * P:(f + 1) * P], chunk(M.h, c),
                                  start=True, stop=True).then_inc(up_ready, 1)
                    if c:
                        down(c - 1)
                down(NCH - 1)

            @block.scalar
            def _(act):
                for c in range(NCH):
                    for f in range(4):
                        act.wait_ge(up_ready, 4 * c + f + 1)
                        if c >= 2:
                            act.wait_ge(down_ready, c - 1)
                        act.activation(hid[:, c % 2, f, :], M.ps[:, f, :], ACT.Gelu,
                                       bias=col("b1")[:, f:f + 1]).then_inc(hidden_ready, 1)

            @block.vector
            def _(dve):
                for c in range(NCH):
                    dve.wait_ge(down_ready, c + 1)
                    dve.scalar_tensor_tensor(chunk(dst, c), M.ps[:, 4 + c % 2, :], col("b2"), chunk(dst, c),
                                             ALU.add, ALU.add).then_inc(added, 1)


def add_scaled(nc, M, update, gain):
    with phase(nc, "added") as (block, added):
        @block.vector
        def _(dve):
            for b in range(B):
                t = slice(b * T, (b + 1) * T)
                dve.scalar_tensor_tensor(M.x[:, t], update[:, t], gain(b), M.x[:, t], ALU.mult, ALU.add)


def transformer(nc, M, D):
    with ExitStack() as ctx:
        z = ctx.enter_context(sbuf(nc, "z_T", [P, N], F32))
        W = ctx.enter_context(sbuf(nc, "l0_weights", [P, L0_WIDTH], F32))
        fin = ctx.enter_context(sbuf(nc, "l0_final", [P, 2], F32))
        A = Attention(nc, D, ctx)

        def col(name):
            a, b = L0_COLS[name]
            return W[:, a:b]

        layer_norm(nc, M, M.x, z, lambda b: M.mod[:, 0, 1, b:b + 1], lambda b: M.mod[:, 0, 0, b:b + 1],
                   [(fin[:], D["l0_final"])] + A.loads)
        with nc.Fori(0, 4) as layer:
            layer_norm(nc, M, z, M.h, lambda b: col("ln1w"), lambda b: col("ln1b"),
                       [(W[:], D["l0_weights"][bass.ds(layer * P, P), :])])
            qkv(nc, M, A, W, L0_COLS, DH ** -0.5)
            attention_core(nc, M, A, [D["alibi"][g * 6:g * 6 + 6].rearrange("r (j t) -> r j t", j=GROUP)
                                      for g in range(NGRP)])
            attention_out(nc, M, A, col("wo"), col("bo"), z)
            layer_norm(nc, M, z, M.h, lambda b: col("ln2w"), lambda b: col("ln2b"))
            feed_forward(nc, M, W, z)
        layer_norm(nc, M, z, M.h, lambda b: fin[:, 0:1], lambda b: fin[:, 1:2])
        add_scaled(nc, M, M.h, lambda b: M.mod[:, 0, 2, b:b + 1])


def store(nc, M, out):
    with phase(nc, "stored") as (block, stored):
        @block.sync
        def _(sp):
            sp.dma_start(out, M.x[:]).then_inc(stored, 16)
            sp.wait_ge(stored, 16)


def steps(eng, sem):
    count = [0]

    def done(ins):
        ins.then_inc(sem, 1)
        count[0] += 1
        eng.wait_ge(sem, count[0])
    return done


class Gates:

    PARTS_AT = 32

    def __init__(self, nc, D, ctx, full=False):
        self.parts = ctx.enter_context(sbuf(nc, "gate_parts", [96, N], BF16))
        self.full = ctx.enter_context(sbuf(nc, "gate_full", [P if full else 16, N]))
        self.sel = ctx.enter_context(sbuf(nc, "spread_rows", [96, 16, P], BF16))
        self.needs_full = full
        self.loads = [(self.sel[:].rearrange("r e p -> r (e p)"), D["spread"])]


def route(nc, M, G, E, kind, router, bias=None):
    with ExitStack() as tmp:
        def sb(name, shape, dt=F32):
            return tmp.enter_context(sbuf(nc, name, shape, dt))
        lg = sb("logits", [P, NBLK, E])
        pr = sb("scores", [P, NBLK, E])
        sel = sb("selected", [P, NBLK, E])
        one = [sb("first_hot", [P, NBLK, E]), sb("second_hot", [P, NBLK, E])]
        stat = sb("row_stat", [P, NBLK])
        ok = sb("row_ok", [P, NBLK])
        top = sb("top8", [P, NBLK, 8])
        idx = sb("top8_at", [P, NBLK, 8], U32)
        idxf = sb("top8_at_f", [P, NBLK, 8])
        iota = sb("expert_ids", [P, E])
        w = sb("gates", [P, NBLK, E])
        rest = sb("gate_rest", [16, N])
        mid = sb("gate_mid", [16, N], BF16)
        with phase(nc, "made", "logits_ready", "shifted", "exped", "chain", "gates_ready",
                   "turned", "hi_ready", "rest_ready", "mid_ready") as (
                block, made, logits_ready, shifted, exped, chain, gates_ready, turned, hi_ready, rest_ready,
                mid_ready):
            @block.gpsimd
            def _(pool):
                pool.iota(iota[:], pattern=[[1, E]], base=0, channel_multiplier=0,
                          allow_small_or_imprecise_dtypes=True).then_inc(made, 1)
                pool.memset(G.parts[:], 0.0).then_inc(made, 1)
                pool.memset(G.full[:], 0.0).then_inc(made, 1)

            @block.tensor
            def _(pe):
                for blk in range(NBLK):
                    mm = pe.matmul(M.ps[:, 0, blk * E:(blk + 1) * E], M.h[:, blk * P:(blk + 1) * P], router,
                                   start=True, stop=True)
                mm.then_inc(logits_ready, 1)
                pe.wait_ge(gates_ready, 1)
                for blk in range(NBLK):
                    mm = pe.transpose(M.ps[0:E, 4 + blk // 4, (blk % 4) * P:(blk % 4 + 1) * P], w[:, blk, :],
                                      M.ident[:])
                mm.then_inc(turned, 1)

            @block.scalar
            def _(act):
                logits = M.ps[:, 0, 0:NBLK * E].rearrange("p (n e) -> p n e", e=E)
                if kind == "sigmoid":
                    act.wait_ge(logits_ready, 1)
                    act.activation(pr[:], logits, ACT.Sigmoid).then_inc(exped, 1)
                else:
                    act.wait_ge(shifted, 1)
                    act.activation(pr[:], lg[:], ACT.Exp).then_inc(exped, 1)

                def middle(c):
                    act.wait_ge(rest_ready, c + 1)
                    act.activation(chunk(mid, c)[0:E], chunk(rest, c)[0:E], ACT.Copy).then_inc(mid_ready, 1)
                    act.wait_ge(mid_ready, c + 1)
                    act.activation(chunk(G.parts, c)[32:32 + E], chunk(mid, c)[0:E], ACT.Copy)

                act.wait_ge(turned, 1)
                act.wait_ge(made, 3)
                for c in range(NCH):
                    act.activation(chunk(G.parts, c)[0:E], M.ps[0:E, 4 + c, :], ACT.Copy).then_inc(hi_ready, 1)
                    if c:
                        middle(c - 1)
                middle(NCH - 1)

            @block.vector
            def _(dve):
                done = steps(dve, chain)
                logits = M.ps[:, 0, 0:NBLK * E].rearrange("p (n e) -> p n e", e=E)
                dve.wait_ge(logits_ready, 1)
                if kind == "sigmoid":
                    dve.wait_ge(exped, 1)
                    done(dve.tensor_tensor(sel[:], pr[:], bias.unsqueeze(1).to_broadcast([P, NBLK, E]), ALU.add))
                    choice = sel
                else:
                    if bias is not None:
                        done(dve.tensor_tensor(lg[:], logits, bias.unsqueeze(1).to_broadcast([P, NBLK, E]), ALU.add))
                    else:
                        done(dve.tensor_copy(lg[:], logits))
                    done(dve.tensor_reduce(stat[:], lg[:], AX_X, ALU.max))
                    dve.tensor_tensor(lg[:], lg[:], wide(stat[:], E), ALU.subtract).then_inc(shifted, 1)
                    dve.wait_ge(exped, 1)
                    done(dve.tensor_reduce(stat[:], pr[:], AX_X, ALU.add))
                    done(dve.reciprocal(stat[:], stat[:]))
                    done(dve.tensor_tensor(pr[:], pr[:], wide(stat[:], E), ALU.mult))
                    choice = pr
                for blk in range(NBLK):
                    ins = dve.max(top[:, blk, :], choice[:, blk, :])
                done(ins)
                for blk in range(NBLK):
                    ins = dve.max_index(idx[:, blk, :], top[:, blk, :], choice[:, blk, :])
                done(ins)
                done(dve.tensor_copy(idxf[:], idx[:]))
                dve.wait_ge(made, 3)
                for k in range(2):
                    done(dve.tensor_tensor(one[k][:], iota[:].unsqueeze(1).to_broadcast([P, NBLK, E]),
                                           wide(idxf[:, :, k], E), ALU.is_equal))
                if kind == "sigmoid":
                    done(dve.tensor_tensor(sel[:], one[0][:], one[1][:], ALU.add))
                    done(dve.tensor_tensor(w[:], sel[:], pr[:], ALU.mult))
                    done(dve.tensor_reduce(stat[:], w[:], AX_X, ALU.add))
                    done(dve.tensor_scalar(ok[:], stat[:], 1e-9, None, ALU.is_gt))
                    done(dve.tensor_scalar(stat[:], stat[:], 1e-9, None, ALU.add))
                    done(dve.reciprocal(stat[:], stat[:]))
                    done(dve.tensor_tensor(stat[:], stat[:], ok[:], ALU.mult))
                    done(dve.tensor_tensor(w[:], w[:], wide(stat[:], E), ALU.mult))
                    done(dve.tensor_scalar(ok[:], ok[:], -0.5, 0.5, ALU.mult, ALU.add))
                    done(dve.tensor_tensor(sel[:], sel[:], wide(ok[:], E), ALU.mult))
                    dve.tensor_tensor(w[:], w[:], sel[:], ALU.add).then_inc(gates_ready, 1)
                else:
                    by = [top[:, :, k] if kind == "softmax" else pr[:, :, k] for k in range(2)]
                    for k in range(2):
                        done(dve.tensor_tensor(one[k][:], one[k][:], wide(by[k], E), ALU.mult))
                    dve.tensor_tensor(w[:], one[0][:], one[1][:], ALU.add).then_inc(gates_ready, 1)
                def last_part(c):
                    dve.wait_ge(mid_ready, c + 1)
                    dve.tensor_tensor(chunk(G.parts, c)[64:64 + E], chunk(rest, c)[0:E], chunk(mid, c)[0:E],
                                      ALU.subtract)

                dve.wait_ge(turned, 1)
                dve.wait_ge(made, 3)
                for c in range(NCH):
                    dve.wait_ge(hi_ready, c + 1)
                    dve.tensor_tensor(chunk(rest, c)[0:E], M.ps[0:E, 4 + c, :], chunk(G.parts, c)[0:E],
                                      ALU.subtract).then_inc(rest_ready, 1)
                    if G.needs_full:
                        dve.tensor_copy(chunk(G.full, c)[0:E], M.ps[0:E, 4 + c, :])
                    if c:
                        last_part(c - 1)
                last_part(NCH - 1)


def spread(pe, G, out, e, c):
    return pe.matmul(out, G.sel[:, e, :], chunk(G.parts, c), start=True, stop=True)


def moe_l0(nc, M, D):
    E = 16
    with ExitStack() as ctx:
        def sb(name, shape, dt=F32):
            return ctx.enter_context(sbuf(nc, name, shape, dt))
        we = sb("experts", [P, E, P])
        small = sb("router_and_bias", [P, 2 * E])
        G = Gates(nc, D, ctx)
        layer_norm(nc, M, M.x, M.h, lambda b: M.mod[:, 0, 4, b:b + 1], lambda b: M.mod[:, 0, 3, b:b + 1],
                   [(small[:], D["l0_small"]), (we[:], D["l0_experts"].rearrange("p (e d) -> p e d", e=E))] + G.loads)
        route(nc, M, G, E, "softmax", small[:, 0:E])
        R = 3
        act_out = sb("expert_out", [P, R, CH])
        weighed = sb("expert_weighed", [P, R, CH])
        acc = sb("moe_sum", [P, N])
        units = [(e, c) for e in range(E) for c in range(NCH)]
        with phase(nc, "cleared", "proj_ready", "spread_ready", "relu_ready", "weighed_ready", "summed") as (
                block, cleared, proj_ready, spread_ready, relu_ready, weighed_ready, summed):
            @block.tensor
            def _(pe):
                for u, (e, c) in enumerate(units):
                    if u >= 4:
                        pe.wait_ge(relu_ready, u - 3)
                    pe.matmul(M.ps[:, u % 4, :], we[:, e, :], chunk(M.h, c), start=True,
                              stop=True).then_inc(proj_ready, 1)
                    if u >= 4:
                        pe.wait_ge(weighed_ready, u - 3)
                    spread(pe, G, M.ps[:, 4 + u % 4, :], e, c).then_inc(spread_ready, 1)

            @block.scalar
            def _(act):
                for u, (e, c) in enumerate(units):
                    act.wait_ge(proj_ready, u + 1)
                    if u >= R:
                        act.wait_ge(weighed_ready, u - R + 1)
                    act.activation(act_out[:, u % R, :], M.ps[:, u % 4, :], ACT.Relu,
                                   bias=small[:, E + e:E + e + 1]).then_inc(relu_ready, 1)

            @block.vector
            def _(dve):
                for u, (e, c) in enumerate(units):
                    dve.wait_ge(relu_ready, u + 1)
                    dve.wait_ge(spread_ready, u + 1)
                    if u >= R:
                        dve.wait_ge(summed, u - R + 1)
                    dve.tensor_tensor(weighed[:, u % R, :], act_out[:, u % R, :], M.ps[:, 4 + u % 4, :],
                                      ALU.mult).then_inc(weighed_ready, 1)

            @block.gpsimd
            def _(pool):
                pool.memset(acc[:], 0.0).then_inc(cleared, 1)
                pool.wait_ge(cleared, 1)
                for u, (e, c) in enumerate(units):
                    pool.wait_ge(weighed_ready, u + 1)
                    if e:
                        pool.wait_ge(summed, u - NCH + 1)
                    pool.tensor_tensor(chunk(acc, c), chunk(acc, c), weighed[:, u % R, :], ALU.add).then_inc(summed, 1)
        add_scaled(nc, M, acc, lambda b: M.mod[:, 0, 5, b:b + 1])


def moe_l1(nc, M, D):
    E, S = 8, 2
    with ExitStack() as ctx:
        def sb(name, shape, dt=F32):
            return ctx.enter_context(sbuf(nc, name, shape, dt))
        up = sb("experts_up", [P, E, P])
        down = sb("experts_down", [P, E, P])
        shared = sb("shared", [P, 3, S, P])
        small = sb("router_and_bias", [P, 2 * E])
        G = Gates(nc, D, ctx)
        layer_norm(nc, M, M.x, M.h, lambda b: M.mod[:, 1, 4, b:b + 1], lambda b: M.mod[:, 1, 3, b:b + 1],
              [(up[:], D["l1_up"].rearrange("p (e d) -> p e d", e=E)),
               (down[:], D["l1_down"].rearrange("p (e d) -> p e d", e=E)),
               (shared[:], D["l1_shared"].rearrange("p (k s d) -> p k s d", k=3, s=S)),
               (small[:], D["l1_small"])] + G.loads)
        route(nc, M, G, E, "sigmoid", small[:, 0:E], small[:, E:2 * E])
        R = 3
        gated = sb("shared_hidden", [P, NCH, S, CH])
        silu = sb("shared_silu", [P, 2, CH])
        hid = sb("expert_hidden", [P, R, CH])
        weighed = sb("expert_weighed", [P, R, CH])
        pairs = [(c, s) for c in range(NCH) for s in range(S)]
        units = [(c, e) for c in range(NCH) for e in range(E)]
        with phase(nc, "shared_ready", "silu_ready", "gated_ready", "up_ready", "spread_ready", "hidden_ready",
                   "weighed_ready", "down_ready", "added") as (
                block, shared_ready, silu_ready, gated_ready, up_ready, spread_ready, hidden_ready, weighed_ready,
                down_ready, added):
            @block.tensor
            def _(pe):
                for i, (c, s) in enumerate(pairs):
                    if i >= 2:
                        pe.wait_ge(gated_ready, i - 1)
                    pe.matmul(M.ps[:, 2 * (i % 2), :], shared[:, 0, s, :], chunk(M.h, c), start=True, stop=True)
                    pe.matmul(M.ps[:, 2 * (i % 2) + 1, :], shared[:, 1, s, :], chunk(M.h, c), start=True,
                              stop=True).then_inc(shared_ready, 1)
                pe.wait_ge(gated_ready, len(pairs))

                def finish(u):
                    c, e = units[u]
                    if e == 0:
                        if c >= 2:
                            pe.wait_ge(added, c - 1)
                        for s in range(S):
                            pe.matmul(M.ps[:, 6 + c % 2, :], shared[:, 2, s, :], gated[:, c, s, :],
                                      start=s == 0, stop=False)
                    pe.wait_ge(weighed_ready, u + 1)
                    pe.matmul(M.ps[:, 6 + c % 2, :], down[:, e, :], weighed[:, u % R, :], start=False,
                              stop=e == E - 1).then_inc(down_ready, 1)

                for u, (c, e) in enumerate(units):
                    if u >= 3:
                        pe.wait_ge(hidden_ready, u - 2)
                    pe.matmul(M.ps[:, u % 3, :], up[:, e, :], chunk(M.h, c), start=True, stop=True).then_inc(up_ready, 1)
                    if u >= 3:
                        pe.wait_ge(weighed_ready, u - 2)
                    spread(pe, G, M.ps[:, 3 + u % 3, :], e, c).then_inc(spread_ready, 1)
                    if u:
                        finish(u - 1)
                finish(len(units) - 1)

            @block.scalar
            def _(act):
                for i, (c, s) in enumerate(pairs):
                    act.wait_ge(shared_ready, i + 1)
                    if i >= 2:
                        act.wait_ge(gated_ready, i - 1)
                    act.activation(silu[:, i % 2, :], M.ps[:, 2 * (i % 2), :], ACT.Silu).then_inc(silu_ready, 1)
                for u in range(len(units)):
                    act.wait_ge(up_ready, u + 1)
                    if u >= R:
                        act.wait_ge(weighed_ready, u - R + 1)
                    act.activation(hid[:, u % R, :], M.ps[:, u % 3, :], ACT.Gelu).then_inc(hidden_ready, 1)

            @block.vector
            def _(dve):
                for i, (c, s) in enumerate(pairs):
                    dve.wait_ge(silu_ready, i + 1)
                    dve.tensor_tensor(gated[:, c, s, :], silu[:, i % 2, :], M.ps[:, 2 * (i % 2) + 1, :],
                                      ALU.mult).then_inc(gated_ready, 1)
                for u, (c, e) in enumerate(units):
                    dve.wait_ge(hidden_ready, u + 1)
                    dve.wait_ge(spread_ready, u + 1)
                    if u >= R:
                        dve.wait_ge(down_ready, u - R + 1)
                    dve.tensor_tensor(weighed[:, u % R, :], hid[:, u % R, :], M.ps[:, 3 + u % 3, :],
                                      ALU.mult).then_inc(weighed_ready, 1)
                    if e == E - 1:
                        dve.wait_ge(down_ready, u + 1)
                        dve.scalar_tensor_tensor(chunk(M.x, c), M.ps[:, 6 + c % 2, :],
                                                 M.mod[:, 1, 5, c // 2:c // 2 + 1], chunk(M.x, c),
                                                 ALU.mult, ALU.add).then_inc(added, 1)


def moe_l2(nc, M, D):
    E = 8
    with ExitStack() as ctx:
        def sb(name, shape, dt=F32):
            return ctx.enter_context(sbuf(nc, name, shape, dt))
        w = sb("experts", [P, 3, E, P])
        bias = sb("expert_bias", [P, 2, E])
        b3 = sb("expert_bias3", [P, P])
        small = sb("router_and_bias", [P, 2 * E])
        G = Gates(nc, D, ctx, full=True)
        layer_norm(nc, M, M.x, M.h, lambda b: M.mod[:, 2, 4, b:b + 1], lambda b: M.mod[:, 2, 3, b:b + 1],
              [(w[:], D["l2_experts"].rearrange("p (k e d) -> p k e d", k=3, e=E)),
               (bias[:], D["l2_bias"].rearrange("p (k e) -> p k e", k=2)), (b3[:], D["l2_b3"]),
               (small[:], D["l2_small"])] + G.loads)
        route(nc, M, G, E, "softmax01", small[:, 0:E], small[:, E:2 * E])
        R = 3
        h1 = sb("hidden_1", [P, R, CH])
        h2 = sb("hidden_2", [P, R, CH])
        weighed = sb("hidden_weighed", [P, R, CH])
        units = [(c, e) for c in range(NCH) for e in range(E)]
        U = len(units)
        with phase(nc, "up1", "relu1", "up2", "relu2", "spread_ready", "weighed_ready", "down_ready", "added") as (
                block, up1, relu1, up2, relu2, spread_ready, weighed_ready, down_ready, added):
            @block.tensor
            def _(pe):
                for t in range(U + 2):
                    if t < U:
                        c, e = units[t]
                        if t >= 2:
                            pe.wait_ge(relu1, t - 1)
                        pe.matmul(M.ps[:, t % 2, :], w[:, 0, e, :], chunk(M.h, c), start=True, stop=True).then_inc(up1, 1)
                    if 1 <= t <= U:
                        u = t - 1
                        c, e = units[u]
                        pe.wait_ge(relu1, u + 1)
                        if u >= 2:
                            pe.wait_ge(relu2, u - 1)
                        pe.matmul(M.ps[:, 2 + u % 2, :], w[:, 1, e, :], h1[:, u % R, :], start=True,
                                  stop=True).then_inc(up2, 1)
                        if u >= 2:
                            pe.wait_ge(weighed_ready, u - 1)
                        spread(pe, G, M.ps[:, 4 + u % 2, :], e, c).then_inc(spread_ready, 1)
                    if t >= 2:
                        u = t - 2
                        c, e = units[u]
                        if e == 0:
                            if c >= 2:
                                pe.wait_ge(added, c - 1)
                            pe.matmul(M.ps[:, 6 + c % 2, :], b3[:], chunk(G.full, c), start=True, stop=False)
                        pe.wait_ge(weighed_ready, u + 1)
                        pe.matmul(M.ps[:, 6 + c % 2, :], w[:, 2, e, :], weighed[:, u % R, :], start=False,
                                  stop=e == E - 1).then_inc(down_ready, 1)

            @block.scalar
            def _(act):
                for t in range(U + 1):
                    if t < U:
                        act.wait_ge(up1, t + 1)
                        if t >= R:
                            act.wait_ge(up2, t - R + 1)
                        act.activation(h1[:, t % R, :], M.ps[:, t % 2, :], ACT.Relu,
                                       bias=bias[:, 0, units[t][1]:units[t][1] + 1]).then_inc(relu1, 1)
                    if t:
                        u = t - 1
                        act.wait_ge(up2, u + 1)
                        if u >= R:
                            act.wait_ge(weighed_ready, u - R + 1)
                        act.activation(h2[:, u % R, :], M.ps[:, 2 + u % 2, :], ACT.Relu,
                                       bias=bias[:, 1, units[u][1]:units[u][1] + 1]).then_inc(relu2, 1)

            @block.vector
            def _(dve):
                for u, (c, e) in enumerate(units):
                    dve.wait_ge(relu2, u + 1)
                    dve.wait_ge(spread_ready, u + 1)
                    if u >= R:
                        dve.wait_ge(down_ready, u - R + 1)
                    dve.tensor_tensor(weighed[:, u % R, :], h2[:, u % R, :], M.ps[:, 4 + u % 2, :],
                                      ALU.mult).then_inc(weighed_ready, 1)
                    if e == E - 1:
                        dve.wait_ge(down_ready, u + 1)
                        dve.scalar_tensor_tensor(chunk(M.x, c), M.ps[:, 6 + c % 2, :],
                                                 M.mod[:, 2, 5, c // 2:c // 2 + 1], chunk(M.x, c),
                                                 ALU.mult, ALU.add).then_inc(added, 1)


L3_COLS = {}
_at = 0
for _name, _w in (("wq", P), ("wqr", P), ("wk", P), ("wkr", P), ("wv", P), ("bv", P), ("wo", NGRP * P),
                  ("bq", 1), ("bqr", 1), ("bk", 1), ("bkr", 1), ("bo", 1)):
    L3_COLS[_name] = (_at, _at + _w)
    _at += _w
L3_WIDTH = _at


def attn_l3(nc, M, D):
    with ExitStack() as ctx:
        W = ctx.enter_context(sbuf(nc, "l3_weights", [P, L3_WIDTH]))
        A = Attention(nc, D, ctx)
        with ExitStack() as tmp:
            xpos = tmp.enter_context(sbuf(nc, "xpos", [P, 4, T]))
            layer_norm(nc, M, M.x, M.h, lambda b: M.mod[:, 3, 1, b:b + 1], lambda b: M.mod[:, 3, 0, b:b + 1],
                       [(W[:], D["l3_weights"]), (xpos[:].rearrange("p k t -> p (k t)"), D["xpos"])] + A.loads)

            def tables(what, c):
                t = slice((c % 2) * CH, (c % 2 + 1) * CH)
                return xpos[:, 2 * what, t], xpos[:, 2 * what + 1, t]

            qkv(nc, M, A, W, L3_COLS, 1.0, tables)
        attention_core(nc, M, A, [D["no_bias"].rearrange("r (j t) -> r j t", j=GROUP)] * NGRP)
        a, b = L3_COLS["wo"]
        o = L3_COLS["bo"]
        attention_out(nc, M, A, W[:, a:b], W[:, o[0]:o[1]], M.x, lambda b: M.mod[:, 3, 2, b:b + 1])


L1_COLS = {}
_at = 0
for _name, _w in (("wq", P), ("wqr", P), ("wk", P), ("wkr", P), ("wv", P), ("bv", P), ("wo", P),
                  ("bq", 1), ("bqr", 1), ("bk", 1), ("bkr", 1), ("bo", 1),
                  ("freq", 1), ("bit0", 1), ("bit1", 1), ("bit2", 1), ("bit3", 1), ("turn", 1), ("sign", 1)):
    L1_COLS[_name] = (_at, _at + _w)
    _at += _w
L1_WIDTH = _at


def attn_l1(nc, M, D):
    H1, DH1 = 2, 64
    layer_norm(nc, M, M.x, M.h, lambda b: M.mod[:, 1, 1, b:b + 1], lambda b: M.mod[:, 1, 0, b:b + 1])
    PI = 3.1415925
    with ExitStack() as ctx:
        def sb(name, shape, dt=F32):
            return ctx.enter_context(sbuf(nc, name, shape, dt))
        W = sb("l1_weights", [P, L1_WIDTH])

        def col(name):
            a, b = L1_COLS[name]
            return W[:, a:b]

        cos = sb("cos", [P, T])
        sin = sb("sin", [P, T])
        kT = sb("k_T", [P, N])
        qz = [sb("q_T_head0", [P, N]), sb("q_T_head1", [P, N])]
        v = sb("v_and_ones", [P, NBLK, H1, P])
        onT = sb("o_normed_T", [P, N])
        ones = sb("ones", [96, P], BF16)
        mrow = sb("neg_max_rows", [96, B * H1, T], BF16)
        with ExitStack() as tmp:
            def tb(name, shape, dt=F32):
                return tmp.enter_context(sbuf(nc, name, shape, dt))
            f = tb("freq", [P, 16])
            pos = tb("positions", [P, T])
            ang = tb("angle", [P, T])
            half = tb("half_angle", [P, T])
            with phase(nc, "weights_in", "positions_made", "cleared", "base_ready", "log_ready", "root_ready",
                       "chain", "angles_ready", "half_ready", "sines_ready") as (
                    block, weights_in, positions_made, cleared, base_ready, log_ready, root_ready, chain,
                    angles_ready, half_ready, sines_ready):
                @block.sync
                def _(sp):
                    sp.dma_start(W[:], D["l1_weights"]).then_inc(weights_in, 16)
                    sp.wait_ge(weights_in, 16)

                @block.gpsimd
                def _(pool):
                    pool.iota(pos[:], pattern=[[1, T]], base=0, channel_multiplier=0,
                              allow_small_or_imprecise_dtypes=True).then_inc(positions_made, 1)
                    pool.wait_ge(positions_made, 1)
                    done = steps(pool, cleared)
                    done(pool.memset(qz[0][DH1:P, :], 0.0))
                    done(pool.memset(qz[1][0:DH1, :], 0.0))
                    done(pool.memset(v[:, :, :, DH1:P], 1.0))
                    done(pool.memset(ones[:], 1.0))
                    done(pool.memset(mrow[:], 0.0))

                @block.scalar
                def _(act):
                    act.wait_ge(weights_in, 16)
                    act.activation(f[:, 0:1], col("freq"), ACT.Sigmoid).then_inc(base_ready, 1)
                    act.wait_ge(base_ready, 2)
                    act.activation(f[:, 2:3], f[:, 1:2], ACT.Ln).then_inc(log_ready, 1)
                    act.wait_ge(log_ready, 1)
                    act.activation(f[:, 3:4], f[:, 2:3], ACT.Exp, scale=-1.0 / 16).then_inc(root_ready, 1)
                    act.wait_ge(angles_ready, 1)
                    act.activation(sin[:], ang[:], ACT.Sin).then_inc(sines_ready, 1)
                    act.wait_ge(half_ready, 1)
                    act.activation(cos[:], half[:], ACT.Sin).then_inc(sines_ready, 1)

                @block.vector
                def _(dve):
                    done = steps(dve, chain)

                    def c(k):
                        return f[:, k:k + 1]

                    dve.wait_ge(base_ready, 1)
                    dve.tensor_scalar(c(1), c(0), (10000.0 - 0.83 * 10000.0) * 2.0, 0.83 * 10000.0,
                                      ALU.mult, ALU.add).then_inc(base_ready, 1)
                    dve.wait_ge(root_ready, 1)
                    for a, b in ((3, 4), (4, 5), (5, 6), (6, 7)):
                        done(dve.tensor_tensor(c(b), c(a), c(a), ALU.mult))
                    done(dve.tensor_tensor(c(7), c(7), c(1), ALU.mult))
                    done(dve.tensor_scalar(c(7), c(7), -1.0 / 16, 17.0 / 16, ALU.mult, ALU.add))
                    done(dve.tensor_tensor(c(3), c(3), c(7), ALU.mult))
                    done(dve.tensor_copy(c(8), col("turn")))
                    for k in range(4):
                        done(dve.tensor_scalar(c(9), c(3), -1.0, None, ALU.add))
                        done(dve.tensor_scalar(c(9), c(9), col(f"bit{k}"), 1.0, ALU.mult, ALU.add))
                        done(dve.tensor_tensor(c(8), c(8), c(9), ALU.mult))
                        done(dve.tensor_tensor(c(3), c(3), c(3), ALU.mult))
                    dve.wait_ge(positions_made, 1)
                    done(dve.tensor_scalar(pos[:], pos[:], c(8), None, ALU.mult))
                    dve.tensor_scalar(ang[:], pos[:], -3.14159265, PI, ALU.add, ALU.min).then_inc(angles_ready, 1)
                    dve.tensor_scalar(half[:], pos[:], 0.5, PI, ALU.mult, ALU.min).then_inc(half_ready, 1)
                    dve.wait_ge(sines_ready, 1)
                    dve.tensor_scalar(sin[:], sin[:], col("sign"), None, ALU.mult)
                    dve.wait_ge(sines_ready, 2)
                    done(dve.tensor_tensor(cos[:], cos[:], cos[:], ALU.mult))
                    dve.tensor_scalar(cos[:], cos[:], -2.0, 1.0, ALU.mult, ALU.add)

        units = [(what, c) for c in range(NCH) for what in range(2)]
        with ExitStack() as tmp:
            plain = tmp.enter_context(sbuf(nc, "plain", [P, 2, CH]))
            turned = tmp.enter_context(sbuf(nc, "turned", [P, 2, CH]))
            with phase(nc, "proj_ready", "part_a", "part_b", "v_ready") as (block, proj_ready, part_a, part_b,
                                                                             v_ready):
                @block.tensor
                def _(pe):
                    for u, (what, c) in enumerate(units):
                        if u >= 2:
                            pe.wait_ge(part_b, u - 1)
                        for k, name in enumerate(("wq", "wqr") if what == 0 else ("wk", "wkr")):
                            mm = pe.matmul(M.ps[:, 2 * (u % 2) + k, :], col(name), chunk(M.h, c), start=True, stop=True)
                        mm.then_inc(proj_ready, 1)
                    for blk in range(NBLK):
                        mm = pe.matmul(M.ps[:, 4 + blk // 4, (blk % 4) * P:(blk % 4 + 1) * P],
                                       M.h[:, blk * P:(blk + 1) * P], col("wv"), start=True, stop=True)
                        if blk % 4 == 3:
                            mm.then_inc(v_ready, 1)

                @block.vector
                def _(dve):
                    for u, (what, c) in enumerate(units):
                        t = slice((c % 2) * CH, (c % 2 + 1) * CH)
                        dve.wait_ge(proj_ready, u + 1)
                        dve.scalar_tensor_tensor(plain[:, u % 2, :], M.ps[:, 2 * (u % 2), :],
                                                 col("bq" if what == 0 else "bk"), cos[:, t],
                                                 ALU.add, ALU.mult).then_inc(part_a, 1)
                        dve.scalar_tensor_tensor(turned[:, u % 2, :], M.ps[:, 2 * (u % 2) + 1, :],
                                                 col("bqr" if what == 0 else "bkr"), sin[:, t],
                                                 ALU.add, ALU.mult).then_inc(part_b, 1)
                        dve.wait_ge(part_a, u + 1)
                        dve.wait_ge(part_b, u + 1)
                        for dst, rows in (((qz[0], slice(0, DH1)), (qz[1], slice(DH1, P))) if what == 0
                                          else ((kT, slice(0, P)),)):
                            dve.tensor_tensor(dst[rows, c * CH:(c + 1) * CH], plain[rows, u % 2, :],
                                              turned[rows, u % 2, :], ALU.add)
                    bv = col("bv").rearrange("p (h d) -> p h d", h=H1)
                    for blk in range(NBLK):
                        dve.wait_ge(v_ready, blk // 4 + 1)
                        src = M.ps[:, 4 + blk // 4, (blk % 4) * P:(blk % 4 + 1) * P]
                        dve.tensor_tensor(v[:, blk, :, 0:DH1], src.rearrange("p (h d) -> p h d", h=H1), bv, ALU.add)

        pairs = [(b, h) for b in range(B) for h in range(H1)]
        with ExitStack() as tmp:
            mparts = tmp.enter_context(sbuf(nc, "max_parts", [P, len(pairs) * QB, 2]))
            rowmax = tmp.enter_context(sbuf(nc, "row_max", [P, len(pairs) * QB]))
            mfull = tmp.enter_context(sbuf(nc, "neg_max", [len(pairs) * QB, P]))
            mrest = tmp.enter_context(sbuf(nc, "neg_max_rest", [len(pairs) * QB, P]))
            m3 = tmp.enter_context(sbuf(nc, "neg_max_parts", [len(pairs) * QB, 3, P], BF16))
            pieces = [(n, i, half) for n in range(len(pairs)) for i in range(QB) for half in range(2)]
            with phase(nc, "s1_ready", "piece_max", "max_joined", "max_turned", "chain", "max_rows_in") as (
                    block, s1_ready, piece_max, max_joined, max_turned, chain, max_rows_in):
                @block.tensor
                def _(pe):
                    for u, (n, i, half) in enumerate(pieces):
                        b, h = pairs[n]
                        if u >= 4:
                            pe.wait_ge(piece_max, u - 3)
                        q0 = b * T + i * P
                        k0 = b * T + half * CH
                        pe.matmul(M.ps[:, u % 4, :], qz[h][:, q0:q0 + P], kT[:, k0:k0 + CH], start=True,
                                  stop=True).then_inc(s1_ready, 1)
                    pe.wait_ge(max_joined, 1)
                    pe.transpose(M.ps[0:len(pairs) * QB, 4, 0:P], rowmax[:], M.ident[:]).then_inc(max_turned, 1)

                @block.vector
                def _(dve):
                    done = steps(dve, chain)
                    for u, (n, i, half) in enumerate(pieces):
                        dve.wait_ge(s1_ready, u + 1)
                        dve.reduce_max(mparts[:, n * QB + i, half:half + 1], M.ps[:, u % 4, :],
                                       AX_X).then_inc(piece_max, 1)
                    dve.wait_ge(piece_max, len(pieces))
                    dve.tensor_reduce(rowmax[:], mparts[:], AX_X, ALU.max).then_inc(max_joined, 1)
                    dve.wait_ge(max_turned, 1)
                    done(dve.tensor_scalar(mfull[:], M.ps[0:len(pairs) * QB, 4, 0:P], -1.0, None, ALU.mult))
                    done(dve.tensor_copy(m3[:, 0, :], mfull[:]))
                    done(dve.tensor_tensor(mrest[:], mfull[:], m3[:, 0, :], ALU.subtract))
                    done(dve.tensor_copy(m3[:, 1, :], mrest[:]))
                    done(dve.tensor_tensor(m3[:, 2, :], mrest[:], m3[:, 1, :], ALU.subtract))

                @block.sync
                def _(sp):
                    sp.wait_ge(chain, 5)
                    for part in range(3):
                        sp.dma_start(mrow[part:part + 1, :, :].rearrange("o n (i q) -> o (n i) q", i=QB),
                                     m3[:, part, :]).then_inc(max_rows_in, 16)
                    sp.wait_ge(max_rows_in, 48)

        sets = [(n, half) for n in range(len(pairs)) for half in range(2)]
        units = [(s, kb) for s in range(len(sets)) for kb in range(QB)]
        with ExitStack() as tmp:
            prob = tmp.enter_context(sbuf(nc, "prob", [P, 3, CH]))
            rec = tmp.enter_context(sbuf(nc, "sum_recip", [DH1, 2, CH]))
            with phase(nc, "s2_ready", "exp_done", "pv_done", "recip_ready", "normed") as (
                    block, s2_ready, exp_done, pv_done, recip_ready, normed):
                @block.tensor
                def _(pe):
                    def weigh(u):
                        s, kb = units[u]
                        b, h = pairs[sets[s][0]]
                        pe.wait_ge(exp_done, u + 1)
                        if kb == 0 and s >= 2:
                            pe.wait_ge(normed, s - 1)
                        pe.matmul(M.ps[:, 4 + s % 2, :], v[:, b * QB + kb, h, :], prob[:, u % 3, :],
                                  start=kb == 0, stop=kb == QB - 1).then_inc(pv_done, 1)

                    for u, (s, kb) in enumerate(units):
                        n, half = sets[s]
                        b, h = pairs[n]
                        if u >= 4:
                            pe.wait_ge(exp_done, u - 3)
                        k0, q0 = b * T + kb * P, b * T + half * CH
                        pe.matmul(M.ps[:, u % 4, :], kT[:, k0:k0 + P], qz[h][:, q0:q0 + CH], start=True, stop=False)
                        pe.matmul(M.ps[:, u % 4, :], ones[:], mrow[:, n, half * CH:(half + 1) * CH], start=False,
                                  stop=True).then_inc(s2_ready, 1)
                        if u:
                            weigh(u - 1)
                    weigh(len(units) - 1)

                @block.scalar
                def _(act):
                    for u in range(len(units)):
                        act.wait_ge(s2_ready, u + 1)
                        if u >= 3:
                            act.wait_ge(pv_done, u - 2)
                        act.activation(prob[:, u % 3, :], M.ps[:, u % 4, :], ACT.Exp,
                                       scale=DH1 ** -0.5).then_inc(exp_done, 1)

                @block.vector
                def _(dve):
                    for s, (n, half) in enumerate(sets):
                        b, h = pairs[n]
                        q0 = b * T + half * CH
                        dve.wait_ge(pv_done, QB * (s + 1))
                        dve.reciprocal(rec[:, s % 2, :], M.ps[DH1:P, 4 + s % 2, :]).then_inc(recip_ready, 1)
                        dve.wait_ge(recip_ready, s + 1)
                        dve.tensor_tensor(onT[h * DH1:(h + 1) * DH1, q0:q0 + CH], M.ps[0:DH1, 4 + s % 2, :],
                                          rec[:, s % 2, :], ALU.mult).then_inc(normed, 1)

            upd = tmp.enter_context(sbuf(nc, "o_update", [P, NCH, CH]))
            with phase(nc, "out_ready", "scaled") as (block, out_ready, scaled):
                @block.tensor
                def _(pe):
                    for c in range(NCH):
                        pe.matmul(M.ps[:, c, :], col("wo"), chunk(onT, c), start=True, stop=True).then_inc(out_ready, 1)

                @block.vector
                def _(dve):
                    for c in range(NCH):
                        dve.wait_ge(out_ready, c + 1)
                        dve.tensor_scalar(upd[:, c, :], M.ps[:, c, :], col("bo"), M.mod[:, 1, 2, c // 2:c // 2 + 1],
                                          ALU.add, ALU.mult).then_inc(scaled, 1)

                @block.gpsimd
                def _(pool):
                    for c in range(NCH):
                        pool.wait_ge(scaled, c + 1)
                        pool.tensor_tensor(chunk(M.x, c), chunk(M.x, c), upd[:, c, :], ALU.add)


L2_COLS = {}
_at = 0
DI, NS, TAPS, RANK = 2, 16, 4, 8
for _name, _w in (("in", 2 * DI * P), ("xproj", DI * 96), ("dtproj", DI * P), ("out", DI * P),
                  ("conv_w", DI * TAPS), ("conv_b", DI), ("dt_b", DI), ("a_log", DI * NS), ("d", DI)):
    L2_COLS[_name] = (_at, _at + _w)
    _at += _w
L2_WIDTH = _at


def mamba(nc, M, D):
    seqs = [(d, b) for d in range(DI) for b in range(B)]
    PAD = TAPS - 1
    with ExitStack() as ctx:
        def sb(name, shape, dt=F32):
            return ctx.enter_context(sbuf(nc, name, shape, dt))
        W = sb("l2_weights", [P, L2_WIDTH])

        def col(name, k=0, w=None):
            a, b = L2_COLS[name]
            return W[:, a:b] if w is None else W[:, a + k * w:a + (k + 1) * w]

        u = sb("u", [P, DI, N])
        gate = sb("silu_z", [P, DI, N])
        delta = sb("delta", [P, DI, N])
        du = sb("delta_u", [P, DI, N])
        negA = sb("neg_a", [P, DI * NS])
        bparts = sb("b_parts", [96, N], BF16)
        cparts = sb("c_parts", [96, N], BF16)
        sel = sb("spread_rows", [96, 16, P], BF16)
        layer_norm(nc, M, M.x, M.h, lambda b: M.mod[:, 2, 1, b:b + 1], lambda b: M.mod[:, 2, 0, b:b + 1],
                   [(W[:], D["l2_weights"]), (sel[:].rearrange("r e p -> r (e p)"), D["spread"])])
        with ExitStack() as tmp:
            def tb(name, shape, dt=F32):
                return tmp.enter_context(sbuf(nc, name, shape, dt))
            xin = tb("x_in", [P, DI, B, T + PAD])
            conv = tb("conv", [P, DI, N])
            with phase(nc, "padded", "in_ready", "copied", "gated", "a_ready", "tap", "silu_done") as (
                    block, padded, in_ready, copied, gated, a_ready, tap, silu_done):
                units = [(k, c) for c in range(NCH) for k in range(2 * DI)]

                @block.gpsimd
                def _(pool):
                    pool.memset(xin[:, :, :, 0:PAD], 0.0).then_inc(padded, 1)
                    pool.memset(bparts[:], 0.0)
                    pool.memset(cparts[:], 0.0)

                @block.tensor
                def _(pe):
                    for i, (k, c) in enumerate(units):
                        if i >= 8:
                            pe.wait_ge(copied if k < DI else gated, DI * (c - 2) + k % DI + 1)
                        pe.matmul(M.ps[:, i % 8, :], col("in", k, P), chunk(M.h, c), start=True,
                                  stop=True).then_inc(in_ready, 1)

                @block.scalar
                def _(act):
                    for i, (k, c) in enumerate(units):
                        if k >= DI:
                            act.wait_ge(in_ready, i + 1)
                            act.activation(chunk(gate[:, k - DI, :], c), M.ps[:, i % 8, :], ACT.Silu).then_inc(gated, 1)
                    for s, (d, b) in enumerate(seqs):
                        act.wait_ge(tap, TAPS * (s + 1))
                        act.activation(u[:, d, b * T:(b + 1) * T], conv[:, d, b * T:(b + 1) * T], ACT.Silu,
                                       bias=col("conv_b", d, 1)).then_inc(silu_done, 1)
                    act.activation(negA[:], col("a_log"), ACT.Exp).then_inc(a_ready, 1)

                @block.vector
                def _(dve):
                    for i, (k, c) in enumerate(units):
                        if k < DI:
                            at = PAD + (c % 2) * CH
                            dve.wait_ge(in_ready, i + 1)
                            dve.tensor_copy(xin[:, k, c // 2, at:at + CH], M.ps[:, i % 8, :]).then_inc(copied, 1)
                    dve.wait_ge(copied, DI * NCH)
                    dve.wait_ge(padded, 1)
                    for s, (d, b) in enumerate(seqs):
                        out = conv[:, d, b * T:(b + 1) * T]
                        for k in range(TAPS):
                            wk = W[:, L2_COLS["conv_w"][0] + d * TAPS + k:L2_COLS["conv_w"][0] + d * TAPS + k + 1]
                            if k == 0:
                                dve.tensor_scalar(out, xin[:, d, b, 0:T], wk, None, ALU.mult).then_inc(tap, 1)
                            else:
                                dve.wait_ge(tap, TAPS * s + k)
                                dve.scalar_tensor_tensor(out, xin[:, d, b, k:k + T], wk, out, ALU.mult,
                                                         ALU.add).then_inc(tap, 1)
                    dve.wait_ge(a_ready, 1)
                    dve.tensor_scalar(negA[:], negA[:], -1.0, None, ALU.mult)

        with ExitStack() as tmp:
            def tb(name, shape, dt=F32):
                return tmp.enter_context(sbuf(nc, name, shape, dt))
            dbl = tb("x_dbl", [96, N])
            rest = tb("bc_rest", [NS, 2, CH])
            mid = tb("bc_mid", [NS, 2, CH], BF16)
            pre = tb("step_pre", [P, DI, N])
            ex = tb("step_exp", [P, DI, N])
            one = tb("step_one_plus", [P, DI, N])
            ln = tb("step_log", [P, DI, N])
            slope = du
            with phase(nc, "dbl_ready", "dbl_copied", "step_ready", "chain", "biased", "abs_done", "exp_done", "plus",
                       "slope_ready", "log_done", "delta_ready") as (
                    block, dbl_ready, dbl_copied, step_ready, chain, biased, abs_done, exp_done, plus, slope_ready,
                    log_done, delta_ready):
                @block.tensor
                def _(pe):
                    for c in range(NCH):
                        for d in range(DI):
                            mm = pe.matmul(M.ps[0:96, c, :], col("xproj", d, 96), chunk(u[:, d, :], c), start=d == 0,
                                           stop=d == DI - 1)
                        mm.then_inc(dbl_ready, 1)
                    for c in range(NCH):
                        pe.wait_ge(dbl_copied, c + 1)
                        for d in range(DI):
                            i = c * DI + d
                            if i >= 4:
                                pe.wait_ge(biased, i - 3)
                            pe.matmul(M.ps[:, 4 + i % 4, :], W[0:96, L2_COLS["dtproj"][0] + d * P:
                                                               L2_COLS["dtproj"][0] + (d + 1) * P],
                                      chunk(dbl, c), start=True, stop=True).then_inc(step_ready, 1)

                @block.scalar
                def _(act):
                    for c in range(NCH):
                        act.wait_ge(dbl_ready, c + 1)
                        act.activation(chunk(dbl, c), M.ps[0:96, c, :], ACT.Copy).then_inc(dbl_copied, 1)
                    for i in range(NCH * DI):
                        c, d = divmod(i, DI)
                        act.wait_ge(step_ready, i + 1)
                        act.activation(chunk(pre[:, d, :], c), M.ps[:, 4 + i % 4, :], ACT.Identity,
                                       bias=col("dt_b", d, 1)).then_inc(biased, 1)
                    act.wait_ge(biased, NCH * DI)
                    for d in range(DI):
                        act.activation(ex[:, d, :], pre[:, d, :], ACT.Abs).then_inc(abs_done, 1)
                    for d in range(DI):
                        act.wait_ge(abs_done, d + 1)
                        act.activation(ex[:, d, :], ex[:, d, :], ACT.Exp, scale=-1.0).then_inc(exp_done, 1)
                    for d in range(DI):
                        act.wait_ge(plus, d + 1)
                        act.activation(ln[:, d, :], one[:, d, :], ACT.Ln).then_inc(log_done, 1)

                @block.gpsimd
                def _(pool):
                    for d in range(DI):
                        pool.wait_ge(exp_done, d + 1)
                        pool.tensor_scalar(one[:, d, :], ex[:, d, :], 1.0, None, ALU.add).then_inc(plus, 1)
                    for d in range(DI):
                        pool.tensor_scalar(slope[:, d, :], ex[:, d, :], 0.5, -1.0, ALU.mult, ALU.add
                                           ).then_inc(slope_ready, 1)
                    for d in range(DI):
                        pool.wait_ge(delta_ready, d + 1)
                        pool.tensor_tensor(du[:, d, :], delta[:, d, :], u[:, d, :], ALU.mult)

                @block.vector
                def _(dve):
                    done = steps(dve, chain)
                    for c in range(NCH):
                        dve.wait_ge(dbl_copied, c + 1)
                        for k, (parts, row) in enumerate(((bparts, 32), (cparts, 64))):
                            src = dbl[row:row + NS, c * CH:(c + 1) * CH]
                            done(dve.tensor_copy(chunk(parts, c)[0:NS], src))
                            done(dve.tensor_copy(rest[:, k, :], src))
                            done(dve.tensor_tensor(rest[:, k, :], rest[:, k, :], chunk(parts, c)[0:NS], ALU.subtract))
                            done(dve.tensor_copy(mid[:, k, :], rest[:, k, :]))
                            done(dve.tensor_copy(chunk(parts, c)[32:32 + NS], mid[:, k, :]))
                            done(dve.tensor_tensor(chunk(parts, c)[64:64 + NS], rest[:, k, :], mid[:, k, :],
                                                   ALU.subtract))
                    for d in range(DI):
                        dve.wait_ge(log_done, d + 1)
                        t, e, l = one[:, d, :], ex[:, d, :], ln[:, d, :]
                        done(dve.scalar_tensor_tensor(t, t, -1.0, e, ALU.add, ALU.subtract))
                        dve.wait_ge(slope_ready, d + 1)
                        done(dve.tensor_tensor(t, t, slope[:, d, :], ALU.mult))
                        done(dve.tensor_tensor(t, t, l, ALU.add))
                        dve.scalar_tensor_tensor(delta[:, d, :], pre[:, d, :], 0.0, t, ALU.max,
                                                 ALU.add).then_inc(delta_ready, 1)

        y = sb("y", [P, DI, N])
        with ExitStack() as tmp:
            def tb(name, shape, dt=F32):
                return tmp.enter_context(sbuf(nc, name, shape, dt))
            R = 4
            dA = tb("decay", [P, R, T])
            dBu = tb("inflow", [P, R, T])
            st = tb("states", [P, R, T])
            hc = tb("read_out", [P, R, T])
            bsb = tb("b_spread", [P, 3, T])
            groups = [(b, n) for b in range(B) for n in range(NS)]
            with phase(nc, "b_ready", "b_copied", "c_ready", "decay_ready", "inflow_ready", "scanned", "read",
                       "summed", "y_saved") as (
                    block, b_ready, b_copied, c_ready, decay_ready, inflow_ready, scanned, read, summed, y_saved):
                @block.tensor
                def _(pe):
                    def gather(i):
                        b, n = groups[i // DI]
                        d = i % DI
                        pe.wait_ge(read, i + 1)
                        if n == 0 and b:
                            pe.wait_ge(y_saved, DI * (b - 1) + d + 1)
                        for half in range(2):
                            mm = pe.matmul(M.ps[:, 4 + 2 * d + half, :], M.ident[:],
                                           hc[:, i % R, half * CH:(half + 1) * CH], start=n == 0, stop=n == NS - 1)
                        mm.then_inc(summed, 1)

                    def spread_b(g):
                        b, n = groups[g]
                        if g:
                            pe.wait_ge(b_copied, g)
                        for half in range(2):
                            mm = pe.matmul(M.ps[:, half, :], sel[:, n, :], chunk(bparts, 2 * b + half),
                                           start=True, stop=True)
                        mm.then_inc(b_ready, 1)

                    spread_b(0)
                    for g, (b, n) in enumerate(groups):
                        if g + 1 < len(groups):
                            spread_b(g + 1)
                        if g:
                            pe.wait_ge(read, DI * g)
                        for half in range(2):
                            mm = pe.matmul(M.ps[:, 2 + half, :], sel[:, n, :], chunk(cparts, 2 * b + half),
                                           start=True, stop=True)
                        mm.then_inc(c_ready, 1)
                        if g:
                            for d in range(DI):
                                gather(DI * (g - 1) + d)
                    for d in range(DI):
                        gather(DI * (len(groups) - 1) + d)

                @block.scalar
                def _(act):
                    for g, (b, n) in enumerate(groups):
                        act.wait_ge(b_ready, g + 1)
                        if g >= 3:
                            act.wait_ge(inflow_ready, DI * (g - 2))
                        act.activation(bsb[:, g % 3, :], M.ps[:, 0:2, :].rearrange("p a t -> p (a t)"),
                                       ACT.Copy).then_inc(b_copied, 1)
                        for d in range(DI):
                            i = DI * g + d
                            if i >= R:
                                act.wait_ge(scanned, i - R + 1)
                            act.activation(dA[:, i % R, :], delta[:, d, b * T:(b + 1) * T], ACT.Exp,
                                           scale=negA[:, d * NS + n:d * NS + n + 1]).then_inc(decay_ready, 1)

                @block.gpsimd
                def _(pool):
                    for g, (b, n) in enumerate(groups):
                        pool.wait_ge(b_copied, g + 1)
                        for d in range(DI):
                            i = DI * g + d
                            if i >= R:
                                pool.wait_ge(scanned, i - R + 1)
                            pool.tensor_tensor(dBu[:, i % R, :], du[:, d, b * T:(b + 1) * T], bsb[:, g % 3, :],
                                               ALU.mult).then_inc(inflow_ready, 1)

                @block.vector
                def _(dve):
                    def scan(i):
                        dve.wait_ge(decay_ready, i + 1)
                        dve.wait_ge(inflow_ready, i + 1)
                        if i >= R:
                            dve.wait_ge(read, i - R + 1)
                        dve.tensor_tensor_scan(st[:, i % R, :], dA[:, i % R, :], dBu[:, i % R, :], 0.0, ALU.mult,
                                               ALU.add).then_inc(scanned, 1)

                    def read_out(i):
                        dve.wait_ge(scanned, i + 1)
                        dve.wait_ge(c_ready, i // DI + 1)
                        if i >= R:
                            dve.wait_ge(summed, i - R + 1)
                        dve.tensor_tensor(hc[:, i % R, :], st[:, i % R, :],
                                          M.ps[:, 2:4, :].rearrange("p a t -> p (a t)"), ALU.mult).then_inc(read, 1)

                    def save(b):
                        t = slice(b * T, (b + 1) * T)
                        for d in range(DI):
                            dve.wait_ge(summed, DI * (NS * (b + 1) - 1) + d + 1)
                            dve.scalar_tensor_tensor(y[:, d, t], u[:, d, t], col("d", d, 1),
                                                     M.ps[:, 4 + 2 * d:6 + 2 * d, :].rearrange("p a t -> p (a t)"),
                                                     ALU.mult, ALU.add).then_inc(y_saved, 1)

                    scan(0)
                    for i in range(DI * len(groups)):
                        if i + 1 < DI * len(groups):
                            scan(i + 1)
                        read_out(i)
                        if i > 1 and i % (DI * NS) == 1:
                            save(i // (DI * NS) - 1)
                    save(B - 1)

        with phase(nc, "gated", "out_ready", "added") as (block, gated, out_ready, added):
            @block.gpsimd
            def _(pool):
                for c in range(NCH):
                    for d in range(DI):
                        pool.tensor_tensor(chunk(y[:, d, :], c), chunk(y[:, d, :], c), chunk(gate[:, d, :], c),
                                           ALU.mult).then_inc(gated, 1)

            @block.tensor
            def _(pe):
                for c in range(NCH):
                    for d in range(DI):
                        pe.wait_ge(gated, DI * c + d + 1)
                        mm = pe.matmul(M.ps[:, c, :], col("out", d, P), chunk(y[:, d, :], c), start=d == 0,
                                       stop=d == DI - 1)
                    mm.then_inc(out_ready, 1)

            @block.vector
            def _(dve):
                for c in range(NCH):
                    dve.wait_ge(out_ready, c + 1)
                    dve.scalar_tensor_tensor(chunk(M.x, c), M.ps[:, c, :], M.mod[:, 2, 2, c // 2:c // 2 + 1],
                                             chunk(M.x, c), ALU.mult, ALU.add)


class ExpertsL3:
    E, F = 16, 2

    def __init__(self, nc, ctx, D):
        self.up = ctx.enter_context(sbuf(nc, "l3_gate_and_value", [P, 2, self.E, self.F, P]))
        self.down = ctx.enter_context(sbuf(nc, "l3_down", [P, self.E, self.F, P]))
        self.loads = [(self.up[:].rearrange("p k e f d -> p (k e f d)"), D["l3_up"]),
                      (self.down[:].rearrange("p e f d -> p (e f d)"), D["l3_down"])]


def moe_l3(nc, M, D, X=None):
    E, F, CAP = 16, 2, 32
    ROWS = 64
    SEL = E * CAP
    EG = P // CAP
    layer_norm(nc, M, M.x, M.h, lambda b: M.mod[:, 3, 4, b:b + 1], lambda b: M.mod[:, 3, 3, b:b + 1])
    with ExitStack() as ctx:
        def sb(name, shape, dt=F32):
            return ctx.enter_context(sbuf(nc, name, shape, dt))
        loads = []
        if X is None:
            X = ExpertsL3(nc, ctx, D)
            loads = X.loads
        idxb = sb("chosen_at", [P, B, SEL])
        wb = sb("chosen_weight", [P, B, SEL])
        icol = sb("chosen_at_col", [P, B * E // EG])
        xtok = sb("h_by_token", [P, NBLK, P])
        tokid = sb("token_ids", [P, QB])
        pos = sb("positions", [P, T])
        ysel = sb("chosen_out", [P, B, SEL])
        with ExitStack() as tmp:
            def tb(name, shape, dt=F32):
                return tmp.enter_context(sbuf(nc, name, shape, dt))
            router = tb("router", [P, P + 32])
            r1 = tb("router_hidden", [P, N])
            pr = tb("probs", [ROWS, T])
            work = tb("probs_left", [ROWS, T])
            stat = tb("row_stat", [ROWS, 4])
            top = tb("top32", [ROWS, CAP])
            idx = tb("top32_at", [ROWS, CAP], U32)
            idxf = tb("top32_at_f", [ROWS, CAP])
            diag = tb("diagonal", [ROWS, 2, B, SEL])
            ones = tb("ones", [ROWS, P])
            with phase(nc, "loaded", "made", "r1_ready", "r1_done", "logits_ready", "max_ready", "exped", "chain",
                       "diag_ready", "spread_ready", "spread_done", "cols_ready", "turned", "turned_copied") as (
                    block, loaded, made, r1_ready, r1_done, logits_ready, max_ready, exped, chain, diag_ready,
                    spread_ready, spread_done, cols_ready, turned, turned_copied):
                @block.sync
                def _(sp):
                    sp.dma_start(router[:], D["l3_router"]).then_inc(loaded, 16)
                    for dst, src in loads:
                        sp.dma_start(dst, src).then_inc(loaded, 16)
                    sp.wait_ge(loaded, 16 * (1 + len(loads)))

                @block.gpsimd
                def _(pool):
                    pool.iota(tokid[:], pattern=[[P, QB]], base=0, channel_multiplier=1,
                              allow_small_or_imprecise_dtypes=True)
                    pool.iota(pos[:], pattern=[[1, T]], base=0, channel_multiplier=0,
                              allow_small_or_imprecise_dtypes=True)
                    pool.memset(ones[:], 1.0).then_inc(made, 1)

                @block.tensor
                def _(pe):
                    pe.wait_ge(loaded, 16 * (1 + len(loads)))
                    for c in range(NCH):
                        pe.matmul(M.ps[:, c, :], router[:, 0:P], chunk(M.h, c), start=True, stop=True).then_inc(r1_ready, 1)
                    for c in range(NCH):
                        b = c // 2
                        pe.wait_ge(r1_done, c + 1)
                        mm = pe.matmul(M.ps[32 * b:32 * b + 32, 4 + c % 2, :], router[:, P:P + 32], chunk(r1, c),
                                       start=True, stop=True)
                    mm.then_inc(logits_ready, 1)
                    for blk in range(NBLK):
                        mm = pe.transpose(M.ps[:, blk // 4, (blk % 4) * P:(blk % 4 + 1) * P],
                                          M.h[:, blk * P:(blk + 1) * P], M.ident[:])
                        if blk % 4 == 3:
                            mm.then_inc(turned, 1)
                    pe.wait_ge(made, 1)
                    for k in range(2):
                        pe.wait_ge(diag_ready, k + 1)
                        for b in range(B):
                            mm = pe.matmul(M.ps[:, 6 + b, :] if k == 0 else M.ps[:, 4 + b, :], ones[:],
                                           diag[:, k, b, :], start=True, stop=True)
                        mm.then_inc(spread_ready, 1)
                    pe.wait_ge(spread_done, 1)
                    pe.wait_ge(turned_copied, NBLK // 4)
                    for k in range(B * E // EG):
                        b, g = divmod(k, E // EG)
                        mm = pe.matmul(M.ps[:, 0, k:k + 1], idxb[:, b, g * P:(g + 1) * P], M.ident[:, 0:1],
                                       start=True, stop=True)
                    mm.then_inc(cols_ready, 1)

                @block.scalar
                def _(act):
                    for c in range(NCH):
                        act.wait_ge(r1_ready, c + 1)
                        act.activation(chunk(r1, c), M.ps[:, c, :], ACT.Silu).then_inc(r1_done, 1)
                    for k in range(NBLK // 4):
                        act.wait_ge(turned, k + 1)
                        act.activation(xtok[:, 4 * k:4 * k + 4, :].rearrange("p n d -> p (n d)"), M.ps[:, k, :],
                                       ACT.Copy).then_inc(turned_copied, 1)
                    act.wait_ge(max_ready, 1)
                    act.activation(pr[:], M.ps[0:ROWS, 4:6, :].rearrange("p a t -> p (a t)"), ACT.Exp,
                                   bias=stat[:, 0:1]).then_inc(exped, 1)

                @block.vector
                def _(dve):
                    done = steps(dve, chain)
                    logits = M.ps[0:ROWS, 4:6, :].rearrange("p a t -> p (a t)")
                    dve.wait_ge(logits_ready, 1)
                    done(dve.reduce_max(stat[:, 1:2], logits, AX_X))
                    dve.tensor_scalar(stat[:, 0:1], stat[:, 1:2], -1.0, None, ALU.mult).then_inc(max_ready, 1)
                    dve.wait_ge(exped, 1)
                    done(dve.reduce_sum(stat[:, 2:3], pr[:], AX_X))
                    done(dve.reciprocal(stat[:, 2:3], stat[:, 2:3]))
                    done(dve.tensor_scalar(pr[:], pr[:], stat[:, 2:3], None, ALU.mult))
                    left = pr
                    for r in range(CAP // 8):
                        part = slice(8 * r, 8 * r + 8)
                        done(dve.max(top[:, part], left[:]))
                        done(dve.max_index(idx[:, part], top[:, part], left[:]))
                        if r < CAP // 8 - 1:
                            done(dve.match_replace(work[:], top[:, part], left[:], -1.0))
                            left = work
                    done(dve.tensor_copy(idxf[:], idx[:]))
                    done(dve.reduce_sum(stat[:, 3:4], top[:], AX_X))
                    done(dve.tensor_scalar(stat[:, 3:4], stat[:, 3:4], 1e-9, None, ALU.add))
                    done(dve.reciprocal(stat[:, 3:4], stat[:, 3:4]))
                    done(dve.tensor_scalar(top[:], top[:], stat[:, 3:4], None, ALU.mult))
                    for k, vals in enumerate((idxf, top)):
                        for b in range(B):
                            ins = dve.tensor_tensor(
                                diag[:, k, b, :].rearrange("p (e s) -> p e s", s=CAP),
                                vals[:].unsqueeze(1).to_broadcast([ROWS, E, CAP]),
                                wide(M.ident[0:ROWS, 32 * b:32 * b + E], CAP), ALU.mult)
                        ins.then_inc(diag_ready, 1)
                    for k, dst in enumerate((idxb, wb)):
                        dve.wait_ge(spread_ready, k + 1)
                        src = M.ps[:, 6:8, :] if k == 0 else M.ps[:, 4:6, :]
                        dve.tensor_copy(dst[:], src).then_inc(spread_done, 1)
                    dve.wait_ge(cols_ready, 1)
                    dve.tensor_copy(icol[:], M.ps[:, 0, 0:B * E // EG])

        with ExitStack() as tmp:
            def tb(name, shape, dt=F32):
                return tmp.enter_context(sbuf(nc, name, shape, dt))
            hot = tb("one_hot", [P, 4, SEL])
            xsel = tb("chosen_in", [P, B, E, CAP])
            silu = tb("silu_gate", [P, 2, CH])
            hid = tb("hidden", [P, 2, CH])
            NT = B * CAP
            GE = CH // (F * NT)
            with phase(nc, "hot_ready", "gathered", "xsel_ready", "gate_ready", "value_ready", "silu_ready",
                       "hidden_ready", "down_ready", "weighed") as (
                    block, hot_ready, gathered, xsel_ready, gate_ready, value_ready, silu_ready, hidden_ready,
                    down_ready, weighed):
                @block.tensor
                def _(pe):
                    for k in range(NBLK):
                        b, blk = divmod(k, QB)
                        pe.wait_ge(hot_ready, k + 1)
                        pe.matmul(M.ps[:, b, :], xtok[:, k, :], hot[:, k % 4, :], start=blk == 0,
                                  stop=blk == QB - 1).then_inc(gathered, 1)
                    pe.wait_ge(xsel_ready, B)

                    def down(g):
                        pe.wait_ge(hidden_ready, g + 1)
                        if g >= 2:
                            pe.wait_ge(weighed, B * (g - 1))
                        for k in range(GE):
                            for f in range(F):
                                at = (k * F + f) * NT
                                mm = pe.matmul(M.ps[:, 6 + g % 2, k * NT:(k + 1) * NT], X.down[:, g * GE + k, f, :],
                                               hid[:, g % 2, at:at + NT], start=f == 0, stop=f == F - 1)
                        mm.then_inc(down_ready, 1)

                    for g in range(E // GE):
                        for which, ready in ((0, gate_ready), (1, value_ready)):
                            if g >= 2:
                                pe.wait_ge(silu_ready if which == 0 else hidden_ready, g - 1)
                            for k in range(GE):
                                for f in range(F):
                                    at = (k * F + f) * NT
                                    mm = pe.matmul(M.ps[:, 2 + 2 * which + g % 2, at:at + NT],
                                                   X.up[:, which, g * GE + k, f, :], xsel[:, :, g * GE + k, :],
                                                   start=True, stop=True)
                            mm.then_inc(ready, 1)
                        if g:
                            down(g - 1)
                    down(E // GE - 1)

                @block.scalar
                def _(act):
                    for b in range(B):
                        act.wait_ge(gathered, QB * (b + 1))
                        act.activation(xsel[:, b].rearrange("p e s -> p (e s)"), M.ps[:, b, :],
                                       ACT.Copy).then_inc(xsel_ready, 1)
                    for g in range(E // GE):
                        act.wait_ge(gate_ready, g + 1)
                        if g >= 2:
                            act.wait_ge(hidden_ready, g - 1)
                        act.activation(silu[:, g % 2, :], M.ps[:, 2 + g % 2, :], ACT.Silu).then_inc(silu_ready, 1)

                @block.vector
                def _(dve):
                    for k in range(NBLK):
                        b, blk = divmod(k, QB)
                        if k >= 4:
                            dve.wait_ge(gathered, k - 3)
                        dve.tensor_scalar(hot[:, k % 4, :], idxb[:, b, :], tokid[:, blk:blk + 1], None,
                                          ALU.is_equal).then_inc(hot_ready, 1)
                    for g in range(E // GE):
                        dve.wait_ge(silu_ready, g + 1)
                        dve.wait_ge(value_ready, g + 1)
                        if g >= 2:
                            dve.wait_ge(down_ready, g - 1)
                        dve.tensor_tensor(hid[:, g % 2, :], silu[:, g % 2, :], M.ps[:, 4 + g % 2, :],
                                          ALU.mult).then_inc(hidden_ready, 1)
                        dve.wait_ge(down_ready, g + 1)
                        for b in range(B):
                            es = slice(g * GE * CAP, (g + 1) * GE * CAP)
                            src = M.ps[:, 6 + g % 2, 0:GE * NT].rearrange("p (e b s) -> p b e s", b=B, s=CAP)[:, b]
                            dve.tensor_tensor(ysel[:, b, es].rearrange("p (e s) -> p e s", s=CAP), src,
                                              wb[:, b, es].rearrange("p (e s) -> p e s", s=CAP),
                                              ALU.mult).then_inc(weighed, 1)

        with ExitStack() as tmp:
            def tb(name, shape, dt=F32):
                return tmp.enter_context(sbuf(nc, name, shape, dt))
            K = E // EG
            hot = tb("one_hot_rows", [P, B * K, T])
            yT = tb("chosen_out_rows", [P, B * K, P])
            with phase(nc, "hot_ready", "turned", "turned_copied", "scattered", "added") as (
                    block, hot_ready, turned, turned_copied, scattered, added):
                @block.tensor
                def _(pe):
                    for k in range(B * K):
                        b, g = divmod(k, K)
                        pe.transpose(M.ps[:, b, g * P:(g + 1) * P], ysel[:, b, g * P:(g + 1) * P],
                                     M.ident[:]).then_inc(turned, 1)
                    for c in range(NCH):
                        b, half = divmod(c, 2)
                        pe.wait_ge(turned_copied, b + 1)
                        for g in range(K):
                            pe.wait_ge(hot_ready, b * K + g + 1)
                            mm = pe.matmul(M.ps[:, 4 + c, :], yT[:, b * K + g, :],
                                           hot[:, b * K + g, half * CH:(half + 1) * CH], start=g == 0, stop=g == K - 1)
                        mm.then_inc(scattered, 1)

                @block.scalar
                def _(act):
                    for b in range(B):
                        act.wait_ge(turned, K * (b + 1))
                        act.activation(yT[:, b * K:(b + 1) * K, :].rearrange("p k d -> p (k d)"), M.ps[:, b, :],
                                       ACT.Copy).then_inc(turned_copied, 1)

                @block.vector
                def _(dve):
                    for k in range(B * K):
                        dve.tensor_scalar(hot[:, k, :], pos[:], icol[:, k:k + 1], None,
                                          ALU.is_equal).then_inc(hot_ready, 1)
                    for c in range(NCH):
                        dve.wait_ge(scattered, c + 1)
                        dve.scalar_tensor_tensor(chunk(M.x, c), M.ps[:, 4 + c, :], M.mod[:, 3, 5, c // 2:c // 2 + 1],
                                                 chunk(M.x, c), ALU.mult, ALU.add)



def program(nc, D, out, start=0, stop=8):
    stages = [transformer, moe_l0, attn_l1, moe_l1, mamba, moe_l2, attn_l3, moe_l3]
    _used.clear()
    with ExitStack() as ctx:
        M = Memory()
        for name in ("q_parts", "k_parts"):
            D = {**D, name: nc.dram_tensor(name, (NGRP, 3 * DH * GROUP, N), BF16, kind="Internal").ap()}
        setup(nc, M, D, ctx)
        for stage in stages[start:stop]:
            stage(nc, M, D)
        store(nc, M, out)


def constants():
    import math
    bf = np.dtype("bfloat16")
    pos = np.arange(T)
    k_aux = np.zeros((9, T), np.float32)
    k_aux[0:3] = (pos // P) * P
    k_aux[3:6] = pos % P
    k_aux[6:9] = 1.0
    base = 2.0 ** (-2.0 ** (-(math.log2(HEADS) - 3)))
    slopes = (base ** np.arange(1, HEADS + 1)).astype(np.float32)
    hi = slopes.astype(bf)
    r = slopes - hi.astype(np.float32)
    mid = r.astype(bf)
    lo = (r - mid.astype(np.float32)).astype(bf)
    alibi = np.zeros((NGRP, 6, GROUP, T), np.float32)
    for i, part in enumerate((hi, mid, lo)):
        v = part.astype(np.float32).reshape(NGRP, GROUP)[:, :, None]
        alibi[:, i] = v
        alibi[:, 3 + i] = v
    pick = np.zeros((P, NGRP, 32), np.float32)
    unpick = np.zeros((P, NCH, NGRP, P), np.float32)
    for g in range(NGRP):
        for j in range(GROUP):
            pick[32 * j + DH, g, [GROUP * g + j, 16 + GROUP * g + j]] = 1.0
            for c in range(NCH):
                unpick[32 * c + GROUP * g + j, c, g, 32 * j:32 * j + 32] = 1.0
    spread_rows = np.zeros((96, 16, P), np.float32)
    for e in range(16):
        spread_rows[[e, 32 + e, 64 + e], e] = 1.0
    t = np.arange(T, dtype=np.float32)
    even = np.arange(0, DH, 2, dtype=np.float32)
    inv = (np.float32(1.0) / np.float32(10000.0) ** (even / np.float32(DH))).astype(np.float32)
    ang = np.repeat(t[:, None] * inv[None, :], 2, axis=-1).astype(np.float32)
    sbase = ((even + np.float32(0.4 * DH)) / np.float32(1.4 * DH)).astype(np.float32)
    power = ((t - T // 2) / np.float32(512.0)).astype(np.float32)
    sc = sbase[None, :].astype(np.float64) ** power[:, None].astype(np.float64)
    sc = np.concatenate((sc, sc), axis=-1)
    sign = np.tile([-1.0, 1.0], DH // 2)
    cos, sin = np.cos(ang.astype(np.float64)), np.sin(ang.astype(np.float64)) * sign
    qs = 1.0 / math.sqrt(DH * HEADS)
    tab = np.stack([cos * sc * qs, sin * sc * qs, cos / sc, sin / sc], 0)
    rows = np.tile(np.repeat(np.arange(DH), GROUP), NGRP)
    xpos = tab.transpose(2, 0, 1)[rows].astype(np.float32)
    return {"spread": spread_rows.reshape(96, -1).astype(bf), "xpos": xpos.reshape(P, -1),
            "no_bias": np.zeros((6, GROUP * T), bf), "k_aux": np.tile(k_aux, (1, GROUP)).astype(bf), "alibi": alibi.reshape(NGRP * 6, GROUP * T).astype(bf),
            "pick_sums": pick.reshape(P, -1), "unpick_sums": unpick.reshape(P, -1)}


def wo_groups(w):
    wt = np.asarray(w)
    out = np.zeros((P, NGRP, P), np.float32)
    for h in range(HEADS):
        g, j = divmod(h, GROUP)
        out[32 * j:32 * j + DH, g] = wt[DH * h:DH * h + DH]
    return out.reshape(P, NGRP * P)


def layout(i):
    i = {k: np.asarray(v) for k, v in i.items()}
    a = constants()
    a["x_T"] = np.ascontiguousarray(i["L0_attn_x"].reshape(N, P).T)
    a["c_T"] = np.stack([i[f"L{l}_c"].T for l in range(4)], 1).reshape(P, 4 * B)
    a["wmod"] = np.concatenate([i[f"L{l}_wmod"] for l in range(4)], 1)
    perm = np.arange(P).reshape(NGRP, GROUP, DH).transpose(0, 2, 1).reshape(P)
    layers = []
    for l in range(4):
        w, b = i["L0_attn_in_proj_w"][l], i["L0_attn_in_proj_b"][l]
        v = lambda n: i["L0_attn_" + n][l][:, None]
        layers.append(np.concatenate([
            w[0:P][perm].T, w[P:2 * P][perm].T, w[2 * P:].T, np.broadcast_to(b[2 * P:], (P, P)),
            wo_groups(i["L0_attn_out_proj_w"][l].T), i["L0_attn_ffn1_w"][l].T,
            i["L0_attn_ffn2_w"][l].T.reshape(4, P, P).transpose(1, 0, 2).reshape(P, 4 * P),
            b[0:P][perm, None], b[P:2 * P][perm, None], v("out_proj_b"), i["L0_attn_ffn1_b"][l].reshape(4, P).T,
            v("ffn2_b"), v("ln1_w"), v("ln1_b"), v("ln2_w"), v("ln2_b")], 1))
    a["l0_weights"] = np.concatenate(layers, 0)
    a["l0_final"] = np.stack([i["L0_attn_final_w"], i["L0_attn_final_b"]], 1)
    a["l0_experts"] = i["L0_ffn_expert_w"].transpose(2, 0, 1).reshape(P, -1)
    a["l0_small"] = np.concatenate([i["L0_ffn_gate_w"].T, i["L0_ffn_expert_b"].T], 1)
    a["l1_up"] = i["L1_ffn_ew1"].transpose(1, 0, 2).reshape(P, -1)
    a["l1_down"] = i["L1_ffn_ew2"].transpose(1, 0, 2).reshape(P, -1)
    a["l1_shared"] = np.concatenate([i["L1_ffn_sw1"], i["L1_ffn_sw3"],
                                     i["L1_ffn_sw2"].reshape(2, P, P).transpose(1, 0, 2).reshape(P, -1)], 1)
    a["l1_small"] = np.concatenate([i["L1_ffn_router_w"].T, np.broadcast_to(i["L1_ffn_router_bias"], (P, 8))], 1)
    a["l2_experts"] = np.concatenate([i[f"L2_ffn_w{k}"].transpose(1, 0, 2).reshape(P, -1) for k in (1, 2, 3)], 1)
    a["l2_bias"] = np.concatenate([i["L2_ffn_b1"].T, i["L2_ffn_b2"].T], 1)
    b3 = np.zeros((P, P), np.float32)
    b3[0:8] = i["L2_ffn_b3"]
    a["l2_b3"] = b3
    a["l2_small"] = np.concatenate([i["L2_ffn_gate_w"].T, np.broadcast_to(i["L2_ffn_gate_b"], (P, 8))], 1)
    swap = (np.arange(P) ^ 1)[perm]
    col = lambda n: i["L3_attn_" + n][:, None]
    wq, wk, wv = (i["L3_attn_" + n].T for n in ("Wq", "Wv", "Wk"))
    a["l3_weights"] = np.concatenate([
        wq[:, perm], wq[:, swap], wk[:, perm], wk[:, swap], wv, np.broadcast_to(i["L3_attn_bk"], (P, P)),
        wo_groups(i["L3_attn_Wo"].T), col("bq")[perm], col("bq")[swap], col("bv")[perm], col("bv")[swap], col("bo")], 1)
    dim = np.arange(P) % 64
    spatial = dim >= 32
    swap1 = np.where(spatial, np.arange(P) ^ 16, np.arange(P))
    j = np.where(spatial, (dim - 32) % 16, 0)
    bits = [((j >> k) & 1).astype(np.float32)[:, None] for k in range(4)]
    turn = np.where(spatial, 2 * np.pi / (T - 1), 0.0).astype(np.float32)[:, None]
    sign = np.where(spatial, np.where(dim < 48, 1.0, -1.0), 0.0).astype(np.float32)[:, None]
    g = {n: i["L1_attn_" + n] for n in ("Wq", "Wk", "Wv", "Wo", "bq", "bk", "bv", "bo")}
    a["l1_weights"] = np.concatenate([
        g["Wq"], g["Wq"][:, swap1], g["Wk"], g["Wk"][:, swap1], g["Wv"], np.broadcast_to(g["bv"], (P, P)), g["Wo"],
        g["bq"][:, None], g["bq"][swap1, None], g["bk"][:, None], g["bk"][swap1, None], g["bo"][:, None],
        np.broadcast_to(i["L1_attn_nrope_freq"], (P, 1)), *bits, turn, sign], 1)
    m = {n: i["L2_attn_h_" + n] for n in ("in_proj_w", "conv_w", "conv_b", "x_proj_w", "dt_proj_w", "dt_proj_b",
                                          "A_log", "D_param", "out_proj_w")}
    tiles = lambda v: v.reshape(DI, P, -1).transpose(1, 0, 2).reshape(P, -1)
    xproj = np.zeros((DI * P, 96), np.float32)
    xproj[:, 0:RANK] = m["x_proj_w"][0:RANK].T
    xproj[:, 32:32 + NS] = m["x_proj_w"][RANK:RANK + NS].T
    xproj[:, 64:64 + NS] = m["x_proj_w"][RANK + NS:].T
    dtproj = np.zeros((P, DI * P), np.float32)
    dtproj[0:RANK] = m["dt_proj_w"].T
    a["l2_weights"] = np.concatenate([
        m["in_proj_w"].T, tiles(xproj), dtproj, tiles(m["out_proj_w"].T), tiles(m["conv_w"]), tiles(m["conv_b"]),
        tiles(m["dt_proj_b"]), tiles(m["A_log"]), tiles(m["D_param"])], 1)
    rw2 = np.zeros((P, 32), np.float32)
    rw2[:, 0:16] = i["L3_ffn_router_w2"]
    a["l3_router"] = np.concatenate([i["L3_ffn_router_w1"], rw2], 1)
    byp = lambda w: w.reshape(16, P, -1).transpose(1, 0, 2).reshape(P, -1)
    a["l3_up"] = np.concatenate([byp(i["L3_ffn_w1"]), byp(i["L3_ffn_w2"])], 1)
    a["l3_down"] = i["L3_ffn_w3"].reshape(16, 2, P, P).transpose(2, 0, 1, 3).reshape(P, -1)
    return {k: np.ascontiguousarray(v) for k, v in a.items()}


def kernel(**inputs):
    import concourse.bacc as bacc
    from concourse.bass_utils import run_bass_kernel_spmd

    nc = bacc.Bacc("TRN2", target_bir_lowering=False, num_devices=1)
    arrays = layout(inputs)
    drams = {k: nc.dram_tensor(k, v.shape, mybir.dt.from_np(v.dtype), kind="ExternalInput").ap()
             for k, v in arrays.items()}
    out = nc.dram_tensor("out", (P, N), F32, kind="ExternalOutput").ap()
    program(nc, drams, out)
    r = run_bass_kernel_spmd(nc, [arrays], core_ids=[0])
    return np.ascontiguousarray(r.results[0]["out"].T).reshape(B, T, P)
```
